# Optimizing a Trainium2 kernel written in Bass

```python
import numpy as np
import jax
import jax.numpy as jnp

def _softmax(x, axis=-1):
    return jax.nn.softmax(x, axis=axis)

def _gelu(x):
    return jax.nn.gelu(x, approximate=True)

def _silu(x):
    return jax.nn.silu(x)

def _sigmoid(x):
    return jax.nn.sigmoid(x)

def _layernorm(x, axis=-1, eps=1e-05):
    m = jnp.mean(x, axis=axis, keepdims=True)
    v = jnp.var(x, axis=axis, keepdims=True)
    return (x - m) / jnp.sqrt(v + eps)

def _scatter_add(tgt, idx, src, axis=0):
    return tgt.at[idx].add(src)

def _segment_sum(src, seg, n):
    return jax.ops.segment_sum(src, seg, n)
kernel_name = 'mk_flamingo_gated_d4_seqx_r4_ddd3a8'

def setup_inputs(seed: int=0):
    np.random.seed(seed)
    _w = jnp.asarray

    def _rec_inputs():
        import jax
        import jax.numpy as jnp
        _rk = jax.random.key(seed)
        x = -0.0002928 + 1 * jax.random.normal(jax.random.fold_in(_rk, 1), (4, 512, 256), jnp.float32)
        _lenS = 512 - jax.random.randint(jax.random.fold_in(_rk, 7), (4,), 0, max(1, 512 // 4) + 1, jnp.int32)
        _lenS2 = 64 - jax.random.randint(jax.random.fold_in(_rk, 8), (4,), 0, max(1, 64 // 4) + 1, jnp.int32)
        _ctx_512P = jax.random.normal(jax.random.fold_in(_rk, 11), (4, 16, 128), jnp.float32)
        _ctx_512c = jax.random.dirichlet(jax.random.fold_in(_rk, 511), 0.3 * jnp.ones((16,), jnp.float32), (4, 64))
        _ctx_512t = jnp.einsum('bsk,bkd->bsd', _ctx_512c, _ctx_512P)
        _ctx_512t = _ctx_512t * jax.lax.rsqrt(jnp.mean(jnp.square(_ctx_512t)) + 1e-12) * 0.953939
        ctx_512 = 0.00222621 + 0.99962 * (_ctx_512t + 0.3 * jax.random.normal(jax.random.fold_in(_rk, 611), (4, 64, 128), jnp.float32))
        _g = jax.random.normal(jax.random.fold_in(_rk, 9001), (2, 4), jnp.float32)
        _g = jnp.sign(_g) * jnp.maximum(jnp.abs(_g), 1.0) + (_g == 0) * 1.0
        g_xattn = _g[0]
        g_ffn = _g[1]
        return (x, ctx_512, g_xattn, g_ffn)
    x, ctx_512, g_xattn, g_ffn = _rec_inputs()

    def _L0_xattn_setup():
        import jax, jax.numpy as jnp
        import numpy as np
        B, T, TC, C, CC, H = (2, 512, 128, 256, 128, 16)
        D = C // H

        def _heads(t):
            b, l, _ = t.shape
            return t.reshape(b, l, H, D).transpose(0, 2, 1, 3)
        key = jax.random.key(seed)
        ks = jax.random.split(key, 18)
        w = lambda k, i, o: jax.random.normal(k, (i, o), jnp.float32) / np.sqrt(i).astype(np.float32)
        return {'x': jax.random.normal(ks[0], (B, T, C), jnp.float32), 'cross_input': jax.random.normal(ks[1], (B, TC, CC), jnp.float32), 'Wk': w(ks[2], C, C), 'bk': jnp.zeros((C,), jnp.float32), 'Wq': w(ks[3], C, C), 'bq': jnp.zeros((C,), jnp.float32), 'Wv': w(ks[4], C, C), 'bv': jnp.zeros((C,), jnp.float32), 'Wck': w(ks[5], CC, C), 'bck': jnp.zeros((C,), jnp.float32), 'Wcq': w(ks[6], C, C), 'bcq': jnp.zeros((C,), jnp.float32), 'Wcv': w(ks[7], CC, C), 'bcv': jnp.zeros((C,), jnp.float32), 'Wp': w(ks[8], C, C), 'bp': jnp.zeros((C,), jnp.float32)}
    _L0_xattn_all = _L0_xattn_setup()
    _L0_xattn_in = {k: v for k, v in _L0_xattn_all.items() if k in ('Wk', 'bk', 'Wq', 'bq', 'Wv', 'bv', 'Wck', 'bck', 'Wcq', 'bcq', 'Wcv', 'bcv', 'Wp', 'bp')}
    del _L0_xattn_all

    def _L0_ffn_setup():
        import jax, jax.numpy as jnp
        import numpy as np
        BITS = 8
        LORA_RANK = 16
        LORA_ALPHA = 32
        SCALING = LORA_ALPHA / LORA_RANK

        def fake_quant_weight(w, bits=BITS):
            qmax = 2.0 ** (bits - 1) - 1
            scale = jnp.max(jnp.abs(w)) / qmax
            wq = jnp.clip(jnp.round(w / scale), -qmax - 1, qmax) * scale
            return w + jax.lax.stop_gradient(wq - w)

        def qat_lora_linear(x, W, b, A, B):
            Wq = fake_quant_weight(W)
            base = jnp.einsum('bsi,oi->bso', x, Wq) + b
            lora = jnp.einsum('bsr,or->bso', jnp.einsum('bsi,ri->bsr', x, A), B)
            return base + SCALING * lora
        key = jax.random.key(seed)
        ks = jax.random.split(key, 9)
        d, f = (256, 1024)
        s_in = 1.0 / np.sqrt(d)
        s_ff = 1.0 / np.sqrt(f)
        return {'hidden_states': jax.random.normal(ks[0], (4, 512, d), jnp.float32), 'W_fc': jax.random.normal(ks[1], (f, d), jnp.float32) * s_in, 'b_fc': jnp.zeros((f,), jnp.float32), 'A_fc': jax.random.normal(ks[2], (LORA_RANK, d), jnp.float32) * s_in, 'B_fc': jnp.zeros((f, LORA_RANK), jnp.float32), 'W_proj': jax.random.normal(ks[3], (d, f), jnp.float32) * s_ff, 'b_proj': jnp.zeros((d,), jnp.float32), 'A_proj': jax.random.normal(ks[4], (LORA_RANK, f), jnp.float32) * s_ff, 'B_proj': jnp.zeros((d, LORA_RANK), jnp.float32)}
    _L0_ffn_all = _L0_ffn_setup()
    _L0_ffn_in = {k: v for k, v in _L0_ffn_all.items() if k in ('W_fc', 'b_fc', 'A_fc', 'B_fc', 'W_proj', 'b_proj', 'A_proj', 'B_proj')}
    del _L0_ffn_all

    def _L1_xattn_setup():
        import jax, jax.numpy as jnp
        import numpy as np
        DIM = 256
        LATENT_DIM = 128
        NUM_HEADS = 16
        HEAD_DIM = DIM // NUM_HEADS
        SCALE = HEAD_DIM ** (-0.5)
        key = jax.random.key(seed)
        k1, k2, k3, k4, k5 = jax.random.split(key, 5)
        B, xN, zN = (2, 512, 512)
        x = jax.random.normal(k1, (B, xN, DIM), dtype=jnp.float32)
        z = jax.random.normal(k2, (B, zN, LATENT_DIM), dtype=jnp.float32)
        Wq = jax.random.normal(k3, (DIM, DIM), dtype=jnp.float32) * DIM ** (-0.5)
        Wkv = jax.random.normal(k4, (2 * DIM, LATENT_DIM), dtype=jnp.float32) * LATENT_DIM ** (-0.5)
        Wo = jax.random.normal(k5, (DIM, DIM), dtype=jnp.float32) * DIM ** (-0.5)
        return {'x': x, 'z': z, 'Wq': Wq, 'Wkv': Wkv, 'Wo': Wo}
    _L1_xattn_all = _L1_xattn_setup()
    _L1_xattn_in = {k: v for k, v in _L1_xattn_all.items() if k in ('Wq', 'Wkv', 'Wo')}
    del _L1_xattn_all

    def _L1_ffn_setup():
        import jax, jax.numpy as jnp
        import numpy as np

        def _ste(w, w_q):
            return w + jax.lax.stop_gradient(w_q - w)

        def quantize_w8_per(w, axis):
            amax = jnp.clip(jnp.max(jnp.abs(w), axis=axis, keepdims=True), 1e-08, None)
            scale = 127.0 / amax
            w_q = jnp.clip(jnp.round(w * scale), -128.0, 127.0) / scale
            return _ste(w, w_q)

        def quantize_a16(x):
            amax = jnp.clip(jnp.max(jnp.abs(x)), 1e-08, None)
            scale = 32767.0 / amax
            x_q = jnp.clip(jnp.round(x * scale), -32768.0, 32767.0) / scale
            return _ste(x, x_q)
        key = jax.random.key(seed)
        k1, k2, k3 = jax.random.split(key, 3)
        d_model, d_ff = (256, 1024)
        x = jax.random.normal(k1, (4, 512, d_model), dtype=jnp.float32)
        W_in = jax.random.normal(k2, (d_model, d_ff), dtype=jnp.float32) / np.sqrt(d_model)
        b_in = jnp.zeros((d_ff,), dtype=jnp.float32)
        W_out = jax.random.normal(k3, (d_ff, d_model), dtype=jnp.float32) / np.sqrt(d_ff)
        b_out = jnp.zeros((d_model,), dtype=jnp.float32)
        return {'x': x, 'W_in': W_in, 'b_in': b_in, 'W_out': W_out, 'b_out': b_out}
    _L1_ffn_all = _L1_ffn_setup()
    _L1_ffn_in = {k: v for k, v in _L1_ffn_all.items() if k in ('W_in', 'b_in', 'W_out', 'b_out')}
    del _L1_ffn_all

    def _L2_xattn_setup():
        import jax, jax.numpy as jnp
        import numpy as np
        B, LQ, LK = (8, 512, 512)
        QD, KD, VD = (256, 128, 128)
        key = jax.random.key(seed)
        ks = jax.random.split(key, 9)
        s = 0.02
        return {'query': jax.random.normal(ks[0], (B, LQ, QD), jnp.float32), 'key': jax.random.normal(ks[1], (B, LK, KD), jnp.float32), 'value': jax.random.normal(ks[2], (B, LK, VD), jnp.float32), 'Wq': jax.random.normal(ks[3], (QD, QD), jnp.float32) * s, 'bq': jnp.zeros((QD,), jnp.float32), 'Wk': jax.random.normal(ks[4], (KD, QD), jnp.float32) * s, 'bk': jnp.zeros((QD,), jnp.float32), 'Wv': jax.random.normal(ks[5], (VD, QD), jnp.float32) * s, 'bv': jnp.zeros((QD,), jnp.float32)}
    _L2_xattn_all = _L2_xattn_setup()
    _L2_xattn_in = {k: v for k, v in _L2_xattn_all.items() if k in ('Wq', 'bq', 'Wk', 'bk', 'Wv', 'bv')}
    del _L2_xattn_all

    def _L2_ffn_setup():
        import jax, jax.numpy as jnp
        import numpy as np
        import math
        N_EXP = 8
        TOP_K = 2
        CAPACITY_FACTOR = 1.25

        def _capacity(num_tokens):
            cap = math.floor(TOP_K * CAPACITY_FACTOR * num_tokens / N_EXP)
            cap += cap % 2
            return int(cap)
        key = jax.random.key(seed)
        k1, k2, k3, k4 = jax.random.split(key, 4)
        B, C, d = (4, 256, 256)
        x = jax.random.normal(k1, (B, C, d), dtype=jnp.float32)
        w_g = jax.random.normal(k2, (d, N_EXP), dtype=jnp.float32) * 0.02
        c_fc = jax.random.normal(k3, (N_EXP, d, 4 * d), dtype=jnp.float32) * 0.02
        c_proj = jax.random.normal(k4, (N_EXP, 4 * d, d), dtype=jnp.float32) * 0.02
        return {'x': x, 'w_g': w_g, 'c_fc': c_fc, 'c_proj': c_proj}
    _L2_ffn_all = _L2_ffn_setup()
    _L2_ffn_in = {k: v for k, v in _L2_ffn_all.items() if k in ('w_g', 'c_fc', 'c_proj')}
    del _L2_ffn_all

    def _L3_xattn_setup():
        import jax, jax.numpy as jnp
        import numpy as np
        H, D, C1, C2, S, M, B, W = (16, 32, 256, 128, 512, 128, 2, 4)

        def _ln(x, g, b):
            m = jnp.mean(x, -1, keepdims=True)
            v = jnp.var(x, -1, keepdims=True)
            return (x - m) * jax.lax.rsqrt(v + 1e-05) * g + b

        def _mha(x, y, wq, wk, wv, li1_w, li1_b, lnx_g, lnx_b, lny_g, lny_b, ln3_g, ln3_b, li2_w, li2_b, li3_w, li3_b, causal):
            xn = _ln(x, lnx_g, lnx_b)
            yn = _ln(y, lny_g, lny_b)
            q = jnp.einsum('bsc,hcd->bhsd', xn, wq)
            k = jnp.einsum('btc,hcd->bhtd', yn, wk)
            v = jnp.einsum('btc,hcd->bhtd', yn, wv)
            a = jax.nn.softmax(jnp.einsum('bhsd,bhtd->bhst', q, k) * D ** (-0.5), axis=-1)
            if causal:
                s, t = (a.shape[-2], a.shape[-1])
                mask = (jnp.arange(t)[None, :] > jnp.arange(s)[:, None]).astype(a.dtype)
                a = a * mask
            o = jnp.einsum('bhst,bhtd->bhsd', a, v)
            o = o.transpose(0, 2, 1, 3).reshape(x.shape[0], x.shape[1], H * D)
            x_out = x + o @ li1_w + li1_b
            h = jax.nn.gelu(_ln(x_out, ln3_g, ln3_b) @ li2_w + li2_b, approximate=False)
            return x_out + h @ li3_w + li3_b
        key = jax.random.key(seed)
        ks = iter(jax.random.split(key, 64))

        def w(shape, scale=0.02):
            return jax.random.normal(next(ks), shape, jnp.float32) * scale
        inp = {'xx': jax.random.normal(next(ks), (B, S, C1), jnp.float32), 'ee': jax.random.normal(next(ks), (B, M, C2), jnp.float32), 'ln1_g': jnp.ones(C1, jnp.float32), 'ln1_b': jnp.zeros(C1, jnp.float32), 'ln2_g': jnp.ones(C1, jnp.float32), 'ln2_b': jnp.zeros(C1, jnp.float32)}
        for pfx, cy in (('a1', C1), ('a2', C2)):
            inp[pfx + '_wq'] = w((H, C1, D))
            inp[pfx + '_wk'] = w((H, cy, D))
            inp[pfx + '_wv'] = w((H, cy, D))
            inp[pfx + '_li1_w'] = w((H * D, C1))
            inp[pfx + '_li1_b'] = jnp.zeros(C1, jnp.float32)
            inp[pfx + '_lnx_g'] = jnp.ones(C1, jnp.float32)
            inp[pfx + '_lnx_b'] = jnp.zeros(C1, jnp.float32)
            inp[pfx + '_lny_g'] = jnp.ones(cy, jnp.float32)
            inp[pfx + '_lny_b'] = jnp.zeros(cy, jnp.float32)
            inp[pfx + '_ln3_g'] = jnp.ones(C1, jnp.float32)
            inp[pfx + '_ln3_b'] = jnp.zeros(C1, jnp.float32)
            inp[pfx + '_li2_w'] = w((C1, C1 * W))
            inp[pfx + '_li2_b'] = jnp.zeros(C1 * W, jnp.float32)
            inp[pfx + '_li3_w'] = w((C1 * W, C1))
            inp[pfx + '_li3_b'] = jnp.zeros(C1, jnp.float32)
        inp['training'] = 0
        return inp
    _L3_xattn_all = _L3_xattn_setup()
    _L3_xattn_in = {k: v for k, v in _L3_xattn_all.items() if k in ('ln1_g', 'ln1_b', 'ln2_g', 'ln2_b', 'a1_wq', 'a1_wk', 'a1_wv', 'a1_li1_w', 'a1_li1_b', 'a1_lnx_g', 'a1_lnx_b', 'a1_lny_g', 'a1_lny_b', 'a1_ln3_g', 'a1_ln3_b', 'a1_li2_w', 'a1_li2_b', 'a1_li3_w', 'a1_li3_b', 'a2_wq', 'a2_wk', 'a2_wv', 'a2_li1_w', 'a2_li1_b', 'a2_lnx_g', 'a2_lnx_b', 'a2_lny_g', 'a2_lny_b', 'a2_ln3_g', 'a2_ln3_b', 'a2_li2_w', 'a2_li2_b', 'a2_li3_w', 'a2_li3_b')}
    del _L3_xattn_all

    def _L3_ffn_setup():
        import jax, jax.numpy as jnp
        import numpy as np
        E = 16
        K = 4
        G = 4
        TG = 2
        NS = 2
        H = 256
        I = 352
        SCALE = 1.0

        def _gate(x2d, gate_w, gate_bias):
            T = x2d.shape[0]
            logits = x2d.astype(jnp.float32) @ gate_w.astype(jnp.float32).T
            scores = jax.nn.sigmoid(logits)
            sfc = scores + gate_bias[None, :]
            grp = sfc.reshape(T, G, E // G)
            top2, _ = jax.lax.top_k(grp, 2)
            group_scores = top2.sum(-1)
            _, gidx = jax.lax.top_k(group_scores, TG)
            gmask = jnp.zeros((T, G), sfc.dtype).at[jnp.arange(T)[:, None], gidx].set(1.0)
            smask = jnp.repeat(gmask, E // G, axis=1) > 0
            tmp = jnp.where(smask, sfc, 0.0)
            _, topk_idx = jax.lax.top_k(tmp, K)
            topk_w = jnp.take_along_axis(scores, topk_idx, axis=1)
            topk_w = topk_w / (topk_w.sum(-1, keepdims=True) + 1e-20)
            return (topk_idx, topk_w * SCALE)
        key = jax.random.key(seed)
        ks = jax.random.split(key, 8)
        bound = 1.0 / np.sqrt(H)
        return {'hidden_states': jax.random.normal(ks[0], (1, 256, H), jnp.float32), 'gate_w': jax.random.uniform(ks[1], (E, H), jnp.float32, -bound, bound), 'gate_bias': jnp.zeros((E,), jnp.float32), 'gate_proj': jax.random.normal(ks[2], (E, I, H), jnp.float32) * 0.02, 'up_proj': jax.random.normal(ks[3], (E, I, H), jnp.float32) * 0.02, 'down_proj': jax.random.normal(ks[4], (E, H, I), jnp.float32) * 0.02, 'shared_gate_w': jax.random.normal(ks[5], (I * NS, H), jnp.float32) * 0.02, 'shared_up_w': jax.random.normal(ks[6], (I * NS, H), jnp.float32) * 0.02, 'shared_down_w': jax.random.normal(ks[7], (H, I * NS), jnp.float32) * 0.02}
    _L3_ffn_all = _L3_ffn_setup()
    _L3_ffn_in = {k: v for k, v in _L3_ffn_all.items() if k in ('gate_w', 'gate_bias', 'gate_proj', 'up_proj', 'down_proj', 'shared_gate_w', 'shared_up_w', 'shared_down_w')}
    del _L3_ffn_all
    return {'x': x, 'ctx_512': ctx_512, 'g_xattn': g_xattn, 'g_ffn': g_ffn, 'L0_xattn_Wk': _L0_xattn_in['Wk'], 'L0_xattn_bk': _L0_xattn_in['bk'], 'L0_xattn_Wq': _L0_xattn_in['Wq'], 'L0_xattn_bq': _L0_xattn_in['bq'], 'L0_xattn_Wv': _L0_xattn_in['Wv'], 'L0_xattn_bv': _L0_xattn_in['bv'], 'L0_xattn_Wck': _L0_xattn_in['Wck'], 'L0_xattn_bck': _L0_xattn_in['bck'], 'L0_xattn_Wcq': _L0_xattn_in['Wcq'], 'L0_xattn_bcq': _L0_xattn_in['bcq'], 'L0_xattn_Wcv': _L0_xattn_in['Wcv'], 'L0_xattn_bcv': _L0_xattn_in['bcv'], 'L0_xattn_Wp': _L0_xattn_in['Wp'], 'L0_xattn_bp': _L0_xattn_in['bp'], 'L0_ffn_W_fc': _L0_ffn_in['W_fc'], 'L0_ffn_b_fc': _L0_ffn_in['b_fc'], 'L0_ffn_A_fc': _L0_ffn_in['A_fc'], 'L0_ffn_B_fc': _L0_ffn_in['B_fc'], 'L0_ffn_W_proj': _L0_ffn_in['W_proj'], 'L0_ffn_b_proj': _L0_ffn_in['b_proj'], 'L0_ffn_A_proj': _L0_ffn_in['A_proj'], 'L0_ffn_B_proj': _L0_ffn_in['B_proj'], 'L1_xattn_Wq': _L1_xattn_in['Wq'], 'L1_xattn_Wkv': _L1_xattn_in['Wkv'], 'L1_xattn_Wo': _L1_xattn_in['Wo'], 'L1_ffn_W_in': _L1_ffn_in['W_in'], 'L1_ffn_b_in': _L1_ffn_in['b_in'], 'L1_ffn_W_out': _L1_ffn_in['W_out'], 'L1_ffn_b_out': _L1_ffn_in['b_out'], 'L2_xattn_Wq': _L2_xattn_in['Wq'], 'L2_xattn_bq': _L2_xattn_in['bq'], 'L2_xattn_Wk': _L2_xattn_in['Wk'], 'L2_xattn_bk': _L2_xattn_in['bk'], 'L2_xattn_Wv': _L2_xattn_in['Wv'], 'L2_xattn_bv': _L2_xattn_in['bv'], 'L2_ffn_w_g': _L2_ffn_in['w_g'], 'L2_ffn_c_fc': _L2_ffn_in['c_fc'], 'L2_ffn_c_proj': _L2_ffn_in['c_proj'], 'L3_xattn_ln1_g': _L3_xattn_in['ln1_g'], 'L3_xattn_ln1_b': _L3_xattn_in['ln1_b'], 'L3_xattn_ln2_g': _L3_xattn_in['ln2_g'], 'L3_xattn_ln2_b': _L3_xattn_in['ln2_b'], 'L3_xattn_a1_wq': _L3_xattn_in['a1_wq'], 'L3_xattn_a1_wk': _L3_xattn_in['a1_wk'], 'L3_xattn_a1_wv': _L3_xattn_in['a1_wv'], 'L3_xattn_a1_li1_w': _L3_xattn_in['a1_li1_w'], 'L3_xattn_a1_li1_b': _L3_xattn_in['a1_li1_b'], 'L3_xattn_a1_lnx_g': _L3_xattn_in['a1_lnx_g'], 'L3_xattn_a1_lnx_b': _L3_xattn_in['a1_lnx_b'], 'L3_xattn_a1_lny_g': _L3_xattn_in['a1_lny_g'], 'L3_xattn_a1_lny_b': _L3_xattn_in['a1_lny_b'], 'L3_xattn_a1_ln3_g': _L3_xattn_in['a1_ln3_g'], 'L3_xattn_a1_ln3_b': _L3_xattn_in['a1_ln3_b'], 'L3_xattn_a1_li2_w': _L3_xattn_in['a1_li2_w'], 'L3_xattn_a1_li2_b': _L3_xattn_in['a1_li2_b'], 'L3_xattn_a1_li3_w': _L3_xattn_in['a1_li3_w'], 'L3_xattn_a1_li3_b': _L3_xattn_in['a1_li3_b'], 'L3_xattn_a2_wq': _L3_xattn_in['a2_wq'], 'L3_xattn_a2_wk': _L3_xattn_in['a2_wk'], 'L3_xattn_a2_wv': _L3_xattn_in['a2_wv'], 'L3_xattn_a2_li1_w': _L3_xattn_in['a2_li1_w'], 'L3_xattn_a2_li1_b': _L3_xattn_in['a2_li1_b'], 'L3_xattn_a2_lnx_g': _L3_xattn_in['a2_lnx_g'], 'L3_xattn_a2_lnx_b': _L3_xattn_in['a2_lnx_b'], 'L3_xattn_a2_lny_g': _L3_xattn_in['a2_lny_g'], 'L3_xattn_a2_lny_b': _L3_xattn_in['a2_lny_b'], 'L3_xattn_a2_ln3_g': _L3_xattn_in['a2_ln3_g'], 'L3_xattn_a2_ln3_b': _L3_xattn_in['a2_ln3_b'], 'L3_xattn_a2_li2_w': _L3_xattn_in['a2_li2_w'], 'L3_xattn_a2_li2_b': _L3_xattn_in['a2_li2_b'], 'L3_xattn_a2_li3_w': _L3_xattn_in['a2_li3_w'], 'L3_xattn_a2_li3_b': _L3_xattn_in['a2_li3_b'], 'L3_ffn_gate_w': _L3_ffn_in['gate_w'], 'L3_ffn_gate_bias': _L3_ffn_in['gate_bias'], 'L3_ffn_gate_proj': _L3_ffn_in['gate_proj'], 'L3_ffn_up_proj': _L3_ffn_in['up_proj'], 'L3_ffn_down_proj': _L3_ffn_in['down_proj'], 'L3_ffn_shared_gate_w': _L3_ffn_in['shared_gate_w'], 'L3_ffn_shared_up_w': _L3_ffn_in['shared_up_w'], 'L3_ffn_shared_down_w': _L3_ffn_in['shared_down_w']}

def reference(x, ctx_512, g_xattn, g_ffn, L0_xattn_Wk, L0_xattn_bk, L0_xattn_Wq, L0_xattn_bq, L0_xattn_Wv, L0_xattn_bv, L0_xattn_Wck, L0_xattn_bck, L0_xattn_Wcq, L0_xattn_bcq, L0_xattn_Wcv, L0_xattn_bcv, L0_xattn_Wp, L0_xattn_bp, L0_ffn_W_fc, L0_ffn_b_fc, L0_ffn_A_fc, L0_ffn_B_fc, L0_ffn_W_proj, L0_ffn_b_proj, L0_ffn_A_proj, L0_ffn_B_proj, L1_xattn_Wq, L1_xattn_Wkv, L1_xattn_Wo, L1_ffn_W_in, L1_ffn_b_in, L1_ffn_W_out, L1_ffn_b_out, L2_xattn_Wq, L2_xattn_bq, L2_xattn_Wk, L2_xattn_bk, L2_xattn_Wv, L2_xattn_bv, L2_ffn_w_g, L2_ffn_c_fc, L2_ffn_c_proj, L3_xattn_ln1_g, L3_xattn_ln1_b, L3_xattn_ln2_g, L3_xattn_ln2_b, L3_xattn_a1_wq, L3_xattn_a1_wk, L3_xattn_a1_wv, L3_xattn_a1_li1_w, L3_xattn_a1_li1_b, L3_xattn_a1_lnx_g, L3_xattn_a1_lnx_b, L3_xattn_a1_lny_g, L3_xattn_a1_lny_b, L3_xattn_a1_ln3_g, L3_xattn_a1_ln3_b, L3_xattn_a1_li2_w, L3_xattn_a1_li2_b, L3_xattn_a1_li3_w, L3_xattn_a1_li3_b, L3_xattn_a2_wq, L3_xattn_a2_wk, L3_xattn_a2_wv, L3_xattn_a2_li1_w, L3_xattn_a2_li1_b, L3_xattn_a2_lnx_g, L3_xattn_a2_lnx_b, L3_xattn_a2_lny_g, L3_xattn_a2_lny_b, L3_xattn_a2_ln3_g, L3_xattn_a2_ln3_b, L3_xattn_a2_li2_w, L3_xattn_a2_li2_b, L3_xattn_a2_li3_w, L3_xattn_a2_li3_b, L3_ffn_gate_w, L3_ffn_gate_bias, L3_ffn_gate_proj, L3_ffn_up_proj, L3_ffn_down_proj, L3_ffn_shared_gate_w, L3_ffn_shared_up_w, L3_ffn_shared_down_w):
    import jax
    import jax.numpy as jnp

    def _L0_xattn_ref(x, cross_input, Wk, bk, Wq, bq, Wv, bv, Wck, bck, Wcq, bcq, Wcv, bcv, Wp, bp):
        import jax, jax.numpy as jnp
        import numpy as np
        B, T, TC, C, CC, H = (2, 512, 128, 256, 128, 16)
        D = C // H

        def _heads(t):
            b, l, _ = t.shape
            return t.reshape(b, l, H, D).transpose(0, 2, 1, 3)
        scale = np.float32(1.0 / np.sqrt(D))
        q = _heads(x @ Wq + bq)
        k = _heads(x @ Wk + bk)
        v = _heads(x @ Wv + bv)
        att = jnp.einsum('bhqd,bhkd->bhqk', q, k) * scale
        causal = jnp.tril(jnp.ones((T, T), bool))
        att = jnp.where(causal[None, None], att, -jnp.inf)
        y = jnp.einsum('bhqk,bhkd->bhqd', jax.nn.softmax(att, axis=-1), v)
        qc = _heads(x @ Wcq + bcq)
        kc = _heads(cross_input @ Wck + bck)
        vc = _heads(cross_input @ Wcv + bcv)
        attc = jnp.einsum('bhqd,bhkd->bhqk', qc, kc) * scale
        y = y + jnp.einsum('bhqk,bhkd->bhqd', jax.nn.softmax(attc, axis=-1), vc)
        y = y.transpose(0, 2, 1, 3).reshape(x.shape[0], T, C)
        return y @ Wp + bp

    def _L0_ffn_ref(hidden_states, W_fc, b_fc, A_fc, B_fc, W_proj, b_proj, A_proj, B_proj):
        import jax, jax.numpy as jnp
        import numpy as np
        BITS = 8
        LORA_RANK = 16
        LORA_ALPHA = 32
        SCALING = LORA_ALPHA / LORA_RANK

        def fake_quant_weight(w, bits=BITS):
            qmax = 2.0 ** (bits - 1) - 1
            scale = jnp.max(jnp.abs(w)) / qmax
            wq = jnp.clip(jnp.round(w / scale), -qmax - 1, qmax) * scale
            return w + jax.lax.stop_gradient(wq - w)

        def qat_lora_linear(x, W, b, A, B):
            Wq = fake_quant_weight(W)
            base = jnp.einsum('bsi,oi->bso', x, Wq) + b
            lora = jnp.einsum('bsr,or->bso', jnp.einsum('bsi,ri->bsr', x, A), B)
            return base + SCALING * lora
        h = qat_lora_linear(hidden_states, W_fc, b_fc, A_fc, B_fc)
        h = jax.nn.gelu(h, approximate=False)
        h = qat_lora_linear(h, W_proj, b_proj, A_proj, B_proj)
        return h

    def _L1_xattn_ref(x, z, Wq, Wkv, Wo):
        import jax, jax.numpy as jnp
        import numpy as np
        DIM = 256
        LATENT_DIM = 128
        NUM_HEADS = 16
        HEAD_DIM = DIM // NUM_HEADS
        SCALE = HEAD_DIM ** (-0.5)
        B, xN, _ = x.shape
        _, zN, _ = z.shape
        Q = (x @ Wq.T).reshape(B, xN, NUM_HEADS, HEAD_DIM)
        KV = (z @ Wkv.T).reshape(B, zN, 2, NUM_HEADS, HEAD_DIM)
        K = KV[:, :, 0]
        V = KV[:, :, 1]
        attn = jnp.einsum('bqhd,bkhd->bhqk', Q, K) * SCALE
        attn = jax.nn.softmax(attn, axis=-1)
        O = jnp.einsum('bhqk,bkhd->bqhd', attn, V).reshape(B, xN, DIM)
        return O @ Wo.T

    def _L1_ffn_ref(x, W_in, b_in, W_out, b_out):
        import jax, jax.numpy as jnp
        import numpy as np

        def _ste(w, w_q):
            return w + jax.lax.stop_gradient(w_q - w)

        def quantize_w8_per(w, axis):
            amax = jnp.clip(jnp.max(jnp.abs(w), axis=axis, keepdims=True), 1e-08, None)
            scale = 127.0 / amax
            w_q = jnp.clip(jnp.round(w * scale), -128.0, 127.0) / scale
            return _ste(w, w_q)

        def quantize_a16(x):
            amax = jnp.clip(jnp.max(jnp.abs(x)), 1e-08, None)
            scale = 32767.0 / amax
            x_q = jnp.clip(jnp.round(x * scale), -32768.0, 32767.0) / scale
            return _ste(x, x_q)
        W_in_sim = quantize_w8_per(W_in, axis=0)
        W_out_sim = quantize_w8_per(W_out, axis=1)
        x_sim = quantize_a16(x)
        hidden = jax.nn.gelu(x_sim @ W_in_sim + b_in, approximate=False)
        hidden_sim = quantize_a16(hidden)
        out = hidden_sim @ W_out_sim + b_out
        return out

    def _L2_xattn_ref(query, key, value, Wq, bq, Wk, bk, Wv, bv):
        import jax, jax.numpy as jnp
        import numpy as np
        B, LQ, LK = (8, 512, 512)
        QD, KD, VD = (256, 128, 128)
        q = jnp.einsum('bld,de->ble', query, Wq) + bq
        k = jnp.einsum('bld,de->ble', key, Wk) + bk
        v = jnp.einsum('bld,de->ble', value, Wv) + bv
        scores = jnp.einsum('bqe,bke->bqk', q, k)
        attn = jax.nn.softmax(scores, axis=-1)
        out = jnp.einsum('bqk,bke->bqe', attn, v)
        return out

    def _L2_ffn_ref(x, w_g, c_fc, c_proj):
        import jax, jax.numpy as jnp
        import numpy as np
        import math
        N_EXP = 8
        TOP_K = 2
        CAPACITY_FACTOR = 1.25

        def _capacity(num_tokens):
            cap = math.floor(TOP_K * CAPACITY_FACTOR * num_tokens / N_EXP)
            cap += cap % 2
            return int(cap)
        B, C, d = x.shape
        T = B * C
        cap = _capacity(T)
        xt = x.reshape(T, d)
        logits = xt @ w_g
        top_v, top_i = jax.lax.top_k(logits, TOP_K)
        full = jnp.full_like(logits, -jnp.inf)
        full = full.at[jnp.arange(T)[:, None], top_i].set(top_v)
        probs = jax.nn.softmax(full, axis=-1)
        exp_mask = jax.nn.one_hot(top_i, N_EXP, dtype=jnp.int32)
        exp_mask = jnp.transpose(exp_mask, (1, 0, 2))
        exp_rank = jnp.cumsum(exp_mask.reshape(TOP_K * T, N_EXP), axis=0) - 1
        exp_rank = exp_rank.reshape(TOP_K, T, N_EXP)
        exp_mask = exp_mask * (exp_rank < cap).astype(jnp.int32)
        exp_rank = jnp.sum(exp_mask * exp_rank, axis=-1)
        exp_weights = exp_mask.astype(x.dtype) * probs[None]
        rank_oh = jax.nn.one_hot(exp_rank, cap, dtype=x.dtype)
        cb_weight = jnp.einsum('kte,ktc->tec', exp_weights, rank_oh)
        sec_mask = (cb_weight != 0).astype(x.dtype)
        exp_batches = jnp.einsum('tec,td->ecd', sec_mask, xt)
        h = jax.nn.gelu(jnp.einsum('ecd,edf->ecf', exp_batches, c_fc), approximate=False)
        exp_out = jnp.einsum('ecf,efd->ecd', h, c_proj)
        out = cb_weight.reshape(T, N_EXP * cap) @ exp_out.reshape(N_EXP * cap, d)
        return out.reshape(B, C, d)

    def _L3_xattn_ref(xx, ee, ln1_g, ln1_b, ln2_g, ln2_b, a1_wq, a1_wk, a1_wv, a1_li1_w, a1_li1_b, a1_lnx_g, a1_lnx_b, a1_lny_g, a1_lny_b, a1_ln3_g, a1_ln3_b, a1_li2_w, a1_li2_b, a1_li3_w, a1_li3_b, a2_wq, a2_wk, a2_wv, a2_li1_w, a2_li1_b, a2_lnx_g, a2_lnx_b, a2_lny_g, a2_lny_b, a2_ln3_g, a2_ln3_b, a2_li2_w, a2_li2_b, a2_li3_w, a2_li3_b, training):
        import jax, jax.numpy as jnp
        import numpy as np
        H, D, C1, C2, S, M, B, W = (16, 32, 256, 128, 512, 128, 2, 4)

        def _ln(x, g, b):
            m = jnp.mean(x, -1, keepdims=True)
            v = jnp.var(x, -1, keepdims=True)
            return (x - m) * jax.lax.rsqrt(v + 1e-05) * g + b

        def _mha(x, y, wq, wk, wv, li1_w, li1_b, lnx_g, lnx_b, lny_g, lny_b, ln3_g, ln3_b, li2_w, li2_b, li3_w, li3_b, causal):
            xn = _ln(x, lnx_g, lnx_b)
            yn = _ln(y, lny_g, lny_b)
            q = jnp.einsum('bsc,hcd->bhsd', xn, wq)
            k = jnp.einsum('btc,hcd->bhtd', yn, wk)
            v = jnp.einsum('btc,hcd->bhtd', yn, wv)
            a = jax.nn.softmax(jnp.einsum('bhsd,bhtd->bhst', q, k) * D ** (-0.5), axis=-1)
            if causal:
                s, t = (a.shape[-2], a.shape[-1])
                mask = (jnp.arange(t)[None, :] > jnp.arange(s)[:, None]).astype(a.dtype)
                a = a * mask
            o = jnp.einsum('bhst,bhtd->bhsd', a, v)
            o = o.transpose(0, 2, 1, 3).reshape(x.shape[0], x.shape[1], H * D)
            x_out = x + o @ li1_w + li1_b
            h = jax.nn.gelu(_ln(x_out, ln3_g, ln3_b) @ li2_w + li2_b, approximate=False)
            return x_out + h @ li3_w + li3_b
        x = _ln(xx, ln1_g, ln1_b)
        x = x + _mha(x, x, a1_wq, a1_wk, a1_wv, a1_li1_w, a1_li1_b, a1_lnx_g, a1_lnx_b, a1_lny_g, a1_lny_b, a1_ln3_g, a1_ln3_b, a1_li2_w, a1_li2_b, a1_li3_w, a1_li3_b, causal=True)
        x = _ln(x, ln2_g, ln2_b)
        return x + _mha(x, ee, a2_wq, a2_wk, a2_wv, a2_li1_w, a2_li1_b, a2_lnx_g, a2_lnx_b, a2_lny_g, a2_lny_b, a2_ln3_g, a2_ln3_b, a2_li2_w, a2_li2_b, a2_li3_w, a2_li3_b, causal=False)

    def _L3_ffn_ref(hidden_states, gate_w, gate_bias, gate_proj, up_proj, down_proj, shared_gate_w, shared_up_w, shared_down_w):
        import jax, jax.numpy as jnp
        import numpy as np
        E = 16
        K = 4
        G = 4
        TG = 2
        NS = 2
        H = 256
        I = 352
        SCALE = 1.0

        def _gate(x2d, gate_w, gate_bias):
            T = x2d.shape[0]
            logits = x2d.astype(jnp.float32) @ gate_w.astype(jnp.float32).T
            scores = jax.nn.sigmoid(logits)
            sfc = scores + gate_bias[None, :]
            grp = sfc.reshape(T, G, E // G)
            top2, _ = jax.lax.top_k(grp, 2)
            group_scores = top2.sum(-1)
            _, gidx = jax.lax.top_k(group_scores, TG)
            gmask = jnp.zeros((T, G), sfc.dtype).at[jnp.arange(T)[:, None], gidx].set(1.0)
            smask = jnp.repeat(gmask, E // G, axis=1) > 0
            tmp = jnp.where(smask, sfc, 0.0)
            _, topk_idx = jax.lax.top_k(tmp, K)
            topk_w = jnp.take_along_axis(scores, topk_idx, axis=1)
            topk_w = topk_w / (topk_w.sum(-1, keepdims=True) + 1e-20)
            return (topk_idx, topk_w * SCALE)
        orig_shape = hidden_states.shape
        x = hidden_states.reshape(-1, H)
        topk_idx, topk_w = _gate(x, gate_w, gate_bias)
        combine_w = (jax.nn.one_hot(topk_idx, E, dtype=x.dtype) * topk_w[..., None]).sum(1)
        g = jnp.einsum('th,eih->tei', x, gate_proj)
        u = jnp.einsum('th,eih->tei', x, up_proj)
        act = jax.nn.silu(g) * u
        y = jnp.einsum('tei,ehi,te->th', act, down_proj, combine_w)
        sg = x @ shared_gate_w.T
        su = x @ shared_up_w.T
        y = y + jax.nn.silu(sg) * su @ shared_down_w.T
        return y.reshape(orig_shape)
    x = x + jnp.tanh(g_xattn[0]) * _L0_xattn_ref(_layernorm(x, axis=-1), ctx_512, L0_xattn_Wk, L0_xattn_bk, L0_xattn_Wq, L0_xattn_bq, L0_xattn_Wv, L0_xattn_bv, L0_xattn_Wck, L0_xattn_bck, L0_xattn_Wcq, L0_xattn_bcq, L0_xattn_Wcv, L0_xattn_bcv, L0_xattn_Wp, L0_xattn_bp)
    x = x + jnp.tanh(g_ffn[0]) * _L0_ffn_ref(_layernorm(x, axis=-1), L0_ffn_W_fc, L0_ffn_b_fc, L0_ffn_A_fc, L0_ffn_B_fc, L0_ffn_W_proj, L0_ffn_b_proj, L0_ffn_A_proj, L0_ffn_B_proj)
    x = x + jnp.tanh(g_xattn[1]) * _L1_xattn_ref(_layernorm(x, axis=-1), ctx_512, L1_xattn_Wq, L1_xattn_Wkv, L1_xattn_Wo)
    x = x + jnp.tanh(g_ffn[1]) * _L1_ffn_ref(_layernorm(x, axis=-1), L1_ffn_W_in, L1_ffn_b_in, L1_ffn_W_out, L1_ffn_b_out)
    x = x + jnp.tanh(g_xattn[2]) * _L2_xattn_ref(_layernorm(x, axis=-1), ctx_512, ctx_512, L2_xattn_Wq, L2_xattn_bq, L2_xattn_Wk, L2_xattn_bk, L2_xattn_Wv, L2_xattn_bv)
    x = x + jnp.tanh(g_ffn[2]) * _L2_ffn_ref(_layernorm(x, axis=-1), L2_ffn_w_g, L2_ffn_c_fc, L2_ffn_c_proj)
    x = x + jnp.tanh(g_xattn[3]) * _L3_xattn_ref(_layernorm(x, axis=-1), ctx_512, L3_xattn_ln1_g, L3_xattn_ln1_b, L3_xattn_ln2_g, L3_xattn_ln2_b, L3_xattn_a1_wq, L3_xattn_a1_wk, L3_xattn_a1_wv, L3_xattn_a1_li1_w, L3_xattn_a1_li1_b, L3_xattn_a1_lnx_g, L3_xattn_a1_lnx_b, L3_xattn_a1_lny_g, L3_xattn_a1_lny_b, L3_xattn_a1_ln3_g, L3_xattn_a1_ln3_b, L3_xattn_a1_li2_w, L3_xattn_a1_li2_b, L3_xattn_a1_li3_w, L3_xattn_a1_li3_b, L3_xattn_a2_wq, L3_xattn_a2_wk, L3_xattn_a2_wv, L3_xattn_a2_li1_w, L3_xattn_a2_li1_b, L3_xattn_a2_lnx_g, L3_xattn_a2_lnx_b, L3_xattn_a2_lny_g, L3_xattn_a2_lny_b, L3_xattn_a2_ln3_g, L3_xattn_a2_ln3_b, L3_xattn_a2_li2_w, L3_xattn_a2_li2_b, L3_xattn_a2_li3_w, L3_xattn_a2_li3_b, 0)
    x = x + jnp.tanh(g_ffn[3]) * _L3_ffn_ref(_layernorm(x, axis=-1), L3_ffn_gate_w, L3_ffn_gate_bias, L3_ffn_gate_proj, L3_ffn_up_proj, L3_ffn_down_proj, L3_ffn_shared_gate_w, L3_ffn_shared_up_w, L3_ffn_shared_down_w)
    return x

_drawn_inputs = setup_inputs


def setup_inputs(seed=0):
    import zlib

    import numpy as np

    out = dict(_drawn_inputs(seed))
    spreads = {'L0_xattn_bk': (0.0, 0.8),
     'L0_xattn_bq': (0.0, 0.8),
     'L0_xattn_bv': (0.0, 0.1),
     'L0_xattn_bck': (0.0, 0.8),
     'L0_xattn_bcq': (0.0, 0.529),
     'L0_xattn_bcv': (0.0, 0.1),
     'L0_xattn_bp': (0.0, 0.1),
     'L0_ffn_b_fc': (0.0, 0.1),
     'L0_ffn_B_fc': (0.0, 0.1),
     'L0_ffn_b_proj': (0.0, 0.1),
     'L0_ffn_B_proj': (0.0, 0.1),
     'L1_ffn_b_in': (0.0, 0.1),
     'L1_ffn_b_out': (0.0, 0.1),
     'L2_xattn_bq': (0.0, 0.768),
     'L2_xattn_bk': (0.0, 0.8),
     'L2_xattn_bv': (0.0, 0.1),
     'L3_xattn_ln1_g': (1.0, 0.2),
     'L3_xattn_ln1_b': (0.0, 0.1),
     'L3_xattn_ln2_g': (1.0, 0.2),
     'L3_xattn_ln2_b': (0.0, 0.1),
     'L3_xattn_a1_li1_b': (0.0, 0.1),
     'L3_xattn_a1_lnx_g': (1.0, 0.6),
     'L3_xattn_a1_lnx_b': (0.0, 0.8),
     'L3_xattn_a1_lny_g': (1.0, 0.6),
     'L3_xattn_a1_lny_b': (0.0, 0.637),
     'L3_xattn_a1_ln3_g': (1.0, 0.2),
     'L3_xattn_a1_ln3_b': (0.0, 0.526),
     'L3_xattn_a1_li2_b': (0.0, 0.1),
     'L3_xattn_a1_li3_b': (0.0, 0.1),
     'L3_xattn_a2_li1_b': (0.0, 0.1),
     'L3_xattn_a2_lnx_g': (1.0, 0.6),
     'L3_xattn_a2_lnx_b': (0.0, 0.8),
     'L3_xattn_a2_lny_g': (1.0, 0.6),
     'L3_xattn_a2_lny_b': (0.0, 0.64),
     'L3_xattn_a2_ln3_g': (1.0, 0.2),
     'L3_xattn_a2_ln3_b': (0.0, 0.518),
     'L3_xattn_a2_li2_b': (0.0, 0.1),
     'L3_xattn_a2_li3_b': (0.0, 0.1),
     'L3_ffn_gate_bias': (0.0, 0.706)}
    factors = {'L3_xattn_a1_wq': 8.0,
     'L3_xattn_a1_wk': 8.0,
     'L3_xattn_a2_wq': 8.0,
     'L3_xattn_a2_wk': 8.0,
     'L3_ffn_gate_w': 5.546,
     'L3_ffn_gate_proj': 3.7,
     'L3_ffn_up_proj': 3.678,
     'L3_ffn_down_proj': 3.673}
    for name, (base, spread) in spreads.items():
        noise = np.random.default_rng([zlib.crc32(name.encode()), seed]).standard_normal(out[name].shape)
        drawn = base * np.exp(spread * noise) if base else spread * noise
        out[name] = jnp.asarray(drawn.astype(out[name].dtype))
    for name, factor in factors.items():
        out[name] = (out[name] * factor).astype(out[name].dtype)
    return out
```

```python
import concourse.bass as bass
from concourse import mybir
from contextlib import ExitStack

F32 = mybir.dt.float32
U32 = mybir.dt.uint32
ALU = mybir.AluOpType
ACT = mybir.ActivationFunctionType
AX, AXY = mybir.AxisListType.X, mybir.AxisListType.XY
RMAX = bass.bass_isa.ReduceOp.max

P = 128
B, T, C = 4, 512, 256
QT = T // P
NT = B * QT
KC = C // P
TC, CC = 64, 128
H = 16
FF = 4 * C
FC = FF // P
D0, D3 = 16, 32
SLOT = 32
G = H * SLOT // P
RANK = 16
E2, CAP = 8, 640
E3, I3 = 16, 352
NX3 = E3 + 2
IC3 = [128, 128, 96]
EPS = 1e-5
ROUND = 12582912.0
NEG = -1e30

PACKS = {
    "w0a": dict(wq=2 * 512, wk=2 * 512, wv=2 * 256, wcq=2 * 256, wck=256, wcv=256, wp=2 * 256,
                bq=4, bk=4, bcq=2, bck=2),
    "w0f": dict(wfc=2 * FF, wproj=FC * 256, afc=2 * RANK, aproj=FC * RANK, bfc=FC),
    "w1a": dict(wq=2 * 256, wk=256, wv=256, wo=2 * 256),
    "w1f": dict(winT=FC * 256, wout=FC * 256, bin=FC),
    "w2a": dict(wq=2 * 256, wk=256, wv=256, bq=2, bk=2, wg=2 * E2),
    "w3a": dict(wq=2 * 512, wk=2 * 512, wv=2 * 512, li1=4 * 256, li2=2 * FF, li3=FC * 256,
                xg=2, xb=2, yg=2, yb=2, g3=2, b3=2, bh=FC),
    "w3b": dict(wq=2 * 512, wk=512, wv=512, li1=4 * 256, li2=2 * FF, li3=FC * 256,
                xg=2, xb=2, yg=1, yb=1, g3=2, b3=2, bh=FC),
    "w3g": dict(gw=2 * E3),
}
ROWS = ["b0v", "b0cv", "b0p", "b0proj", "b1out", "b2v", "ln1g", "ln1b", "ln2g", "ln2b",
        "a1li1b", "a1li3b", "a2li1b", "a2li3b"]
NROWS = len(ROWS) * C + E3
S2 = E2 * CAP
GT2 = (3, 2)
W2X = 2 * FF + FC * 256
W3X = 2 * 2 * I3 + 3 * 256


def width(pack):
    return sum(PACKS[pack].values())


def program(nc, stop, x_in, ctxT_in, ctx_in, gates_in, packs_in, lora_in, rows_in, e2_in, e3_in, slots2, yslots2, out):
    ctx = ExitStack()
    with ctx:
        def sems(stage, names):
            return dict(**{n: ctx.enter_context(nc.semaphore(f"{stage}_{n}")) for n in names.split()})

        LAY, at = {}, 0
        regions = [("X", NT * C), ("rows", NROWS), ("lora", FF + C),
                   ("ident", P), ("ones", P), ("causal", P), ("later", P), ("upto", P), ("ctx", 3 * B * TC),
                   ("in16", 8), ("in32", 4), ("in64", 2), ("lower", E3 * E3), ("gates", 8),
                   ("tgate", 8), ("small", 860),
                   ("qT", 4 * T), ("kT", 4 * T), ("V", QT * 512), ("y", QT * 512), ("spare", 1024),
                   ("xn", QT * C), ("xT", KC * T), ("yT", KC * T), ("Pr", 2 * 1024), ("PT", 2 * 1024),
                   ("kv", 10368), ("wa", width("w0a") + width("w0f") + width("w1a")), ("wf", 2 * 2048 + FC)]
        for name, n in regions:
            LAY[name] = (at, n)
            at += n
        arena = ctx.enter_context(nc.sbuf_tensor("arena", [P, at], F32))
        row_of2 = ctx.enter_context(nc.sbuf_tensor("row_of2", [P, 2 * NT], U32))
        spare_u = ctx.enter_context(nc.sbuf_tensor("spare_u", [P, 2 * NT], U32))
        slot_of2 = ctx.enter_context(nc.sbuf_tensor("slot_of2", [P, 2 * NT], U32))
        zeros = ctx.enter_context(nc.sbuf_tensor("zeros", [P, C], F32))

        def region(name, off=0, n=None):
            a, size = LAY[name]
            n = size - off if n is None else n
            assert off + n <= at - a
            return arena[:, a + off:a + off + n]

        def view(name, pattern, start=0, cols=None, **k):
            return region(name, start, cols).rearrange(pattern, **k)

        PS = ctx.enter_context(nc.psum_tensor("PS", [P, 8, 512], F32))
        X = view("X", "p (t c) -> p t c", c=C)
        XN = view("V", "p (t c) -> p t c", 0, NT * C, c=C)
        XNT = view("V", "p (k n) -> p k n", 0, KC * NT * P, k=KC)
        ident = region("ident")
        ones = region("ones")
        small = region("small")
        tg = region("tgate")
        xn = view("xn", "p (t c) -> p t c", c=C)
        xT = view("xT", "p (k n) -> p k n", k=KC)
        xT2 = view("y", "p (k n) -> p k n", 0, KC * T, k=KC)
        x1 = view("spare", "p (t c) -> p t c", c=C)
        xo = view("yT", "p (t c) -> p t c", c=C)
        qT = view("qT", "p (k n) -> p k n", n=T)
        kT = view("kT", "p (k n) -> p k n", n=T)
        hT = arena[:, LAY["qT"][0]:LAY["qT"][0] + FC * T].rearrange("p (k n) -> p k n", n=T)
        PRB = [region("Pr", i * 512, 512) for i in range(2)]
        PTB = [region("PT", i * 512, 512) for i in range(2)]
        row = {n: region("rows", i * C, C) for i, n in enumerate(ROWS)}
        gbias = region("rows", len(ROWS) * C, E3)

        def pack_views(names, start, name):
            off = start
            res = {}
            for pk in names:
                d = {}
                for k, n in PACKS[pk].items():
                    d[k] = region(name, off, n)
                    off += n
                res[pk] = dict(**d)
            return res
        W = pack_views(["w0a", "w0f", "w1a"], 0, "wa")
        W.update(pack_views(["w1f"], 0, "wf"))
        W2A_OFF = 0
        W.update(pack_views(["w2a"], 0, "kv"))
        W3_OFF = width("w2a") + 64
        W.update(pack_views(["w3a", "w3b", "w3g"], W3_OFF, "kv"))
        KV3_OFF = W3_OFF + width("w3a") + width("w3b") + width("w3g")
        win = region("Pr", 0, 2 * FF)

        def kv_views(name, off, d):
            nch = H * d // P
            kb = region(name, off, nch * B * (P // d) * TC).rearrange("p (c b n) -> p c b n", c=nch, b=B)
            off += nch * B * (P // d) * TC
            nv = H // 2 * 2 * (d + 1)
            vb = region(name, off, B * nv).rearrange("p (b r e) -> p b r e", b=B, r=H // 2)
            return dict(k=kb, v=vb, d=d, nch=nch), off + B * nv
        kv0, o1 = kv_views("kv", 0, D0)
        kv1, o1 = kv_views("kv", o1, D0)
        kv3, o3 = kv_views("kv", KV3_OFF, D3)
        assert LAY["kv"][0] + o3 <= at, (LAY["kv"][0] + o3, at)
        assert o1 <= 10368

        ctxT = None
        ctxdup = region("ctx", 0, B * 2 * TC).rearrange("p (b j n) -> p b j n", b=B, j=2)
        ctxT = region("ctx", B * 2 * TC, B * TC)

        so = [0]

        def scratch(n):
            so[0] += n
            assert so[0] <= LAY["small"][1], so[0]
            return small[:, so[0] - n:so[0]]
        stats = scratch(QT * 6)
        mv = scratch(QT * 2)
        rstd = scratch(QT)
        varp = scratch(QT)
        nmax = scratch(64)
        rsum = scratch(64)
        rrec = scratch(64)
        amax = scratch(16)
        mhalf = scratch(4)
        carrier = scratch(1)
        cround = scratch(1)
        wcomb = scratch(NT * NX3)
        aw = scratch(3 * 16)
        ax = scratch(16)
        mv3 = mv.rearrange("p (t k) -> p t k", k=2)

        ld = sems("ld", "zeroed x ctx small w0a w0f w1a w1f w2a w3a w3b w3g e2 e3 stored ctx3")
        cst = sems("const", "step ready")
        norm = sems("norm", "var rstd")
        xf = sems("features", "xn_ready xT_psum xT_act xT_dve")
        N_L01, N_D, N_E, N_F, N_CTX, N_G, N_H = 0, 12, 16, 20, 24, 25, 49
        J_D, J_E, J_F, J_G, J_H = 12, 16, 20, 24, 40

        class Chain:
            def __init__(self, eng, sem, base=0, it=None, per=0):
                self.eng, self.sem, self.base, self.it, self.per, self.n = eng, sem, base, it, per, 0

            def value(self, n):
                return self.base + (n if self.it is None else self.it * self.per + n)

            def mark(self, ins):
                ins.then_inc(self.sem, 1)
                self.n += 1
                return self.n

            def wait(self, n):
                self.eng.wait_ge(self.sem, self.value(n))

            def link(self, ins):
                self.wait(self.mark(ins))

            def close(self):
                assert self.it is None or self.n == self.per, f"{self.sem}: {self.n} steps, {self.per} said"

            def after(self, iterations=1):
                return self.base + self.n * iterations

        def dve_norm(ch, it, src, dst, n=QT):
            v = nc.vector
            v.memset(carrier, 0.0)
            for t in range(n):
                last = v.bn_stats(stats[:, 6 * t:6 * t + 6], src(t))
            ch.link(last)
            v.memset(carrier, 0.0)
            for t in range(n):
                last = v.bn_aggr(mv[:, 2 * t:2 * t + 2], stats[:, 6 * t:6 * t + 6])
            ch.link(last)
            v.tensor_scalar(varp[:, 0:n], mv3[:, 0:n, 1], EPS, None, ALU.add).then_inc(norm["var"], 1)
            v.wait_ge(norm["rstd"], it + 1)
            for t in range(n):
                last = v.tensor_scalar(dst(t), src(t), mv[:, 2 * t:2 * t + 1], rstd[:, t:t + 1],
                                       ALU.subtract, ALU.mult)
            return last

        def pool_norm(pool, it, n=QT):
            pool.wait_ge(norm["var"], it + 1)
            nc.gpsimd.tensor_tensor(rstd[:, 0:n], varp[:, 0:n], mhalf[:, 0:n], ALU.pow).then_inc(norm["rstd"], 1)

        def pe_to_features(src, nchunk, bank0):
            last = []
            for c in range(nchunk):
                for t in range(QT):
                    ins = nc.tensor.transpose(PS[:, bank0 + c, t * P:(t + 1) * P],
                                              src[:, t, c * P:(c + 1) * P], ident)
                last.append(ins)
            return last

        def pe_features(pe, j):
            pe.wait_ge(xf["xn_ready"], j + 1)
            for ins in pe_to_features(xn, KC, 6):
                ins.then_inc(xf["xT_psum"], 1)
            pe.wait_ge(xf["xT_act"], j + 1)
            pe.wait_ge(xf["xT_dve"], j + 1)

        def pe_context(pe, s, kv, wk, wv, kT_src, vdup, ready):
            ready()
            for c in range(kv["nch"]):
                nc.tensor.matmul(PS[:, c, 0:B * TC], wk[:, c * P:(c + 1) * P], kT_src,
                                 start=True, stop=True).then_inc(s["kv_psum"], 1)
            for b in range(B):
                nc.tensor.matmul(PS[:, 4 + b, 0:H * kv["d"]], vdup(b), wv, start=True, stop=True).then_inc(s["kv_psum"], 1)

        def dve_context(v, s, kv, inmask, bk, bv, tmp, ch):
            hc = P // kv["d"]
            for c in range(kv["nch"]):
                v.wait_ge(s["kv_psum"], c + 1)
                src = PS[:, c, 0:B * TC]
                if bk is not None:
                    t = tmp[:, c * B * TC:(c + 1) * B * TC]
                    ch.link(nc.vector.tensor_scalar(t, src, bk[:, c:c + 1], None, ALU.add))
                    src = t
                for b in range(B):
                    nc.vector.tensor_tensor(
                        kv["k"][:, c, b, :].rearrange("p (h n) -> p h n", h=hc),
                        src[:, b * TC:(b + 1) * TC].unsqueeze(1).to_broadcast([P, hc, TC]),
                        inmask.unsqueeze(2).to_broadcast([P, hc, TC]), ALU.mult).then_inc(s["kv_ready"], 1)
            for b in range(B):
                v.wait_ge(s["kv_psum"], kv["nch"] + b + 1)
                src = PS[:, 4 + b, 0:H * kv["d"]]
                if bv is not None:
                    at0 = kv["nch"] * B * TC + b * H * kv["d"]
                    t = tmp[:, at0:at0 + H * kv["d"]]
                    ch.link(nc.vector.tensor_tensor(t, src, bv, ALU.add))
                    src = t
                vb = kv["v"][:, b].rearrange("p r (j e) -> p r j e", j=2)
                for j in range(2):
                    nc.vector.tensor_scalar(
                        vb[:, :, j, 0:kv["d"]],
                        src.rearrange("p (r j e) -> p r j e", j=2, e=kv["d"])[:, :, j, :],
                        half[:, j:j + 1], None, ALU.mult).then_inc(s["kv_ready"], 1)
                    nc.vector.tensor_copy(vb[:, :, j, kv["d"]:kv["d"] + 1],
                                          half[:, j:j + 1].unsqueeze(1).to_broadcast([P, H // 2, 1])
                                          ).then_inc(s["kv_ready"], 1)

        half = region("in64")

        def kv_count(kv):
            return kv["nch"] * B + B * 4

        SELF = [(g, hh, qt) for g in range(G) for hh in range(4) for qt in range(QT)]
        NS = len(SELF)
        SELF_SEMS = ("proj_psum proj_act proj_dve scores nmax probs pT_psum pT "
                     "heads y")

        def evac_engines(values_on):
            return "da" * G + values_on * QT

        def nth(e, engines, j):
            return engines[:j + 1].count(e)

        def keys_of(qt, causal):
            return (list(range(qt + 1)), (qt + 1) * P) if causal else (list(range(qt, QT)), T)

        def pe_self(pe, s, it, j, cfg):
            engines = cfg["engines"]
            n_a, n_d = engines.count("a"), engines.count("d")
            pe_features(pe, j)
            for i, e in enumerate(engines):
                if i >= 2:
                    before = engines[i - 2]
                    if before == "a":
                        pe.wait_ge(s["proj_act"], it * n_a + nth("a", engines, i - 2))
                    else:
                        pe.wait_ge(s["proj_dve"], it * n_d + nth("d", engines, i - 2))
                for k in range(KC):
                    if i < 2 * G:
                        w = (cfg["wq"], cfg["wk"])[i % 2][:, k * 512 + (i // 2) * P:k * 512 + (i // 2 + 1) * P]
                        src = (cfg["xq"], cfg["xkv"])[i % 2]
                        ins = nc.tensor.matmul(PS[:, 6 + i % 2, :], w, src[:, k, :], start=k == 0, stop=k == KC - 1)
                    else:
                        t = i - 2 * G
                        nv = H * cfg["d"]
                        ins = nc.tensor.matmul(PS[:, 6 + i % 2, 0:nv], cfg["xkv"][:, k, t * P:(t + 1) * P],
                                               cfg["wv"][:, k * nv:(k + 1) * nv], start=k == 0, stop=k == KC - 1)
                ins.then_inc(s["proj_psum"], 1)
            pe.wait_ge(s["proj_act"], it * n_a + n_a)
            pe.wait_ge(s["proj_dve"], it * n_d + n_d)

            for n in range(NS + 2):
                if n < NS:
                    g, hh, qt = SELF[n]
                    if n >= 2:
                        pe.wait_ge(s["probs"], it * NS + n - 1)
                    kcs, w = keys_of(qt, cfg["causal"])
                    rows = slice(SLOT * hh, SLOT * (hh + 1))
                    ins = nc.tensor.matmul(PS[:, n % 2, 0:w], qT[rows, g, qt * P:(qt + 1) * P], kT[rows, g, 0:w],
                                           start=True, stop=not cfg["causal"])
                    if cfg["causal"]:
                        ins = nc.tensor.matmul(PS[:, n % 2, qt * P:w], ident, region("causal"), start=False, stop=True)
                    ins.then_inc(s["scores"], 1)
                m = n - 1
                if 0 <= m < NS:
                    g, hh, qt = SELF[m]
                    kcs, w = keys_of(qt, cfg["causal"])
                    pe.wait_ge(s["probs"], it * NS + m + 1)
                    if m >= 2:
                        pe.wait_ge(s["pT"], it * NS + m - 1)
                    for kc in kcs:
                        ins = nc.tensor.transpose(PS[:, 2 + m % 2, kc * P:(kc + 1) * P],
                                                  PRB[m % 2][:, kc * P:(kc + 1) * P], ident)
                    ins.then_inc(s["pT_psum"], 1)
                m = n - 2
                if m >= 0:
                    g, hh, qt = SELF[m]
                    kcs, w = keys_of(qt, cfg["causal"])
                    pe.wait_ge(s["pT"], it * NS + m + 1)
                    if hh == 0 and qt == 0 and g >= 2:
                        pe.wait_ge(s["y"], it * G + g - 1)
                    col = (hh * QT + qt) * cfg["d"]
                    h = g * 4 + hh
                    for kc in kcs:
                        ins = nc.tensor.matmul(PS[:, 4 + g % 2, col:col + cfg["d"]],
                                               PTB[m % 2][:, kc * P:(kc + 1) * P],
                                               cfg["V"][:, kc, h * cfg["d"]:(h + 1) * cfg["d"]],
                                               start=kc == kcs[0], stop=kc == kcs[-1])
                    ins.then_inc(s["heads"], 1)

        def act_self(act, s, it, j, cfg):
            engines = cfg["engines"]
            act.wait_ge(xf["xT_psum"], XT(j))
            cfg["copy_x_act"]()
            for i, e in enumerate(engines):
                if e == "a":
                    act.wait_ge(s["proj_psum"], it * len(engines) + i + 1)
                    if i < 2 * G:
                        bias = cfg["bk"][:, i // 2:i // 2 + 1] if cfg["bk"] is not None else 0.0
                        nc.scalar.activation(kT[:, i // 2, :], PS[:, 6 + i % 2, :], ACT.Identity, bias=bias
                                             ).then_inc(s["proj_act"], 1)
                    else:
                        nc.scalar.activation(cfg["V"][:, i - 2 * G, :], PS[:, 6 + i % 2, 0:H * cfg["d"]], ACT.Copy
                                             ).then_inc(s["proj_act"], 1)
            for n in range(NS):
                g, hh, qt = SELF[n]
                kcs, w = keys_of(qt, cfg["causal"])
                act.wait_ge(s["nmax"], it * NS + n + 1)
                if n >= 2:
                    act.wait_ge(s["pT_psum"], it * NS + n - 1)
                nc.scalar.activation(PRB[n % 2][:, 0:w], PS[:, n % 2, 0:w], ACT.Exp, bias=nmax[:, n:n + 1],
                                     accum_out=rsum[:, n:n + 1]).then_inc(s["probs"], 1)

        def dve_self(v, s, it, j, cfg, ch):
            engines = cfg["engines"]
            v.wait_ge(xf["xT_psum"], XT(j))
            cfg["copy_x_dve"]()
            for i, e in enumerate(engines):
                if e == "d":
                    v.wait_ge(s["proj_psum"], it * len(engines) + i + 1)
                    if i < 2 * G:
                        if cfg["bq"] is not None:
                            nc.vector.tensor_scalar(qT[:, i // 2, :], PS[:, 6 + i % 2, :], cfg["bq"][:, i // 2:i // 2 + 1],
                                                    cfg["scale"], ALU.add, ALU.mult).then_inc(s["proj_dve"], 1)
                        else:
                            nc.vector.tensor_scalar(qT[:, i // 2, :], PS[:, 6 + i % 2, :], cfg["scale"], None,
                                                    ALU.mult).then_inc(s["proj_dve"], 1)
                    else:
                        prod = PS[:, 6 + i % 2, 0:H * cfg["d"]]
                        if cfg["bv"] is not None:
                            ins = nc.vector.tensor_tensor(cfg["V"][:, i - 2 * G, :], prod, cfg["bv"], ALU.add)
                        else:
                            ins = nc.vector.tensor_copy(cfg["V"][:, i - 2 * G, :], prod)
                        ins.then_inc(s["proj_dve"], 1)

            def group_out(g):
                v.wait_ge(s["heads"], it * NS + (g + 1) * 16)
                ch.link(nc.vector.reciprocal(rrec[:, g * 16:(g + 1) * 16], rsum[:, g * 16:(g + 1) * 16]))
                for hh in range(4):
                    h = g * 4 + hh
                    ins = nc.vector.tensor_tensor(
                        cfg["y"][:, :, h * cfg["d"]:(h + 1) * cfg["d"]],
                        PS[:, 4 + g % 2, hh * QT * cfg["d"]:(hh + 1) * QT * cfg["d"]].rearrange("p (t d) -> p t d", t=QT),
                        rrec[:, g * 16 + hh * 4:g * 16 + hh * 4 + 4].unsqueeze(2).to_broadcast([P, QT, cfg["d"]]),
                        ALU.mult)
                ins.then_inc(s["y"], 1)

            for n in range(NS + 1):
                if n < NS:
                    g, hh, qt = SELF[n]
                    kcs, w = keys_of(qt, cfg["causal"])
                    v.wait_ge(s["scores"], it * NS + n + 1)
                    nc.vector.tensor_reduce(nmax[:, n:n + 1], PS[:, n % 2, 0:w], AX, ALU.max, negate=True
                                            ).then_inc(s["nmax"], 1)
                m = n - 1
                if m >= 0:
                    g, hh, qt = SELF[m]
                    kcs, w = keys_of(qt, cfg["causal"])
                    v.wait_ge(s["pT_psum"], it * NS + m + 1)
                    if m >= 2:
                        v.wait_ge(s["heads"], it * NS + m - 1)
                    lo, hi = kcs[0] * P, (kcs[-1] + 1) * P
                    if cfg["causal"]:
                        ins = nc.vector.tensor_copy(PTB[m % 2][:, lo:hi], PS[:, 2 + m % 2, lo:hi])
                    else:
                        ins = nc.vector.tensor_tensor(PTB[m % 2][:, lo:lo + P], PS[:, 2 + m % 2, lo:lo + P],
                                                      region("later"), ALU.mult)
                        if hi > lo + P:
                            ins = nc.vector.tensor_copy(PTB[m % 2][:, lo + P:hi], PS[:, 2 + m % 2, lo + P:hi])
                    ins.then_inc(s["pT"], 1)
                if n % 16 == 4 and n > 16:
                    group_out(n // 16 - 1)
            group_out(G - 1)

        CROSS_SEMS = "q_psum q scores shifted probs pT_psum pT heads y"

        def pe_cross(pe, s, it, j, b, cfg):
            kv = cfg["kv"]
            if cfg["norm"]:
                pe_features(pe, j)
            for c in range(kv["nch"]):
                if c >= 2:
                    pe.wait_ge(s["q"], it * 4 + (c - 1) * (4 // kv["nch"]))
                for k in range(KC):
                    ins = nc.tensor.matmul(PS[:, 6 + c % 2, :], cfg["wq"][:, k * H * kv["d"] + c * P:k * H * kv["d"] + (c + 1) * P],
                                           xT[:, k, :], start=k == 0, stop=k == KC - 1)
                ins.then_inc(s["q_psum"], 4 // kv["nch"])
            pe.wait_ge(s["q"], it * 4 + 4)

            def scores(t):
                if t >= 2:
                    pe.wait_ge(s["shifted"], it * QT + t - 1)
                per = (P // kv["d"]) * TC
                for c in range(kv["nch"]):
                    bank, col = divmod(c * per, 512)
                    ins = nc.tensor.matmul(PS[:, 2 * (t % 2) + bank, col:col + per],
                                           qT[:, c, t * P:(t + 1) * P],
                                           kv["k"][:, c, bass.ds(b, 1), :].rearrange("p b n -> p (b n)"),
                                           start=True, stop=True)
                ins.then_inc(s["scores"], 1)
            scores(0)
            for t in range(QT):
                if t + 1 < QT:
                    scores(t + 1)
                pe.wait_ge(s["probs"], it * QT + t + 1)
                if t >= 1:
                    pe.wait_ge(s["pT"], (it * QT + t) * 2)
                for r in range(H // 2):
                    ins = nc.tensor.transpose(PS[:, 4 + r // 4, (r % 4) * P:(r % 4 + 1) * P],
                                              region("Pr", (t % 2) * 1024 + r * P, P), ident)
                    if r % 4 == 3:
                        ins.then_inc(s["pT_psum"], 1)
                pe.wait_ge(s["pT"], (it * QT + t) * 2 + 2)
                if t >= 1:
                    pe.wait_ge(s["y"], it * QT + t)
                for r in range(H // 2):
                    col = (r % 4) * 2 * (kv["d"] + 1)
                    ins = nc.tensor.matmul(PS[:, 6 + r // 4, col:col + 2 * (kv["d"] + 1)],
                                           region("PT", (t % 2) * 1024 + r * P, P),
                                           kv["v"][:, bass.ds(b, 1), r, :].rearrange("p b e -> p (b e)"),
                                           start=True, stop=True)
                ins.then_inc(s["heads"], 1)

        def act_cross(act, s, it, j, b, cfg):
            if cfg["norm"]:
                act.wait_ge(xf["xT_psum"], XT(j))
                cfg["copy_x_act"]()
            for t in range(QT):
                act.wait_ge(s["shifted"], it * QT + t + 1)
                pr = region("Pr", (t % 2) * 1024, 1024)
                nc.scalar.activation(pr, pr, ACT.Exp).then_inc(s["probs"], 1)
                for i in range(2):
                    act.wait_ge(s["pT_psum"], (it * QT + t) * 2 + i + 1)
                    nc.scalar.activation(region("PT", (t % 2) * 1024 + i * 512, 512), PS[:, 4 + i, :], ACT.Copy
                                         ).then_inc(s["pT"], 1)

        def dve_cross(v, s, it, j, b, cfg, ch):
            kv = cfg["kv"]
            if cfg["norm"]:
                v.wait_ge(xf["xT_psum"], XT(j))
                cfg["copy_x_dve"]()
            for c in range(kv["nch"]):
                v.wait_ge(s["q_psum"], it * 4 + (c + 1) * (4 // kv["nch"]))
                if cfg["bq"] is not None:
                    nc.vector.tensor_scalar(qT[:, c, :], PS[:, 6 + c % 2, :], cfg["bq"][:, c:c + 1], cfg["scale"],
                                            ALU.add, ALU.mult).then_inc(s["q"], 4 // kv["nch"])
                else:
                    nc.vector.tensor_scalar(qT[:, c, :], PS[:, 6 + c % 2, :], cfg["scale"], None, ALU.mult
                                            ).then_inc(s["q"], 4 // kv["nch"])

            def shift(t):
                v.wait_ge(s["scores"], it * QT + t + 1)
                if t >= 2:
                    v.wait_ge(s["pT_psum"], (it * QT + t - 1) * 2)
                sc = PS[:, 2 * (t % 2):2 * (t % 2) + 2, :].rearrange("p a (h n) -> p a h n", n=TC)
                mx = nmax[:, t * H:(t + 1) * H]
                ch.link(nc.vector.tensor_reduce(mx, sc, AX, ALU.max))
                nc.vector.tensor_tensor(
                    region("Pr", (t % 2) * 1024, 1024).rearrange("p (a h n) -> p a h n", a=2, n=TC), sc,
                    mx.rearrange("p (a h) -> p a h", a=2).unsqueeze(3).to_broadcast([P, 2, H // 2, TC]), ALU.subtract
                    ).then_inc(s["shifted"], 1)
            shift(0)
            for t in range(QT):
                if t + 1 < QT:
                    shift(t + 1)
                v.wait_ge(s["heads"], it * QT + t + 1)
                o = PS[:, 6:8, 0:H // 2 * (kv["d"] + 1)].rearrange("p a (h e) -> p a h e", e=kv["d"] + 1)
                rr = rrec[:, t * H:(t + 1) * H].rearrange("p (a h) -> p a h", a=2).unsqueeze(3)
                ch.link(nc.vector.reciprocal(rr, o[:, :, :, kv["d"]:kv["d"] + 1]))
                yt = cfg["y"][:, t, :].rearrange("p (a h e) -> p a h e", a=2, e=kv["d"])
                if cfg["add"]:
                    tmp = xn[:, t, :].rearrange("p (a h e) -> p a h e", a=2, e=kv["d"])
                    ch.link(nc.vector.tensor_tensor(tmp, o[:, :, :, 0:kv["d"]],
                                                    rr.to_broadcast([P, 2, H // 2, kv["d"]]), ALU.mult))
                    nc.vector.tensor_tensor(yt, yt, tmp, ALU.add).then_inc(s["y"], 1)
                else:
                    nc.vector.tensor_tensor(yt, o[:, :, :, 0:kv["d"]], rr.to_broadcast([P, 2, H // 2, kv["d"]]),
                                            ALU.mult).then_inc(s["y"], 1)

        OUT_SEMS = "yT_psum yT_act yT_dve out_psum"

        def pe_out(pe, s, it, cfg, y_wait):
            nch = cfg["nch"]
            y_wait()
            for c in range(nch):
                if c >= 2:
                    if c % 2 == 0:
                        pe.wait_ge(s["yT_act"], it * 2 + (c // 2) * (4 // nch))
                    else:
                        pe.wait_ge(s["yT_dve"], it * 2 + (c // 2) * (4 // nch))
                for t in range(QT):
                    ins = nc.tensor.transpose(PS[:, 6 + c % 2, t * P:(t + 1) * P],
                                              cfg["y"][:, t, c * P:(c + 1) * P], ident)
                ins.then_inc(s["yT_psum"], 4 // nch)
            pe.wait_ge(s["yT_act"], it * 2 + 2)
            pe.wait_ge(s["yT_dve"], it * 2 + 2)
            for t in range(QT):
                for c in range(nch):
                    ins = nc.tensor.matmul(PS[:, t // 2, (t % 2) * C:(t % 2 + 1) * C], qT[:, c, t * P:(t + 1) * P],
                                           cfg["wo"][:, c * C:(c + 1) * C], start=c == 0, stop=c == nch - 1)
                if t % 2:
                    ins.then_inc(s["out_psum"], 1)

        def act_out(act, s, it, cfg):
            for c in range(0, cfg["nch"], 2):
                act.wait_ge(s["yT_psum"], it * 4 + (c + 1) * (4 // cfg["nch"]))
                nc.scalar.activation(qT[:, c, :], PS[:, 6, :], ACT.Copy).then_inc(s["yT_act"], 4 // cfg["nch"])

        def dve_yT(v, s, it, cfg):
            for c in range(1, cfg["nch"], 2):
                v.wait_ge(s["yT_psum"], it * 4 + (c + 1) * (4 // cfg["nch"]))
                nc.vector.tensor_copy(qT[:, c, :], PS[:, 7, :]).then_inc(s["yT_dve"], 4 // cfg["nch"])

        def dve_residual(v, s, it, b, bank0, gate, bias, ch):
            for i in range(2):
                v.wait_ge(s["out_psum"], it * 2 + i + 1)
                prod = PS[:, bank0 + i, :].rearrange("p (t c) -> p t c", t=2)
                xt = X[:, bass.ds(b * QT + 2 * i, 2), :]
                if bias is not None:
                    tmp = xn[:, 2 * i:2 * i + 2, :]
                    ch.link(nc.vector.tensor_tensor(tmp, prod, bias.unsqueeze(1).to_broadcast([P, 2, C]), ALU.add))
                    prod = tmp
                ch.link(nc.vector.scalar_tensor_tensor(out=xt, in0=prod, scalar=gate, in1=xt,
                                                       op0=ALU.mult, op1=ALU.add))

        LORA_SEMS = " a_psum a a2_psum a2"
        FFN_SEMS = "h_psum h out_psum"

        def pe_ffn(pe, s, it, j, cfg):
            pe_features(pe, j)
            if cfg["lora"]:
                for k in range(KC):
                    ins = nc.tensor.matmul(PS[0:RANK, 6, :], W["w0f"]["afc"][:, k * RANK:(k + 1) * RANK], xT[:, k, :],
                                           start=k == 0, stop=k == KC - 1)
                ins.then_inc(s["a_psum"], 1)
            for f in range(FC):
                if f >= 4:
                    pe.wait_ge(s["h"], it * FC + f - 3)
                for k in range(KC):
                    ins = nc.tensor.matmul(PS[:, f % 4, :], cfg["w1"][:, k * FF + f * P:k * FF + (f + 1) * P], xT[:, k, :],
                                           start=k == 0, stop=k == KC - 1 and not cfg["lora"])
                if cfg["lora"]:
                    if f == 0:
                        pe.wait_ge(s["a"], it + 1)
                    ins = nc.tensor.matmul(PS[:, f % 4, :], lora_fc[:, f * P:(f + 1) * P], loraT, start=False, stop=True)
                ins.then_inc(s["h_psum"], 1)
            for t in range(QT):
                for f in range(FC):
                    if t == 0:
                        pe.wait_ge(s["h"], it * FC + f + 1)
                    ins = nc.tensor.matmul(PS[:, 4 + t // 2, (t % 2) * C:(t % 2 + 1) * C], hT[:, f, t * P:(t + 1) * P],
                                           cfg["w2"][:, f * C:(f + 1) * C], start=f == 0, stop=f == FC - 1 and not cfg["lora"])
                if cfg["lora"]:
                    if t == 0:
                        for f in range(FC):
                            ins = nc.tensor.matmul(PS[0:RANK, 6, :], W["w0f"]["aproj"][:, f * RANK:(f + 1) * RANK],
                                                   hT[:, f, :], start=f == 0, stop=f == FC - 1)
                        ins.then_inc(s["a2_psum"], 1)
                        pe.wait_ge(s["a2"], it + 1)
                    ins = nc.tensor.matmul(PS[:, 4 + t // 2, (t % 2) * C:(t % 2 + 1) * C],
                                           loraT[:, t * P:(t + 1) * P], lora_proj, start=False, stop=True)
                if t % 2:
                    ins.then_inc(s["out_psum"], 1)

        def act_ffn(act, s, it, j, cfg):
            act.wait_ge(xf["xT_psum"], XT(j))
            cfg["copy_x_act"]()
            for f in range(FC):
                act.wait_ge(s["h_psum"], it * FC + f + 1)
                nc.scalar.activation(hT[:, f, :], PS[:, f % 4, :], ACT.Gelu, bias=cfg["b1"][:, f:f + 1]).then_inc(s["h"], 1)

        def dve_ffn(v, s, it, j, cfg):
            v.wait_ge(xf["xT_psum"], XT(j))
            cfg["copy_x_dve"]()
            if cfg["lora"]:
                v.wait_ge(s["a_psum"], it + 1)
                nc.vector.tensor_scalar(loraT, PS[0:RANK, 6, :], 2.0, None, ALU.mult).then_inc(s["a"], 1)
                v.wait_ge(s["a2_psum"], it + 1)
                nc.vector.tensor_scalar(loraT, PS[0:RANK, 6, :], 2.0, None, ALU.mult).then_inc(s["a2"], 1)

        lora_fc = arena[0:RANK, LAY["lora"][0]:LAY["lora"][0] + FF]
        lora_proj = arena[0:RANK, LAY["lora"][0] + FF:LAY["lora"][0] + FF + C]
        loraT = arena[0:RANK, LAY["Pr"][0]:LAY["Pr"][0] + T]

        def plain_copy_act():
            nc.scalar.activation(xT[:, 0, :], PS[:, 6, :], ACT.Copy).then_inc(xf["xT_act"], 1)

        def plain_copy_dve():
            nc.vector.tensor_copy(xT[:, 1, :], PS[:, 7, :]).then_inc(xf["xT_dve"], 1)

        def XT(j):
            return j * KC + KC

        def scaled_copies(g, bb, g2=None, b2=None):
            def a():
                ins = nc.scalar.activation(xT[:, 0, :], PS[:, 6, :], ACT.Identity, bias=bb[:, 0:1], scale=g[:, 0:1])
                if g2 is not None:
                    ins = nc.scalar.activation(xT2[:, 0, :], PS[:, 6, :], ACT.Identity, bias=b2[:, 0:1],
                                               scale=g2[:, 0:1])
                ins.then_inc(xf["xT_act"], 1)

            def d():
                ins = nc.vector.tensor_scalar(xT[:, 1, :], PS[:, 7, :], g[:, 1:2], bb[:, 1:2], ALU.mult, ALU.add)
                if g2 is not None:
                    ins = nc.vector.tensor_scalar(xT2[:, 1, :], PS[:, 7, :], g2[:, 1:2], b2[:, 1:2],
                                                  ALU.mult, ALU.add)
                ins.then_inc(xf["xT_dve"], 1)
            return a, d

        w0, w0f, w1, w3, w3b = W["w0a"], W["w0f"], W["w1a"], W["w3a"], W["w3b"]
        V0 = region("V", 0, QT * H * D0).rearrange("p (t c) -> p t c", t=QT)
        y0 = region("y", 0, QT * H * D0).rearrange("p (t c) -> p t c", t=QT)
        V3 = region("V", 0, QT * H * D3).rearrange("p (t c) -> p t c", t=QT)
        y3 = region("y", 0, QT * H * D3).rearrange("p (t c) -> p t c", t=QT)
        c0s = dict(engines=evac_engines("d"), wq=w0["wq"], wk=w0["wk"], wv=w0["wv"], xq=xT, xkv=xT, d=D0, causal=True,
                  V=V0, y=y0, bq=w0["bq"], bk=w0["bk"], bv=row["b0v"], scale=D0 ** -0.5,
                  copy_x_act=plain_copy_act, copy_x_dve=plain_copy_dve)
        c0c = dict(kv=kv0, norm=False, wq=w0["wcq"], bq=w0["bcq"], scale=D0 ** -0.5, y=y0, add=True)
        c0o = dict(nch=2, y=y0, wo=w0["wp"])
        c0f = dict(lora=True, w1=w0f["wfc"], w2=w0f["wproj"], b1=w0f["bfc"],
                  copy_x_act=plain_copy_act, copy_x_dve=plain_copy_dve)
        c1c = dict(kv=kv1, norm=True, wq=w1["wq"], bq=None, scale=D0 ** -0.5, y=y0, add=False,
                  copy_x_act=plain_copy_act, copy_x_dve=plain_copy_dve)
        c1o = dict(nch=2, y=y0, wo=w1["wo"])
        s0k, s1k = sems("kv0", "kv_psum kv_ready"), sems("kv1", "kv_psum kv_ready")
        ss, sc_, so_, sf = (sems("self", SELF_SEMS), sems("cross", CROSS_SEMS), sems("outproj", OUT_SEMS),
                            sems("ffn", FFN_SEMS + LORA_SEMS))
        sq = sems("quant", "amax all w0 w0scale w1scale w1")
        gate_ready = sems("gate", "ready")["ready"]
        dve_step = sems("dve", "step")["step"]
        done = sems("done", "l01 l1ffn l2a route2 l2moe l3a route3 all")

        sd = sems("l1ffn", "win_psum win_act win_dve amax amax_all scale xq_act xq h_psum h hq_act hq out_psum "
                           "used")
        w1f = W["w1f"]
        Hall = arena[:, LAY["kv"][0]:LAY["kv"][0] + FC * B * T].rearrange("p (f n) -> p f n", f=FC)
        assert FC * B * T <= LAY["kv"][1] + LAY["wa"][1]
        lag = ax

        def rows_of(b):
            return bass.ds(b * T, T)

        def pe_l1ffn(pe):
            s = sd
            pe.wait_ge(sq["w1"], 2)
            pe.wait_ge(done["l01"], 1)
            for k in range(KC):
                for f in range(FC):
                    ins = nc.tensor.transpose(PS[:, 2 * k + f // 4, (f % 4) * P:(f % 4 + 1) * P],
                                              w1f["winT"][:, f * C + k * P:f * C + (k + 1) * P], ident)
                ins.then_inc(s["win_psum"], 1)
            with pe.Fori(0, B) as b:
                pe_features(pe, b + J_D)
            pe.wait_ge(s["win_act"], 1)
            pe.wait_ge(s["win_dve"], 1)
            with pe.Fori(0, B) as b:
                pe.wait_ge(s["xq"], b + 1)
                for f in range(FC):
                    if f >= 4:
                        pe.wait_ge(s["h"], b * FC + f - 3)
                    for k in range(KC):
                        ins = nc.tensor.matmul(PS[:, f % 4, :], win[:, k * FF + f * P:k * FF + (f + 1) * P],
                                               xT[:, k, :], start=k == 0, stop=k == KC - 1)
                    ins.then_inc(s["h_psum"], 1)
            with pe.Fori(0, B) as b:
                for t in range(QT):
                    for f in range(FC):
                        if t == 0:
                            pe.wait_ge(s["hq"], b * FC + f + 1)
                        ins = nc.tensor.matmul(PS[:, 4 + t // 2, (t % 2) * C:(t % 2 + 1) * C],
                                               hT[:, f, t * P:(t + 1) * P], w1f["wout"][:, f * C:(f + 1) * C],
                                               start=f == 0, stop=f == FC - 1)
                    if t % 2:
                        ins.then_inc(s["out_psum"], 1)
                nc.tensor.matmul(PS[0:1, 7, 0:1], ident[:, 0:1], ident[:, 0:1], start=True, stop=True
                                 ).then_inc(s["used"], 1)

        def act_l1ffn(act):
            s = sd
            act.wait_ge(s["win_psum"], 1)
            nc.scalar.activation(win[:, 0:FF], PS[:, 0:2, :].rearrange("p a n -> p (a n)"), ACT.Copy
                                 ).then_inc(s["win_act"], 1)
            with act.Fori(0, B) as b:
                act.wait_ge(xf["xT_psum"], XT(b + J_D))
                nc.scalar.activation(XNT[:, 0, rows_of(b)], PS[:, 6, :], ACT.Copy).then_inc(xf["xT_act"], 1)
            act.wait_ge(s["scale"], 1)
            with act.Fori(0, B) as b:
                for k in range(KC):
                    ins = nc.scalar.activation(xT[:, k, :], XNT[:, k, rows_of(b)], ACT.Identity, bias=cround,
                                               scale=ax[:, 11:12])
                ins.then_inc(s["xq_act"], 1)
                for f in range(FC):
                    act.wait_ge(s["h_psum"], b * FC + f + 1)
                    nc.scalar.activation(Hall[:, f, rows_of(b)], PS[:, f % 4, :], ACT.Gelu, bias=w1f["bin"][:, f:f + 1]
                                         ).then_inc(s["h"], 1)
            act.wait_ge(s["scale"], 2)
            with act.Fori(0, B) as b:
                act.wait_ge(s["used"], b + 1)
                for f in range(FC):
                    nc.scalar.activation(hT[:, f, :], Hall[:, f, rows_of(b)], ACT.Identity, bias=cround,
                                         scale=ax[:, 15:16]).then_inc(s["hq_act"], 1)

        def pool_l1ffn(pool):
            for b in range(B):
                pool_norm(pool, N_D + b)
            for i in range(2):
                pool.wait_ge(sd["amax"], i + 1)
                nc.gpsimd.partition_all_reduce(ax[:, 9 + 4 * i:10 + 4 * i], ax[:, 8 + 4 * i:9 + 4 * i], P, RMAX
                                               ).then_inc(sd["amax_all"], 1)

        def dve_scale(v, i, ch):
            c = 8 + 4 * i
            nc.vector.tensor_reduce(ax[:, c:c + 1], ax[:, 4 * i:4 * i + 4], AX, ALU.max).then_inc(sd["amax"], 1)
            v.wait_ge(sd["amax_all"], i + 1)
            ch.link(nc.vector.tensor_scalar(ax[:, c + 2:c + 3], ax[:, c + 1:c + 2], 1e-8, 1.0 / 32767.0,
                                            ALU.max, ALU.mult))
            nc.vector.reciprocal(ax[:, c + 3:c + 4], ax[:, c + 2:c + 3]).then_inc(sd["scale"], 1)

        def dve_l1ffn(v, base):
            s = sd
            v.wait_ge(s["win_psum"], 2)
            nc.vector.tensor_copy(win[:, FF:2 * FF], PS[:, 2:4, :].rearrange("p a n -> p (a n)")).then_inc(s["win_dve"], 1)
            ch = Chain(v, dve_step, base, 0, 3)
            with v.Fori(0, B) as b:
                ch = Chain(v, dve_step, base, b, 3)
                dve_norm(ch, N_D + b, lambda t: X[:, bass.ds(b * QT + t, 1), :].rearrange("p a c -> p (a c)"),
                         lambda t: xn[:, t, :]).then_inc(xf["xn_ready"], 1)
                v.wait_ge(xf["xn_ready"], b + (J_D + 1))
                ch.link(nc.vector.tensor_reduce(ax[:, bass.ds(b, 1)], xn, AXY, ALU.max, apply_absolute_value=True))
                v.wait_ge(xf["xT_psum"], XT(b + J_D))
                nc.vector.tensor_copy(XNT[:, 1, rows_of(b)], PS[:, 7, :]).then_inc(xf["xT_dve"], 1)
                ch.close()
            ch = Chain(v, dve_step, ch.after(B))
            dve_scale(v, 0, ch)
            base = ch.after()
            with v.Fori(0, B) as b:
                ch = Chain(v, dve_step, base, b, 2)
                v.wait_ge(s["xq_act"], b + 1)
                ch.link(nc.vector.tensor_scalar(xT, xT, ROUND, 32767.0, ALU.subtract, ALU.min))
                nc.vector.tensor_scalar(xT, xT, -32768.0, ax[:, 10:11], ALU.max, ALU.mult).then_inc(s["xq"], 1)
                v.wait_ge(s["h"], b * FC + FC)
                ch.link(nc.vector.tensor_reduce(ax[:, bass.ds(b + 4, 1)], Hall[:, :, rows_of(b)], AXY, ALU.max,
                                                apply_absolute_value=True))
                ch.close()
            ch = Chain(v, dve_step, ch.after(B))
            dve_scale(v, 1, ch)
            v.memset(scratch(1), 0.0).then_inc(s["used"], 1)
            base = ch.after()
            with v.Fori(0, B) as b:
                ch = Chain(v, dve_step, base, b, FC + 4)
                for f in range(FC + 1):
                    if f < FC:
                        v.wait_ge(s["hq_act"], b * FC + f + 1)
                        mark = ch.mark(nc.vector.tensor_scalar(hT[:, f, :], hT[:, f, :], ROUND, 32767.0,
                                                               ALU.subtract, ALU.min))
                    if f > 0:
                        ch.wait(mark if f == FC else mark - 1)
                        nc.vector.tensor_scalar(hT[:, f - 1, :], hT[:, f - 1, :], -32768.0, ax[:, 14:15],
                                                ALU.max, ALU.mult).then_inc(s["hq"], 1)
                dve_residual(v, s, b, b, 4, tg[:, 5:6], row["b1out"], ch)
                ch.close()
            v.memset(scratch(1), 0.0).then_inc(done["l1ffn"], 1)
            return ch.after(B)

        s2 = sems("l2a", "kv_psum kv q_psum q vb scores shifted probs pT_psum pT heads")
        w2 = W["w2a"]
        k2T = region("spare", 0, KC * B * TC).rearrange("p (c n) -> p c n", c=KC)
        v2b = region("spare", KC * B * TC, C + 1)
        v2 = region("Pr", 512, B * (C + 1)).rearrange("p (b e) -> p b e", b=B)
        p2, pT2 = region("Pr", 0, QT * TC), region("PT", 0, QT * TC)

        def pe_l2a(pe):
            s = s2
            pe.wait_ge(ld["w2a"], 16)
            pe.wait_ge(done["l1ffn"], 1)
            for c in range(KC):
                nc.tensor.matmul(PS[:, c, 0:B * TC], w2["wk"][:, c * P:(c + 1) * P], ctxT, start=True, stop=True
                                 ).then_inc(s["kv_psum"], 1)
            for b in range(B):
                nc.tensor.matmul(PS[:, 4 + b, 0:C], ctxdup[:, b].rearrange("p j n -> p (j n)"), w2["wv"],
                                 start=True, stop=True).then_inc(s["kv_psum"], 1)
            pe.wait_ge(s["kv"], KC + B)
            with pe.Fori(0, B) as b:
                pe_features(pe, b + J_E)
                for c in range(KC):
                    for k in range(KC):
                        ins = nc.tensor.matmul(PS[:, 6 + c, :], w2["wq"][:, k * C + c * P:k * C + (c + 1) * P],
                                               xT[:, k, :], start=k == 0, stop=k == KC - 1)
                    ins.then_inc(s["q_psum"], 1)
                pe.wait_ge(s["q"], b * KC + KC)
                for t in range(QT):
                    for c in range(KC):
                        ins = nc.tensor.matmul(PS[:, 0, t * TC:(t + 1) * TC], qT[:, c, t * P:(t + 1) * P],
                                               k2T[:, c, bass.ds(b * TC, TC)], start=c == 0, stop=c == KC - 1)
                ins.then_inc(s["scores"], 1)
                pe.wait_ge(s["probs"], b + 1)
                for i in range(2):
                    ins = nc.tensor.transpose(PS[:, 1, i * P:(i + 1) * P], p2[:, i * P:(i + 1) * P], ident)
                ins.then_inc(s["pT_psum"], 1)
                pe.wait_ge(s["pT"], b + 1)
                pe.wait_ge(s["vb"], b + 1)
                for t in range(QT):
                    half_rows = slice(TC * (t % 2), TC * (t % 2) + TC)
                    ins = nc.tensor.matmul(PS[:, 2 + t, 0:C + 1], pT2[half_rows, (t // 2) * P:(t // 2 + 1) * P],
                                           v2b[half_rows, :], start=True, stop=True)
                ins.then_inc(s["heads"], 1)

        def act_l2a(act):
            s = s2
            with act.Fori(0, B) as b:
                act.wait_ge(xf["xT_psum"], XT(b + J_E))
                plain_copy_act()
                act.wait_ge(s["shifted"], b + 1)
                nc.scalar.activation(p2, p2, ACT.Exp).then_inc(s["probs"], 1)
                act.wait_ge(s["pT_psum"], b + 1)
                nc.scalar.activation(pT2, PS[:, 1, 0:2 * P], ACT.Copy).then_inc(s["pT"], 1)

        def dve_l2a(v, base):
            s = s2
            for c in range(KC):
                v.wait_ge(s["kv_psum"], c + 1)
                nc.vector.tensor_scalar(k2T[:, c, :], PS[:, c, 0:B * TC], w2["bk"][:, c:c + 1], None, ALU.add
                                        ).then_inc(s["kv"], 1)
            for b in range(B):
                v.wait_ge(s["kv_psum"], KC + b + 1)
                nc.vector.tensor_tensor(v2[:, b, 0:C], PS[:, 4 + b, 0:C], row["b2v"], ALU.add)
                v.memset(v2[:, b, C:C + 1], 1.0).then_inc(s["kv"], 1)
            v.wait_ge(s["kv"], KC + B)
            with v.Fori(0, B) as b:
                ch = Chain(v, dve_step, base, b, 6)
                dve_norm(ch, N_E + b, lambda t: X[:, bass.ds(b * QT + t, 1), :].rearrange("p a c -> p (a c)"),
                         lambda t: xn[:, t, :]).then_inc(xf["xn_ready"], 1)
                nc.vector.tensor_copy(v2b, v2[:, bass.ds(b, 1), :].rearrange("p b e -> p (b e)")).then_inc(s["vb"], 1)
                v.wait_ge(xf["xT_psum"], XT(b + J_E))
                plain_copy_dve()
                for c in range(KC):
                    v.wait_ge(s["q_psum"], b * KC + c + 1)
                    nc.vector.tensor_scalar(qT[:, c, :], PS[:, 6 + c, :], w2["bq"][:, c:c + 1], None, ALU.add
                                            ).then_inc(s["q"], 1)
                v.wait_ge(s["scores"], b + 1)
                sc = PS[:, 0, 0:QT * TC].rearrange("p (t n) -> p t n", t=QT)
                ch.link(nc.vector.tensor_reduce(nmax[:, 0:QT], sc, AX, ALU.max))
                nc.vector.tensor_tensor(p2.rearrange("p (t n) -> p t n", t=QT), sc,
                                        nmax[:, 0:QT].unsqueeze(2).to_broadcast([P, QT, TC]), ALU.subtract
                                        ).then_inc(s["shifted"], 1)
                v.wait_ge(s["heads"], b + 1)
                ch.link(nc.vector.reciprocal(rrec[:, 0:QT].unsqueeze(2), PS[:, 2:2 + QT, C:C + 1]))
                ch.link(nc.vector.tensor_scalar(rsum[:, 0:QT], rrec[:, 0:QT], tg[:, 2:3], None, ALU.mult))
                for t in range(QT):
                    xt = X[:, bass.ds(b * QT + t, 1), :].rearrange("p a c -> p (a c)")
                    ins = nc.vector.scalar_tensor_tensor(out=xt, in0=PS[:, 2 + t, 0:C], scalar=rsum[:, t:t + 1],
                                                         in1=xt, op0=ALU.mult, op1=ALU.add)
                ch.link(ins)
                ch.close()
            v.memset(scratch(1), 0.0).then_inc(done["l2a"], 1)
            return ch.after(B)

        
        MOE_SEMS = " wa wb act_in dve_in hidden o_psum acc used extra"
        sr = sems("route", "xnt lg_psum")
        s2m = sems("l2moe", "masks rank_psum diff ediff slots scattered x0 x1 xT_psum xT copied y0_stored y1_stored "
                   "gathered00 gathered01 gathered10 gathered11 first wa wb act_in hidden o_psum")
        s3m = sems("l3moe", "sig" + MOE_SEMS)
        gtile = hT.rearrange("p a n -> p (a n)")
        etile = region("Pr", 0, 4096)
        temps = region("spare", 0, 4096)

        def pe_logits(pe, j0, w, e):
            with pe.Fori(0, B) as b:
                pe_features(pe, b + j0)
                for t in range(QT):
                    for k in range(KC):
                        ins = nc.tensor.matmul(PS[:, 5, t * e:(t + 1) * e], xT[:, k, t * P:(t + 1) * P],
                                               w[:, k * e:(k + 1) * e], start=k == 0, stop=k == KC - 1)
                ins.then_inc(sr["lg_psum"], 1)

        def act_logits(act, j0, n0):
            with act.Fori(0, B) as b:
                act.wait_ge(xf["xT_psum"], XT(b + j0))
                plain_copy_act()
                act.wait_ge(sr["xnt"], b + (n0 + 1))

        def act_logits2(act):
            with act.Fori(0, B) as b:
                act.wait_ge(xf["xT_psum"], XT(b + J_F))
                plain_copy_act()
                act.wait_ge(sr["lg_psum"], b + 1)

        def pool_logits2(pool):
            with pool.Fori(0, B) as b:
                pool_norm(pool, b + N_F)
                pool.wait_ge(xf["xn_ready"], b + (J_F + 1))
                nc.gpsimd.tensor_copy(XN[:, bass.ds(b * QT, QT), :], xn).then_inc(sr["xnt"], 1)

        def pool_logits(pool, base, j0):
            with pool.Fori(0, B) as b:
                pool_norm(pool, base + b)
                pool.wait_ge(xf["xT_act"], b + (j0 + 1))
                pool.wait_ge(xf["xT_dve"], b + (j0 + 1))
                nc.gpsimd.tensor_copy(XNT[:, :, rows_of(b)], xT).then_inc(sr["xnt"], 1)

        def dve_logits(v, base, nbase, j0, n0, e, lg):
            with v.Fori(0, B) as b:
                ch = Chain(v, dve_step, base, b, 3)
                dve_norm(ch, nbase + b, lambda t: X[:, bass.ds(b * QT + t, 1), :].rearrange("p a c -> p (a c)"),
                         lambda t: xn[:, t, :]).then_inc(xf["xn_ready"], 1)
                v.wait_ge(xf["xT_psum"], XT(b + j0))
                plain_copy_dve()
                v.wait_ge(sr["lg_psum"], b + (n0 + 1))
                ch.link(nc.vector.tensor_copy(lg[:, bass.ds(b * QT * e, QT * e)], PS[:, 5, 0:QT * e]))
                v.wait_ge(sr["xnt"], b + (n0 + 1))
                ch.close()
            return ch.after(B)

        def dve_rank(ch, val, rank, e, n=NT):
            v = nc.vector
            m = val.shape[1]
            g4 = gtile[:, 0:m * e * e].rearrange("p (t i j) -> p t i j", i=e, j=e)
            e4 = etile[:, 0:m * e * e].rearrange("p (t i j) -> p t i j", i=e, j=e)
            own = val.unsqueeze(3).to_broadcast([P, m, e, e])
            other = val.unsqueeze(2).to_broadcast([P, m, e, e])
            low = view("lower", "p (i j) -> p i j", i=E3)[:, 0:e, 0:e].unsqueeze(1).to_broadcast([P, m, e, e])
            v.tensor_tensor(g4, other, own, ALU.is_gt)
            ch.link(v.tensor_tensor(e4, other, own, ALU.is_equal))
            ch.link(v.tensor_tensor(e4, e4, low, ALU.mult))
            ch.link(v.tensor_tensor(g4, g4, e4, ALU.add))
            ch.link(v.tensor_reduce(rank, g4, AX, ALU.add))

        tcut = [0]

        def temp(n):
            tcut[0] += n
            assert tcut[0] <= 4096
            return temps[:, tcut[0] - n:tcut[0]]

        lg2 = region("PT", 0, NT * E2)
        lg3 = region("PT", 0, NT * E3)

        def dve_route2(v, base):
            s, ch = s2m, Chain(v, dve_step, base)
            V = nc.vector
            tcut[0] = 0
            val = temp(NT * E2).rearrange("p (t e) -> p t e", e=E2)
            ch.link(V.tensor_copy(val, lg2.rearrange("p (t e) -> p t e", e=E2)))
            rank = temp(NT * E2).rearrange("p (t e) -> p t e", e=E2)
            dve_rank(ch, val, rank, E2)
            masks = temp(2 * NT * E2)
            mk = masks.rearrange("p (k t e) -> p k t e", k=2, e=E2)
            for k in range(2):
                ins = V.tensor_scalar(mk[:, k], rank, float(k), None, ALU.is_equal)
            ins.then_inc(s["masks"], 1)
            v.wait_ge(s["masks"], 1)
            tmp = temp(2 * NT * E2)
            t4 = tmp.rearrange("p (k t e) -> p k t e", k=2, e=E2)
            top2 = temp(2 * NT).rearrange("p (k t) -> p k t", k=2)
            ch.link(V.tensor_tensor(t4, mk, val.unsqueeze(1).to_broadcast([P, 2, NT, E2]), ALU.mult))
            ch.link(V.tensor_reduce(top2, t4, AX, ALU.add))
            diff, ed, pk = temp(NT), temp(NT), temp(2 * NT).rearrange("p (k t) -> p k t", k=2)
            V.tensor_tensor(diff, top2[:, 1], top2[:, 0], ALU.subtract).then_inc(s["diff"], 1)
            v.wait_ge(s["ediff"], 1)
            den = temp(NT)
            ch.link(V.tensor_scalar(den, diff, 1.0, None, ALU.add))
            ch.link(V.reciprocal(pk[:, 0], den))
            ch.link(V.tensor_tensor(pk[:, 1], pk[:, 0], diff, ALU.mult))
            v.wait_ge(s["rank_psum"], 1)
            nseg = 2 * NT
            buf = [temp(nseg * E2), temp(nseg * E2)]
            tot = PS[:, 1, 0:nseg * E2]
            ch.link(V.tensor_copy(buf[0], tot))
            step, cur = 1, 0
            while step < nseg:
                a, z = buf[cur], buf[1 - cur]
                V.tensor_copy(z[:, 0:step * E2], a[:, 0:step * E2])
                ch.link(V.tensor_tensor(z[:, step * E2:], a[:, step * E2:], a[:, 0:(nseg - step) * E2], ALU.add))
                step, cur = 2 * step, 1 - cur
            pos = buf[cur]
            ch.link(V.tensor_tensor(pos, pos, tot, ALU.subtract))
            ch.link(V.tensor_tensor(pos, pos, PS[:, 0, 0:nseg * E2], ALU.add))
            m4 = masks.rearrange("p (s e) -> p s e", e=E2)
            first = temp(E2)
            for e in range(E2):
                V.memset(first[:, e:e + 1], float(e * CAP - 1))
            spare = temp(nseg)
            ch.link(V.tensor_copy(spare, spare_u[:, :]))
            ch.link(V.tensor_tensor(pos, pos, masks, ALU.mult))
            place, slot, picked = temp(nseg), temp(nseg), temp(nseg * E2)
            ch.link(V.tensor_reduce(place, pos.rearrange("p (s e) -> p s e", e=E2), AX, ALU.add))
            picked3 = picked.rearrange("p (s e) -> p s e", e=E2)
            ch.link(V.tensor_tensor(picked3, m4, first.unsqueeze(1).to_broadcast([P, nseg, E2]), ALU.mult))
            ch.link(V.tensor_reduce(slot, picked3, AX, ALU.add))
            ch.link(V.tensor_tensor(slot, slot, place, ALU.add))
            ch.link(V.tensor_scalar(place, place, float(CAP), None, ALU.is_le))
            ch.link(V.tensor_tensor(slot, slot, spare, ALU.subtract))
            ch.link(V.tensor_tensor(slot, slot, place, ALU.mult))
            ch.link(V.tensor_tensor(slot, slot, spare, ALU.add))
            V.tensor_copy(slot_of2[:, :], slot).then_inc(s["slots"], 1)
            ch.link(V.tensor_scalar(spare, slot, float(S2), None, ALU.min))
            V.tensor_copy(row_of2[:, :], spare).then_inc(s["slots"], 1)
            w2c = wcomb[:, 0:nseg]
            ch.link(V.tensor_tensor(w2c, pk.rearrange("p k t -> p (k t)"), place, ALU.mult))
            ch.link(V.tensor_scalar(w2c, w2c, tg[:, 6:7], None, ALU.mult))
            for name, n in (("copied", 1), ("o_psum", 1)):
                V.memset(scratch(1), 0.0).then_inc(s[name], n)
            V.memset(scratch(1), 0.0).then_inc(done["route2"], 1)
            return ch.after()

        def dve_route3(v, base):
            s, ch = s3m, Chain(v, dve_step, base)
            V = nc.vector
            tcut[0] = 0
            ng, eg = 4, E3 // 4
            score = temp(NT * E3).rearrange("p (t e) -> p t e", e=E3)
            V.memset(scratch(1), 0.0).then_inc(s["extra"], 1)
            v.wait_ge(s["sig"], 1)
            ch.link(V.tensor_copy(score, lg3.rearrange("p (t e) -> p t e", e=E3)))
            sfc = temp(NT * E3).rearrange("p (t e) -> p t e", e=E3)
            ch.link(V.tensor_tensor(sfc, score, gbias.unsqueeze(1).to_broadcast([P, NT, E3]), ALU.add))
            grp = sfc.rearrange("p t (g e) -> p (t g) e", e=eg)
            pairs = [(i, j) for i in range(eg) for j in range(i + 1, eg)]
            sums = temp(NT * ng * len(pairs)).rearrange("p (n q) -> p n q", q=len(pairs))
            for q, (i, j) in enumerate(pairs):
                ins = V.tensor_tensor(sums[:, :, q], grp[:, :, i], grp[:, :, j], ALU.add)
            ch.link(ins)
            gsc = temp(NT * ng)
            ch.link(V.tensor_reduce(gsc, sums, AX, ALU.max))
            grank = temp(NT * ng)
            dve_rank(ch, gsc.rearrange("p (t g) -> p t g", g=ng), grank.rearrange("p (t g) -> p t g", g=ng), ng)
            ch.link(V.tensor_scalar(grank, grank, float(2), None, ALU.is_lt))
            ch.link(V.tensor_tensor(grp, grp, grank.unsqueeze(2).to_broadcast([P, NT * ng, eg]), ALU.mult))
            rank = temp(NT * E3).rearrange("p (t e) -> p t e", e=E3)
            dve_rank(ch, sfc, rank, E3)
            ch.link(V.tensor_scalar(rank, rank, 4.0, None, ALU.is_lt))
            ch.link(V.tensor_tensor(rank, rank, score, ALU.mult))
            tot = temp(NT)
            ch.link(V.tensor_reduce(tot, rank, AX, ALU.add))
            ch.link(V.tensor_scalar(tot, tot, 1e-20, None, ALU.add))
            ch.link(V.reciprocal(tot, tot))
            ch.link(V.tensor_scalar(tot, tot, tg[:, 7:8], None, ALU.mult))
            w3c = wcomb.rearrange("p (t e) -> p t e", e=NX3)
            V.tensor_copy(w3c[:, :, E3:NX3], tg[:, 7:8].unsqueeze(1).to_broadcast([P, NT, 2]))
            ch.link(V.tensor_tensor(w3c[:, :, 0:E3], rank, tot.unsqueeze(2).to_broadcast([P, NT, E3]), ALU.mult))
            V.memset(scratch(1), 0.0).then_inc(s["acc"], 4)
            V.memset(scratch(1), 0.0).then_inc(s["used"], 1)
            V.memset(scratch(1), 0.0).then_inc(done["route3"], 1)
            return ch.after()

        ebuf2 = [region("spare", 0, W2X), region("Pr", 0, W2X)]
        ebuf3 = [region("spare", 0, W3X), region("Pr", 0, W3X)]
        sgate = [region("Pr", W3X + c * T, T) for c in range(3)]
        ARRIVED = ("wa", "wb")

        def sp_experts(sp, s, src, bufs, npairs):
            def load(e_static, e, i):
                sp.dma_start(bufs[i], src[e, :, :] if e_static else
                             src[bass.ds(e, 1), :, :].rearrange("e p n -> p (e n)")
                             ).then_inc((s["wa"], s["wb"])[i], 16)
            for i in range(2):
                load(True, i, i)
            with sp.Fori(1, npairs) as ep:
                for i in range(2):
                    sp.wait_ge(s["used"], ep * 8 + (4 * i - 3))
                    load(False, ep * 2 + i, i)

        def pe_down(pe, s, it, w2off, buf, chunks_of):
            for t in range(QT):
                for c, n in enumerate(chunks_of):
                    if t == 0:
                        pe.wait_ge(s["hidden"], it * len(chunks_of) + c + 1)
                    if c == 0:
                        pe.wait_ge(s["acc"], it * QT + t + 1)
                    ins = nc.tensor.matmul(PS[:, 4 + t, 0:C], hT[0:n, c, t * P:(t + 1) * P],
                                           buf[0:n, w2off + c * C:w2off + (c + 1) * C],
                                           start=c == 0, stop=c == len(chunks_of) - 1)
                ins.then_inc(s["o_psum"], 1)
            nc.tensor.matmul(PS[0:1, 3, 0:1], ident[:, 0:1], ident[:, 0:1], start=True, stop=True
                             ).then_inc(s["used"], 1)

        def dve_accumulate(v, s, it, b, e, ne):
            for t in range(QT):
                v.wait_ge(s["o_psum"], it * QT + t + 1)
                v.wait_ge(s["acc"], it * QT + t + 1)
                xt = X[:, bass.ds(b * QT + t, 1), :].rearrange("p a c -> p (a c)")
                nc.vector.scalar_tensor_tensor(out=xt, in0=PS[:, 4 + t, 0:C],
                                               scalar=wcomb[:, bass.ds((b * QT + t) * ne + e, 1)],
                                               in1=xt, op0=ALU.mult, op1=ALU.add).then_inc(s["acc"], 1)

        GC = GT2[0] * C
        xs = [view("V", "p (t c) -> p t c", g * GC, GT2[g] * C, c=C) for g in range(2)]
        xsT = [view("V", "p (k n) -> p k n", 2 * GC + g * GC, KC * GT2[g] * P, k=KC) for g in range(2)]
        ys = [view("kv", "p (t c) -> p t c", KV3_OFF + g * GC, GT2[g] * C, c=C) for g in range(2)]
        yk = [view("V", "p (t c) -> p t c", 0, NT * C, c=C),
              view("kv", "p (t c) -> p t c", KV3_OFF + 2 * GC, NT * C, c=C)]

        def slot_rows(dram, e, g):
            first, n = e * CAP + g * GT2[0] * P, GT2[g] * P
            return dram[bass.ds(first, n), :].rearrange("(t p) c -> p t c", p=P)

        def sp_moe2(sp):
            s = s2m
            for i in range(2):
                sp.dma_start(ebuf2[i], e2_in[i, :, :]).then_inc((s["wa"], s["wb"])[i], 16)
            sp.wait_ge(s["scattered"], 2 * NT * 16)
            for g in range(2):
                sp.dma_start(xs[g], slot_rows(slots2, 0, g)).then_inc(s[f"x{g}"], 16)

            def rows(e):
                for g in range(2):
                    sp.wait_ge(s["xT_psum"], e * 2 + (g - 1))
                    sp.dma_start(xs[g], slot_rows(slots2, e, g)).then_inc(s[f"x{g}"], 16)
            with sp.Fori(0, E2 // 2 - 1) as ep:
                for i in range(2):
                    rows(ep * 2 + (i + 1))
                    sp.wait_ge(s["o_psum"], ep * 10 + (5 * i + 6))
                    sp.dma_start(ebuf2[i], e2_in[bass.ds(ep * 2 + (i + 2), 1), :, :].rearrange("e p n -> p (e n)")
                                 ).then_inc((s["wa"], s["wb"])[i], 16)
            rows(E2 - 1)

        def pe_moe2(pe):
            s = s2m

            def transposes(e, g, first=False):
                pe.wait_ge(s[f"x{g}"], e * 16 + 16)
                if not first:
                    pe.wait_ge(s["xT"], e * 2 + g)
                for k in range(KC):
                    for t in range(GT2[g]):
                        ins = nc.tensor.transpose(PS[:, (3, 7)[k], t * P:(t + 1) * P],
                                                  xs[g][:, t, k * P:(k + 1) * P], ident)
                ins.then_inc(s["xT_psum"], 1)

            def expert(e, i, last=False):
                for g in range(2):
                    n, N = e * 2 + g, GT2[g] * P
                    if g == 0:
                        pe.wait_ge((s["wa"], s["wb"])[i], (e - i) * 8 + 16)
                    pe.wait_ge(s["xT"], n + 1)
                    for f in range(FC):
                        if f >= 3:
                            pe.wait_ge(s["hidden"], n * FC + f - 2)
                        for k in range(KC):
                            ins = nc.tensor.matmul(PS[:, f % 3, 0:N], ebuf2[i][:, k * FF + f * P:k * FF + (f + 1) * P],
                                                   xsT[g][:, k, :], start=k == 0, stop=k == KC - 1)
                        ins.then_inc(s["act_in"], 1)
                    if g == 0:
                        transposes(e, 1)
                    elif not last:
                        transposes(e + 1, 0)
                    for t in range(GT2[g]):
                        for c in range(FC):
                            if t == 0:
                                pe.wait_ge(s["hidden"], n * FC + c + 1)
                            if t == 0 and c == 0:
                                pe.wait_ge(s["copied"], e * 5 + (g * 3 + 1))
                            ins = nc.tensor.matmul(PS[:, 4 + t, 0:C], hT[:, c, t * P:(t + 1) * P],
                                                   ebuf2[i][:, 2 * FF + c * C:2 * FF + (c + 1) * C],
                                                   start=c == 0, stop=c == FC - 1)
                        ins.then_inc(s["o_psum"], 1)
            transposes(0, 0, first=True)
            with pe.Fori(0, E2 // 2 - 1) as ep:
                for i in range(2):
                    expert(ep * 2 + i, i)
            expert(E2 - 2, 0)
            expert(E2 - 1, 1, last=True)

        def act_moe2(act):
            s = s2m
            act.wait_ge(done["route2"], 1)
            with act.Fori(0, E2) as e:
                for g in range(2):
                    act.wait_ge(s["o_psum"], e * 5 + (3 * g + 1))
                    for f in range(FC):
                        act.wait_ge(s["act_in"], e * 2 * FC + (g * FC + f + 1))
                        nc.scalar.activation(hT[:, f, 0:GT2[g] * P], PS[:, f % 3, 0:GT2[g] * P], ACT.Gelu
                                             ).then_inc(s["hidden"], 1)

        def dve_moe2(v):
            s = s2m

            def rows_copy(e, g):
                v.wait_ge(s["xT_psum"], e * 2 + (g + 1))
                for k in range(KC):
                    ins = nc.vector.tensor_copy(xsT[g][:, k, :], PS[:, (3, 7)[k], 0:GT2[g] * P])
                ins.then_inc(s["xT"], 1)

            def outputs(e, g, first):
                if not first:
                    v.wait_ge(s[f"y{g}_stored"], e * 16)
                for t in range(GT2[g]):
                    v.wait_ge(s["o_psum"], e * 5 + (3 * g + t + 2))
                    nc.vector.tensor_copy(ys[g][:, t, :], PS[:, 4 + t, 0:C]).then_inc(s["copied"], 1)

            def expert(e, first=False, last=False):
                rows_copy(e, 1)
                outputs(e, 0, first)
                if not last:
                    rows_copy(e + 1, 0)
                outputs(e, 1, first)
            rows_copy(0, 0)
            expert(0, first=True)
            with v.Fori(1, E2 - 1) as e:
                expert(e)
            expert(E2 - 1, last=True)
            for k in range(2):
                for q in range(2):
                    v.wait_ge(s[f"gathered{k}{q}"], NT // 2 * 16)
                    for t in range(q * NT // 2, (q + 1) * NT // 2):
                        if k == 1 and t % (NT // 2) == 0:
                            v.wait_ge(s["first"], q + 1)
                        ins = nc.vector.scalar_tensor_tensor(out=X[:, t, :], in0=yk[k][:, t, :],
                                                             scalar=wcomb[:, k * NT + t:k * NT + t + 1],
                                                             in1=X[:, t, :], op0=ALU.mult, op1=ALU.add)
                    ins.then_inc(s["first"], 1)
            v.wait_ge(s["first"], 4)
            v.memset(scratch(1), 0.0).then_inc(done["l2moe"], 1)

        def pool_scatter2(pool):
            s = s2m
            pool.wait_ge(ld["zeroed"], 32)
            pool.wait_ge(sr["xnt"], B)
            pool.wait_ge(s["slots"], 1)
            for k in range(2):
                for t in range(NT):
                    at_ = bass.IndirectOffsetOnAxis(ap=slot_of2[:, k * NT + t:k * NT + t + 1], axis=0)
                    nc.gpsimd.indirect_dma_start(out=slots2, out_offset=at_, in_=XN[:, t, :], in_offset=None
                                                 ).then_inc(s["scattered"], 16)

        def pool_moe2(pool):
            s = s2m
            with pool.Fori(0, E2) as e:
                for g in range(2):
                    pool.wait_ge(s["copied"], e * 5 + (1 + (3, 5)[g]))
                    pool.dma_start(slot_rows(yslots2, e, g), ys[g]).then_inc(s[f"y{g}_stored"], 16)
            for g in range(2):
                pool.wait_ge(s[f"y{g}_stored"], E2 * 16)
            pool.wait_ge(s["slots"], 2)
            for k in range(2):
                for t in range(NT):
                    at_ = bass.IndirectOffsetOnAxis(ap=row_of2[:, k * NT + t:k * NT + t + 1], axis=0)
                    nc.gpsimd.indirect_dma_start(out=yk[k][:, t, :], out_offset=None, in_=yslots2, in_offset=at_
                                                 ).then_inc(s[f"gathered{k}{t // (NT // 2)}"], 16)

        def pe_moe3(pe):
            s = s3m
            with pe.Fori(0, NX3 // 2) as ep:
                for i in range(2):
                    with pe.Fori(0, B) as b:
                        pe.wait_ge((s["wa"], s["wb"])[i], ep * 16 + 16)
                        it = ep * 8 + (i * 4) + b
                        for j in range(6):
                            c, up = j // 2, j % 2
                            n = IC3[c]
                            if j == 3:
                                pe.wait_ge(s["extra"], it * 3 + 2)
                            if j >= 4:
                                pe.wait_ge(s["hidden"], it * 3 + j - 3)
                            for k in range(KC):
                                off = up * 2 * I3 + k * I3 + c * P
                                ins = nc.tensor.matmul(PS[0:n, j % 3, :], ebuf3[i][:, off:off + n],
                                                       XNT[:, k, rows_of(b)], start=k == 0, stop=k == KC - 1)
                            ins.then_inc((s["act_in"], s["dve_in"])[up], 1)
                        pe_down(pe, s, it, 4 * I3, ebuf3[i], IC3)

        def act_moe3(act):
            s = s3m
            act.wait_ge(done["route3"], 1)
            with act.Fori(0, NX3 * B) as it:
                for c, n in enumerate(IC3):
                    act.wait_ge(s["act_in"], it * 3 + c + 1)
                    nc.scalar.activation(sgate[c][0:n, :], PS[0:n, (2 * c) % 3, :], ACT.Silu).then_inc(s["extra"], 1)

        def dve_moe3(v):
            s = s3m
            with v.Fori(0, NX3) as e:
                with v.Fori(0, B) as b:
                    it = e * B + b
                    v.wait_ge(s["used"], it + 1)
                    for c, n in enumerate(IC3):
                        v.wait_ge(s["dve_in"], it * 3 + c + 1)
                        v.wait_ge(s["extra"], it * 3 + c + 2)
                        nc.vector.tensor_tensor(hT[0:n, c, :], sgate[c][0:n, :], PS[0:n, (2 * c + 1) % 3, :], ALU.mult
                                                ).then_inc(s["hidden"], 1)
                    dve_accumulate(v, s, it, b, e, NX3)
            v.wait_ge(s["acc"], 4 + NX3 * NT)
            v.memset(scratch(1), 0.0).then_inc(done["all"], 1)

        s3k = sems("kv3", "tok xT_psum xT kv_psum kv_ready")
        ca, cd = scaled_copies(w3["xg"], w3["xb"], w3["yg"], w3["yb"])
        c3s = dict(engines=evac_engines("d"), wq=w3["wq"], wk=w3["wk"], wv=w3["wv"], xq=xT, xkv=xT2, d=D3, causal=False,
                  V=V3, y=y3, bq=None, bk=None, bv=None, scale=D3 ** -0.5, copy_x_act=ca, copy_x_dve=cd)
        c3o = dict(nch=4, y=y3, wo=w3["li1"])
        ca, cd = scaled_copies(w3["g3"], w3["b3"])
        c3f = dict(lora=False, w1=w3["li2"], w2=w3["li3"], b1=w3["bh"], copy_x_act=ca, copy_x_dve=cd)
        ca, cd = scaled_copies(w3b["xg"], w3b["xb"])
        c3c = dict(kv=kv3, norm=True, wq=w3b["wq"], bq=None, scale=D3 ** -0.5, y=y3, add=False,
                  copy_x_act=ca, copy_x_dve=cd)
        c3p = dict(nch=4, y=y3, wo=w3b["li1"])
        ca, cd = scaled_copies(w3b["g3"], w3b["b3"])
        c3g = dict(lora=False, w1=w3b["li2"], w2=w3b["li3"], b1=w3b["bh"], copy_x_act=ca, copy_x_dve=cd)
        ctok = region("ctx", 0, B * CC).rearrange("p (b c) -> p b c", b=B)
        ctx3 = xT.rearrange("p k n -> p (k n)")[:, 0:B * 2 * TC]

        def pe_context3(pe):
            pe.wait_ge(ld["w3b"], 16)
            pe.wait_ge(s3k["tok"], 1)
            for b in range(B):
                ins = nc.tensor.transpose(PS[:, 0, b * P:(b + 1) * P], xn[:, b, 0:CC], ident)
            ins.then_inc(s3k["xT_psum"], 1)
            pe_context(pe, s3k, kv3, w3b["wk"], w3b["wv"], ctx3.rearrange("p (b j n) -> p b j n", b=B, j=2)[:, :, 0, :],
                       lambda b: ctx3[:, b * P:(b + 1) * P], lambda: pe.wait_ge(s3k["xT"], 1))
            pe.wait_ge(s3k["kv_ready"], kv_count(kv3))

        def dve_context3(v, base):
            ch = Chain(v, dve_step, base)
            v.wait_ge(ld["ctx3"], 16)
            dve_norm(ch, N_CTX, lambda t: ctok[:, t, :], lambda t: xn[:, t, 0:CC]).then_inc(s3k["tok"], 1)
            v.wait_ge(s3k["xT_psum"], 1)
            v.wait_ge(ld["w3b"], 16)
            nc.vector.tensor_scalar(ctx3, PS[:, 0, :], w3b["yg"][:, 0:1], w3b["yb"][:, 0:1], ALU.mult, ALU.add
                                    ).then_inc(s3k["xT"], 1)
            dve_context(v, s3k, kv3, region("in32"), None, None, None, ch)
            return ch.after()

        def dve_affine(ch, g, bb):
            for x, r, op in ((xn, g, ALU.mult), (x1, bb, ALU.add)):
                ch.link(nc.vector.tensor_tensor(x1, x, r.unsqueeze(1).to_broadcast([P, QT, C]), op))

        def dve_add(v, s, it, bank0, src, bias, ch):
            for i in range(2):
                v.wait_ge(s["out_psum"], it * 2 + i + 1)
                prod = PS[:, bank0 + i, :].rearrange("p (t c) -> p t c", t=2)
                tiles = slice(2 * i, 2 * i + 2)
                ch.link(nc.vector.tensor_tensor(xn[:, tiles, :], prod, bias.unsqueeze(1).to_broadcast([P, 2, C]),
                                                ALU.add))
                ch.link(nc.vector.tensor_tensor(xo[:, tiles, :], xn[:, tiles, :], src[:, tiles, :], ALU.add))

        def dve_l3a(v, base):
            with v.Fori(0, B) as b:
                ch = Chain(v, dve_step, base, b, DVE3_STEPS)
                nb, j = b * 6 + N_G, b * 4 + J_G
                of = lambda z: (lambda t: z[:, t, :])
                ch.link(dve_norm(ch, nb, lambda t: X[:, bass.ds(b * QT + t, 1), :].rearrange("p a c -> p (a c)"),
                                 of(xn)))
                dve_affine(ch, row["ln1g"], row["ln1b"])
                dve_norm(ch, nb + 1, of(x1), of(xn)).then_inc(xf["xn_ready"], 1)
                dve_self(v, ss, b + B, j, c3s, ch)
                dve_yT(v, so_, b * 2 + 2 * B, c3o)
                dve_add(v, so_, b * 2 + 2 * B, 0, x1, row["a1li1b"], ch)
                dve_norm(ch, nb + 2, of(xo), of(xn)).then_inc(xf["xn_ready"], 1)
                dve_ffn(v, sf, b * 2 + B, j + 1, c3f)
                dve_add(v, sf, b * 2 + B, 4, xo, row["a1li3b"], ch)
                ch.link(nc.vector.tensor_tensor(xo, xo, x1, ALU.add))
                ch.link(dve_norm(ch, nb + 3, of(xo), of(xn)))
                dve_affine(ch, row["ln2g"], row["ln2b"])
                dve_norm(ch, nb + 4, of(x1), of(xn)).then_inc(xf["xn_ready"], 1)
                dve_cross(v, sc_, b + 2 * B, j + 2, b, c3c, ch)
                dve_yT(v, so_, b * 2 + (2 * B + 1), c3p)
                dve_add(v, so_, b * 2 + (2 * B + 1), 0, x1, row["a2li1b"], ch)
                dve_norm(ch, nb + 5, of(xo), of(xn)).then_inc(xf["xn_ready"], 1)
                dve_ffn(v, sf, b * 2 + (B + 1), j + 3, c3g)
                dve_add(v, sf, b * 2 + (B + 1), 4, xo, row["a2li3b"], ch)
                ch.link(nc.vector.tensor_tensor(xo, xo, x1, ALU.add))
                xr = X[:, bass.ds(b * QT, QT), :]
                ch.link(nc.vector.scalar_tensor_tensor(out=xr, in0=xo, scalar=tg[:, 3:4], in1=xr,
                                                       op0=ALU.mult, op1=ALU.add))
                ch.close()
            v.memset(scratch(1), 0.0).then_inc(done["l3a"], 1)
            return ch.after(B)

        DVE1_STEPS, DVE3_STEPS = 40, 49
        block = ctx.enter_context(nc.Block())

        @block.sync
        def _(sp):
            sp.dma_start(X, x_in.rearrange("(t p) c -> p t c", p=P)).then_inc(ld["x"], 16)
            sp.dma_start(region("ctx"), ctxT_in).then_inc(ld["ctx"], 16)
            sp.dma_start(region("rows"), rows_in.rearrange("a n -> (a n)").partition_broadcast(P)).then_inc(ld["small"], 16)
            sp.dma_start(region("gates"), gates_in.rearrange("a n -> (a n)").partition_broadcast(P)).then_inc(ld["small"], 16)
            sp.dma_start(arena[0:RANK, LAY["lora"][0]:LAY["lora"][0] + FF + C], lora_in).then_inc(ld["small"], 16)
            n = width("w0a")
            sp.dma_start(region("wa", 0, n), packs_in["w0a"]).then_inc(ld["w0a"], 16)
            sp.dma_start(region("wa", n + width("w0f"), width("w1a")), packs_in["w1a"]).then_inc(ld["w1a"], 16)
            sp.dma_start(region("wa", n, width("w0f")), packs_in["w0f"]).then_inc(ld["w0f"], 16)
            sp.dma_start(region("wf", 0, width("w1f")), packs_in["w1f"]).then_inc(ld["w1f"], 16)
            sp.wait_ge(cst["ready"], 1)
            sp.dma_start(slots2[0:S2, :].rearrange("(t p) c -> p t c", p=P),
                         zeros[:, :].unsqueeze(1).to_broadcast([P, S2 // P, C])).then_inc(ld["zeroed"], 16)
            sp.dma_start(yslots2[S2:S2 + P, :], zeros[:, :]).then_inc(ld["zeroed"], 16)
            if stop >= 5:
                sp.wait_ge(done["l1ffn"], 1)
                sp.dma_start(region("kv", 0, width("w2a")), packs_in["w2a"]).then_inc(ld["w2a"], 16)
            if stop >= 7:
                off = W3_OFF
                for name in ("w3a", "w3b", "w3g"):
                    sp.dma_start(region("kv", off, width(name)), packs_in[name]).then_inc({"w3a": ld["w3a"], "w3b": ld["w3b"], "w3g": ld["w3g"]}[name], 16)
                    off += width(name)
            if stop >= 6:
                sp.wait_ge(done["route2"], 1)
                sp_moe2(sp)
            if stop >= 7:
                sp.dma_start(ctok, ctx_in.rearrange("p (b c) -> p b c", b=B)).then_inc(ld["ctx3"], 16)
            if stop >= 8:
                sp.wait_ge(done["route3"], 1)
                sp_experts(sp, s3m, e3_in, ebuf3, NX3 // 2)
            sp.wait_ge(done["all"], 1)
            sp.dma_start(out.rearrange("(t p) c -> p t c", p=P), X).then_inc(ld["stored"], 16)
            sp.wait_ge(ld["stored"], 16)

        @block.gpsimd
        def _(pool):
            g = nc.gpsimd
            n = [0]

            def link(ins):
                n[0] += 1
                ins.then_inc(cst["step"], 1)
                pool.wait_ge(cst["step"], n[0])

            def select(out, pattern, op, fill, base, mult):
                return g.affine_select(out=out, in_=out, compare_op=op, fill=fill, base=base, pattern=pattern,
                                       channel_multiplier=mult)
            g.memset(ident, 0.0)
            g.memset(region("causal"), 0.0)
            g.memset(mhalf, -0.5)
            g.memset(zeros[:, :], 0.0)
            g.memset(cround, ROUND)
            g.iota(spare_u[:, :], pattern=[[P, 2 * NT]], base=S2, channel_multiplier=1)
            for name in ("ones", "later", "upto", "in16", "in32", "in64", "lower"):
                last = g.memset(region(name), 1.0)
            link(last)
            link(select(ident, [[-1, P]], ALU.not_equal, 1.0, 0, 1))
            link(select(region("causal"), [[-1, P]], ALU.is_ge, NEG, 0, 1))
            link(select(region("later"), [[-1, P]], ALU.is_gt, 0.0, 0, 1))
            link(select(region("upto"), [[1, P]], ALU.is_ge, 0.0, 0, -1))
            for name, w in (("in16", 16), ("in32", 32), ("in64", 64)):
                link(select(region(name), [[-w, P // w]], ALU.is_ge, 0.0, 0, 1))
                link(select(region(name), [[w, P // w]], ALU.is_ge, 0.0, w - 1, -1))
            select(view("lower", "p (i j) -> p i j", i=E3), [[1, E3], [-1, E3]], ALU.is_gt, 0.0, 0, 0
                   ).then_inc(cst["ready"], 1)
            pool.wait_ge(sq["amax"], 1)
            link(g.partition_all_reduce(amax[:, 2:4], amax[:, 0:2], P, RMAX))
            g.tensor_copy(amax[:, 6:8], amax[:, 2:4]).then_inc(sq["all"], 1)
            pool.wait_ge(sq["w0scale"], 1)
            pool_norm(pool, N_L01)
            for i, w in enumerate((w0f["wfc"], w0f["wproj"])):
                sc = amax[:, 4 + i:5 + i]
                link(g.tensor_scalar(w, w, amax[:, 8 + i:9 + i], ROUND, ALU.mult, ALU.add))
                link(g.tensor_scalar(w, w, ROUND, 127.0, ALU.subtract, ALU.min))
                g.tensor_scalar(w, w, -128.0, sc, ALU.max, ALU.mult).then_inc(sq["w0"], 1)
            pool.wait_ge(sq["w1scale"], 1)
            for i, w in enumerate((w1f["winT"], w1f["wout"])):
                w = w.rearrange("p (f c) -> p f c", f=FC)
                inv, sc = (aw[:, o + 8 * i:o + 8 * i + 8].unsqueeze(2).to_broadcast([P, FC, C]) for o in (16, 32))
                link(g.tensor_tensor(w, w, sc, ALU.mult))
                link(g.tensor_scalar(w, w, ROUND, ROUND, ALU.add, ALU.subtract))
                link(g.tensor_scalar(w, w, 127.0, -128.0, ALU.min, ALU.max))
                g.tensor_tensor(w, w, inv, ALU.mult).then_inc(sq["w1"], 1)
            with pool.Fori(1, 3 * B) as i:
                pool_norm(pool, i)
            if stop >= 4:
                pool_l1ffn(pool)
            if stop >= 5:
                with pool.Fori(0, B) as b:
                    pool_norm(pool, N_E + b)
            if stop >= 6:
                pool_logits2(pool)
                pool_scatter2(pool)
                pool_moe2(pool)
            if stop >= 7:
                with pool.Fori(N_CTX, N_H) as i:
                    pool_norm(pool, i)
            if stop >= 8:
                pool_logits(pool, N_H, J_H)

        @block.tensor
        def _(pe):
            pe.wait_ge(ld["ctx"], 16)
            pe.wait_ge(cst["ready"], 1)

            def w0_here():
                pe.wait_ge(ld["w0a"], 16)
            pe_context(pe, s0k, kv0, w0["wck"], w0["wcv"], ctxT, lambda b: ctxdup[:, b].rearrange("p j n -> p (j n)"), w0_here)

            def w1_here():
                pe.wait_ge(ld["w1a"], 16)
                pe.wait_ge(s0k["kv_ready"], kv_count(kv0))
            pe_context(pe, s1k, kv1, w1["wk"], w1["wv"], ctxT, lambda b: ctxdup[:, b].rearrange("p j n -> p (j n)"), w1_here)
            pe.wait_ge(s1k["kv_ready"], kv_count(kv1))
            pe.wait_ge(ld["small"], 48)
            with pe.Fori(0, B) as b:
                pe_self(pe, ss, b, b * 3, c0s)
                pe.wait_ge(ss["y"], b * G + G)
                pe_cross(pe, sc_, b * 2, None, b, c0c)
                pe_out(pe, so_, b * 2, c0o, lambda: pe.wait_ge(sc_["y"], b * 2 * QT + QT))
                pe.wait_ge(sq["w0"], 2)
                pe_ffn(pe, sf, b, b * 3 + 1, c0f)
                pe_cross(pe, sc_, b * 2 + 1, b * 3 + 2, b, c1c)
                pe_out(pe, so_, b * 2 + 1, c1o, lambda: pe.wait_ge(sc_["y"], b * 2 * QT + 2 * QT))
            if stop >= 4:
                pe_l1ffn(pe)
            if stop >= 5:
                pe_l2a(pe)
            if stop >= 6:
                pe_logits(pe, J_F, w2["wg"], E2)
                pe.wait_ge(s2m["masks"], 1)
                masks = temps[:, 2 * NT * E2:4 * NT * E2]
                nc.tensor.matmul(PS[:, 0, 0:2 * NT * E2], region("upto"), masks, start=True, stop=True)
                nc.tensor.matmul(PS[:, 1, 0:2 * NT * E2], ones, masks, start=True, stop=True
                                 ).then_inc(s2m["rank_psum"], 1)
                pe.wait_ge(done["route2"], 1)
                pe_moe2(pe)
            if stop >= 7:
                pe.wait_ge(done["l2moe"], 1)
                pe_context3(pe)
                pe.wait_ge(ld["w3a"], 16)
                with pe.Fori(0, B) as b:
                    j = b * 4 + J_G
                    pe_self(pe, ss, b + B, j, c3s)
                    pe_out(pe, so_, b * 2 + 2 * B, c3o, lambda: pe.wait_ge(ss["y"], b * G + (B * G + G)))
                    pe_ffn(pe, sf, b * 2 + B, j + 1, c3f)
                    pe_cross(pe, sc_, b + 2 * B, j + 2, b, c3c)
                    pe_out(pe, so_, b * 2 + (2 * B + 1), c3p, lambda: pe.wait_ge(sc_["y"], b * QT + (2 * B * QT + QT)))
                    pe_ffn(pe, sf, b * 2 + (B + 1), j + 3, c3g)
            if stop >= 8:
                pe.wait_ge(ld["w3g"], 16)
                pe_logits(pe, J_H, W["w3g"]["gw"], E3)
                pe.wait_ge(done["route3"], 1)
                pe_moe3(pe)

        @block.scalar
        def _(act):
            act.wait_ge(ld["small"], 48)
            nc.scalar.activation(tg, region("gates"), ACT.Tanh).then_inc(gate_ready, 1)
            act.wait_ge(ld["w0a"], 16)
            act.wait_ge(ld["w0f"], 16)
            with act.Fori(0, B) as b:
                act_self(act, ss, b, b * 3, c0s)
                act_cross(act, sc_, b * 2, None, b, c0c)
                act_out(act, so_, b * 2, c0o)
                act_ffn(act, sf, b, b * 3 + 1, c0f)
                act_cross(act, sc_, b * 2 + 1, b * 3 + 2, b, c1c)
                act_out(act, so_, b * 2 + 1, c1o)
            if stop >= 4:
                act_l1ffn(act)
            if stop >= 5:
                act_l2a(act)
            if stop >= 6:
                act_logits2(act)
                act.wait_ge(s2m["diff"], 1)
                diff = temps[:, 6 * NT * E2 + 2 * NT:6 * NT * E2 + 3 * NT]
                nc.scalar.activation(diff, diff, ACT.Exp).then_inc(s2m["ediff"], 1)
                act_moe2(act)
            if stop >= 7:
                act.wait_ge(ld["w3a"], 16)
                act.wait_ge(ld["w3b"], 16)
                with act.Fori(0, B) as b:
                    j = b * 4 + J_G
                    act_self(act, ss, b + B, j, c3s)
                    act_out(act, so_, b * 2 + 2 * B, c3o)
                    act_ffn(act, sf, b * 2 + B, j + 1, c3f)
                    act_cross(act, sc_, b + 2 * B, j + 2, b, c3c)
                    act_out(act, so_, b * 2 + (2 * B + 1), c3p)
                    act_ffn(act, sf, b * 2 + (B + 1), j + 3, c3g)
            if stop >= 8:
                act_logits(act, J_H, B)
                act.wait_ge(s3m["extra"], 1)
                nc.scalar.activation(lg3, lg3, ACT.Sigmoid).then_inc(s3m["sig"], 1)
                act_moe3(act)

        @block.vector
        def _(v):
            ch = Chain(v, dve_step)
            v.wait_ge(cst["ready"], 1)
            v.wait_ge(ld["small"], 48)
            v.wait_ge(ld["w0a"], 16)
            dve_context(v, s0k, kv0, region("in16"), w0["bck"], row["b0cv"], region("y"), ch)
            dve_context(v, s1k, kv1, region("in16"), None, None, region("y"), ch)
            v.wait_ge(ld["w0f"], 16)
            nc.vector.tensor_reduce(amax[:, 0:1], w0f["wfc"], AX, ALU.max, apply_absolute_value=True)
            nc.vector.tensor_reduce(amax[:, 1:2], w0f["wproj"], AX, ALU.max, apply_absolute_value=True).then_inc(sq["amax"], 1)
            v.wait_ge(ld["w1f"], 16)
            for i, w in enumerate((w1f["winT"], w1f["wout"])):
                ins = nc.vector.tensor_reduce(aw[:, 8 * i:8 * i + 8], w.rearrange("p (f c) -> p f c", f=FC), AX,
                                              ALU.max, apply_absolute_value=True)
            ch.link(ins)
            ch.link(nc.vector.tensor_scalar(aw[:, 16:32], aw[:, 0:16], 1e-8, 1.0 / 127.0, ALU.max, ALU.mult))
            nc.vector.reciprocal(aw[:, 32:48], aw[:, 16:32]).then_inc(sq["w1scale"], 1)
            v.wait_ge(sq["all"], 1)
            ch.link(nc.vector.tensor_scalar(amax[:, 4:6], amax[:, 6:8], 1.0 / 127.0, None, ALU.mult))
            nc.vector.reciprocal(amax[:, 8:10], amax[:, 4:6]).then_inc(sq["w0scale"], 1)
            v.wait_ge(gate_ready, 1)
            v.wait_ge(ld["x"], 16)
            def x_tile(b):
                return lambda t: X[:, bass.ds(b * QT + t, 1), :].rearrange("p a c -> p (a c)")
            xnt = lambda t: xn[:, t, :]
            base = ch.after()
            with v.Fori(0, B) as b:
                ch = Chain(v, dve_step, base, b, DVE1_STEPS)
                dve_norm(ch, b * 3, x_tile(b), xnt).then_inc(xf["xn_ready"], 1)
                dve_self(v, ss, b, b * 3, c0s, ch)
                dve_cross(v, sc_, b * 2, None, b, c0c, ch)
                dve_yT(v, so_, b * 2, c0o)
                dve_residual(v, so_, b * 2, b, 0, tg[:, 0:1], row["b0p"], ch)
                dve_norm(ch, b * 3 + 1, x_tile(b), xnt).then_inc(xf["xn_ready"], 1)
                dve_ffn(v, sf, b, b * 3 + 1, c0f)
                dve_residual(v, sf, b, b, 4, tg[:, 4:5], row["b0proj"], ch)
                dve_norm(ch, b * 3 + 2, x_tile(b), xnt).then_inc(xf["xn_ready"], 1)
                dve_cross(v, sc_, b * 2 + 1, b * 3 + 2, b, c1c, ch)
                dve_yT(v, so_, b * 2 + 1, c1o)
                dve_residual(v, so_, b * 2 + 1, b, 0, tg[:, 1:2], None, ch)
                ch.close()
            v.memset(scratch(1), 0.0).then_inc(done["l01"], 1)
            base = ch.after(B)
            if stop >= 4:
                base = dve_l1ffn(v, base)
            if stop >= 5:
                base = dve_l2a(v, base)
            if stop >= 6:
                base = dve_logits(v, base, N_F, J_F, 0, E2, lg2)
                base = dve_route2(v, base)
                dve_moe2(v)
            if stop >= 7:
                base = dve_context3(v, base)
                base = dve_l3a(v, base)
            if stop >= 8:
                base = dve_logits(v, base, N_H, J_H, B, E3, lg3)
                base = dve_route3(v, base)
                dve_moe3(v)
            else:
                v.memset(scratch(1), 0.0).then_inc(done["all"], 1)


def kernel(**inputs):
    import numpy as np
    import concourse.bacc as bacc
    from concourse.bass_utils import run_bass_kernel_spmd

    a = {k: np.asarray(v) for k, v in inputs.items()}

    def chunks(w):
        k, m = w.shape
        return w.reshape(k // P, P, m).transpose(1, 0, 2).reshape(P, -1)

    def column(v):
        return v.reshape(-1, P).T

    def slots(w):
        z = np.zeros(w.shape[:-1] + (H, SLOT), w.dtype)
        z[..., :D0] = w.reshape(w.shape[:-1] + (H, D0))
        return z.reshape(w.shape[:-1] + (H * SLOT,))

    def heads(w):
        return w.transpose(1, 0, 2).reshape(w.shape[1], -1)

    x0 = {k[9:]: v for k, v in a.items() if k.startswith("L0_xattn_")}
    f0 = {k[7:]: v for k, v in a.items() if k.startswith("L0_ffn_")}
    x1 = {k[9:]: v for k, v in a.items() if k.startswith("L1_xattn_")}
    f1 = {k[7:]: v for k, v in a.items() if k.startswith("L1_ffn_")}
    x2 = {k[9:]: v for k, v in a.items() if k.startswith("L2_xattn_")}
    f2 = {k[7:]: v for k, v in a.items() if k.startswith("L2_ffn_")}
    x3 = {k[9:]: v for k, v in a.items() if k.startswith("L3_xattn_")}
    f3 = {k[7:]: v for k, v in a.items() if k.startswith("L3_ffn_")}
    packs = {
        "w0a": [chunks(slots(x0["Wq"])), chunks(slots(x0["Wk"])), chunks(x0["Wv"]), chunks(x0["Wcq"]), x0["Wck"],
                x0["Wcv"], chunks(x0["Wp"]), column(slots(x0["bq"])), column(slots(x0["bk"])), column(x0["bcq"]),
                column(x0["bck"])],
        "w0f": [chunks(f0["W_fc"].T), chunks(f0["W_proj"].T), chunks(f0["A_fc"].T), chunks(f0["A_proj"].T),
                column(f0["b_fc"])],
        "w1a": [chunks(x1["Wq"].T), x1["Wkv"].T[:, :C], x1["Wkv"].T[:, C:], chunks(x1["Wo"].T)],
        "w1f": [chunks(f1["W_in"].T), chunks(f1["W_out"]), column(f1["b_in"])],
        "w2a": [chunks(x2["Wq"]), x2["Wk"], x2["Wv"], column(x2["bq"]), column(x2["bk"]), chunks(f2["w_g"])],
        "w3g": [chunks(f3["gate_w"].T)],
    }
    for name, n in (("w3a", "a1_"), ("w3b", "a2_")):
        w = {k[3:]: v for k, v in x3.items() if k.startswith(n)}
        packs[name] = [chunks(heads(w["wq"])), chunks(heads(w["wk"])), chunks(heads(w["wv"])), chunks(w["li1_w"]),
                       chunks(w["li2_w"]), chunks(w["li3_w"]), column(w["lnx_g"]), column(w["lnx_b"]),
                       column(w["lny_g"]), column(w["lny_b"]), column(w["ln3_g"]), column(w["ln3_b"]),
                       column(w["li2_b"])]
    rows = [x0["bv"], x0["bcv"], x0["bp"], f0["b_proj"], f1["b_out"], x2["bv"], x3["ln1_g"], x3["ln1_b"],
            x3["ln2_g"], x3["ln2_b"], x3["a1_li1_b"], x3["a1_li3_b"], x3["a2_li1_b"], x3["a2_li3_b"], f3["gate_bias"]]
    ctx = a["ctx_512"]
    ctxT = ctx.transpose(2, 0, 1)
    e2 = np.concatenate([np.stack([chunks(w) for w in f2["c_fc"]]), np.stack([chunks(w) for w in f2["c_proj"]])], 2)

    def expert3(gate, up, down):
        d = np.zeros((3 * P, C), down.dtype)
        d[:I3] = down.T
        return np.concatenate([chunks(gate.T), chunks(up.T), chunks(d)], 1)
    e3 = [expert3(f3["gate_proj"][e], f3["up_proj"][e], f3["down_proj"][e]) for e in range(E3)]
    for i in range(2):
        part = slice(i * I3, (i + 1) * I3)
        e3.append(expert3(f3["shared_gate_w"][part], f3["shared_up_w"][part], f3["shared_down_w"][:, part]))

    arrays = {
        "x": a["x"].reshape(B * T, C),
        "ctxT": np.concatenate([np.stack([ctxT, ctxT], 2).reshape(P, -1), ctxT.reshape(P, -1)], 1),
        "ctx": np.concatenate([ctx, ctx], 1).transpose(1, 0, 2).reshape(P, -1),
        "gates": np.concatenate([a["g_xattn"], a["g_ffn"]])[None],
        "lora": np.concatenate([f0["B_fc"].T, f0["B_proj"].T], 1),
        "rows": np.concatenate(rows)[None],
        "e2": e2, "e3": np.stack(e3),
    }
    arrays.update({k: np.concatenate(v, 1) for k, v in packs.items()})
    arrays = {k: np.ascontiguousarray(v) for k, v in arrays.items()}
    nc = bacc.Bacc("TRN2", target_bir_lowering=False, num_devices=1)
    ap = {k: nc.dram_tensor(k, v.shape, F32, kind="ExternalInput").ap() for k, v in arrays.items()}
    scratch = [nc.dram_tensor(name, (n, C), F32, kind="Internal").ap()
               for name, n in (("slots2", S2 + 2 * NT * P), ("yslots2", S2 + P))]
    out = nc.dram_tensor("out", (B * T, C), F32, kind="ExternalOutput").ap()
    program(nc, STOP, ap["x"], ap["ctxT"], ap["ctx"], ap["gates"], {k: ap[k] for k in packs}, ap["lora"], ap["rows"],
            ap["e2"], ap["e3"], *scratch, out)
    r = run_bass_kernel_spmd(nc, [arrays], core_ids=[0])
    return r.results[0]["out"].reshape(B, T, C)


STOP = 8
```

```python
import concourse.bass as bass
from concourse import mybir
from contextlib import ExitStack

F32 = mybir.dt.float32
U32 = mybir.dt.uint32
BF16 = mybir.dt.bfloat16
ALU = mybir.AluOpType
ACT = mybir.ActivationFunctionType
AX, AXY = mybir.AxisListType.X, mybir.AxisListType.XY
RMAX = bass.bass_isa.ReduceOp.max

P = 128
B, T, C = 4, 512, 256
QT = T // P
NT = B * QT
KC = C // P
TC, CC = 64, 128
H = 16
FF = 4 * C
FC = FF // P
D0, D3 = 16, 32
SLOT = 32
G = H * SLOT // P
RANK = 16
LORA_SCALE = 32 / RANK
E2, CAP = 8, 640
E3, I3 = 16, 352
NX3 = E3 + 2
IC3 = [128, 128, 96]
EPS = 1e-5
ROUND = 12582912.0
NEG = -1e30

PACKS = {
    "w0a": dict(wq=2 * 512, wk=2 * 512, wv=2 * 256, wcq=2 * 256, wck=256, wcv=256, wp=2 * 256,
                bq=4, bk=4, bcq=2, bck=2),
    "w0f": dict(wfc=2 * FF, wproj=FC * 256, bfc=FC),
    "w1a": dict(wq=2 * 256, wk=256, wv=256, wo=2 * 256),
    "w1f": dict(winT=FC * 256, wout=FC * 256, bin=FC),
    "w2a": dict(wq=2 * 256, wk=256, wv=256, bq=2, bk=2, wg=2 * E2),
    "w3a": dict(wq=2 * 512, wk=2 * 512, wv=2 * 512, li1=4 * 256, li2=2 * FF, li3=FC * 256,
                xg=2, xb=2, yg=2, yb=2, g3=2, b3=2, bh=FC),
    "w3b": dict(wq=2 * 512, wk=512, wv=512, li1=4 * 256, li2=2 * FF, li3=FC * 256,
                xg=2, xb=2, yg=1, yb=1, g3=2, b3=2, bh=FC),
    "w3g": dict(gw=2 * E3),
}
ROWS = ["b0v", "b0cv", "b0p", "b0proj", "b1out", "b2v", "ln1g", "ln1b", "ln2g", "ln2b",
        "a1li1b", "a1li3b", "a2li1b", "a2li3b"]
NROWS = len(ROWS) * C + E3
S2 = E2 * CAP
TOPK3 = 4
ST3 = 2
NB3 = -(-(TOPK3 * B * T // (ST3 * P) + E3) // 3) * 3
GT2 = (3, 2)
W2X = 2 * FF + FC * 256
W3X = 2 * 2 * I3 + 3 * 256


def width(pack):
    return sum(PACKS[pack].values())


def program(nc, x_in, ctxT_in, ctx_in, gates_in, packs_in, lora_in, rows_in, e2_in, e3_in,
            slots2, yslots2, slots3, yslots3, out):
    ctx = ExitStack()
    with ctx:
        def sems(stage, names):
            return dict(**{n: ctx.enter_context(nc.semaphore(f"{stage}_{n}")) for n in names.split()})

        LAY, at = {}, 0
        regions = [("X", NT * C), ("rows", NROWS),
                   ("ident", P), ("ones", P), ("causal", P), ("later", P), ("upto", P), ("ctx", 3 * B * TC),
                   ("in16", 8), ("in32", 4), ("in64", 2), ("lower", E3 * E3), ("gates", 8),
                   ("tgate", 8), ("small", 860),
                   ("qT", 4 * T), ("kT", 4 * T), ("V", QT * 512), ("y", QT * 512), ("spare", 1024),
                   ("xn", QT * C), ("xT", KC * T), ("yT", KC * T), ("Pr", 2 * 1024), ("PT", 2 * 1024),
                   ("kv", 10368), ("wa", width("w0a") + width("w0f") + width("w1a")), ("wf", 2 * 2048 + FC)]
        for name, n in regions:
            LAY[name] = (at, n)
            at += n
        arena = ctx.enter_context(nc.sbuf_tensor("arena", [P, at], F32))
        slot_of3 = ctx.enter_context(nc.sbuf_tensor("slot_of3", [P, TOPK3 * NT], U32))
        weight_row3 = ctx.enter_context(nc.sbuf_tensor("weight_row3", [P, NB3], U32))
        batch_row3 = ctx.enter_context(nc.sbuf_tensor("batch_row3", [P, 3], U32))
        batch_u = ctx.enter_context(nc.sbuf_tensor("batch_u", [P, NB3], U32))
        lane_u = ctx.enter_context(nc.sbuf_tensor("lane_u", [P, 1], U32))
        row_of2 = ctx.enter_context(nc.sbuf_tensor("row_of2", [P, 2 * NT], U32))
        spare_u = ctx.enter_context(nc.sbuf_tensor("spare_u", [P, 2 * NT], U32))
        slot_of2 = ctx.enter_context(nc.sbuf_tensor("slot_of2", [P, 2 * NT], U32))
        ident16 = ctx.enter_context(nc.sbuf_tensor("ident16", [P, P], BF16))
        causal16 = ctx.enter_context(nc.sbuf_tensor("causal16", [P, P], BF16))
        zeros = ctx.enter_context(nc.sbuf_tensor("zeros", [P, C], F32))

        def region(name, off=0, n=None):
            a, size = LAY[name]
            n = size - off if n is None else n
            assert off + n <= at - a
            return arena[:, a + off:a + off + n]

        def view(name, pattern, start=0, cols=None, **k):
            return region(name, start, cols).rearrange(pattern, **k)

        PS = ctx.enter_context(nc.psum_tensor("PS", [P, 8, 512], F32))
        X = view("X", "p (t c) -> p t c", c=C)
        XN = view("V", "p (t c) -> p t c", 0, NT * C, c=C)
        XNT = view("V", "p (k n) -> p k n", 0, KC * NT * P, k=KC)
        ident = region("ident")
        ones = region("ones")
        small = region("small")
        tg = region("tgate")
        xn = view("xn", "p (t c) -> p t c", c=C)
        xT = view("xT", "p (k n) -> p k n", k=KC)
        xT2 = view("y", "p (k n) -> p k n", 0, KC * T, k=KC)
        x1 = view("spare", "p (t c) -> p t c", c=C)
        xo = view("yT", "p (t c) -> p t c", c=C)
        qT = view("qT", "p (k n) -> p k n", n=T)
        kT = view("kT", "p (k n) -> p k n", n=T)
        hT = arena[:, LAY["qT"][0]:LAY["qT"][0] + FC * T].rearrange("p (k n) -> p k n", n=T)
        PRB = [region("Pr", i * 512, 512) for i in range(3)]
        PTB = [region("PT", i * 512, 512) for i in range(2)]
        QM0, QM3 = ([[region(n, i * T, T) for n, i in heads4] for heads4 in
                     ((("xn", 0), ("xn", 1), (free, 0), (free, 1)), (("yT", 0), ("yT", 1), ("PT", 2), ("PT", 3)))]
                    for free in ("spare", "xT"))
        row = {n: region("rows", i * C, C) for i, n in enumerate(ROWS)}
        gbias = region("rows", len(ROWS) * C, E3)

        def pack_views(names, start, name):
            off = start
            res = {}
            for pk in names:
                d = {}
                for k, n in PACKS[pk].items():
                    d[k] = region(name, off, n)
                    off += n
                res[pk] = dict(**d)
            return res
        W = pack_views(["w0a", "w0f", "w1a"], 0, "wa")
        W.update(pack_views(["w1f"], 0, "wf"))
        W.update(pack_views(["w2a"], 0, "kv"))
        W3_OFF = width("w2a") + 64
        W.update(pack_views(["w3a", "w3b", "w3g"], W3_OFF, "kv"))
        KV3_OFF = W3_OFF + width("w3a") + width("w3b") + width("w3g")
        win = region("Pr", 0, 2 * FF)

        def kv_views(name, off, d):
            nch = H * d // P
            kb = region(name, off, nch * B * (P // d) * TC).rearrange("p (c b n) -> p c b n", c=nch, b=B)
            off += nch * B * (P // d) * TC
            nv = H // 2 * 2 * (d + 1)
            vb = region(name, off, B * nv).rearrange("p (b r e) -> p b r e", b=B, r=H // 2)
            return dict(k=kb, v=vb, d=d, nch=nch), off + B * nv
        kv0, o1 = kv_views("kv", 0, D0)
        kv1, o1 = kv_views("kv", o1, D0)
        kv3, o3 = kv_views("kv", KV3_OFF, D3)
        assert LAY["kv"][0] + o3 <= at, (LAY["kv"][0] + o3, at)
        assert o1 <= 10368

        ctxdup = region("ctx", 0, B * 2 * TC).rearrange("p (b j n) -> p b j n", b=B, j=2)
        ctxT = region("ctx", B * 2 * TC, B * TC)

        so = [0]

        def scratch(n):
            so[0] += n
            assert so[0] <= LAY["small"][1], so[0]
            return small[:, so[0] - n:so[0]]
        stats = scratch(QT * 6)
        mv = scratch(QT * 2)
        rstd = scratch(QT)
        varp = scratch(QT)
        nmax = scratch(64)
        rsum = scratch(64)
        rrec = scratch(64)
        amax = scratch(16)
        mhalf = scratch(4)
        carrier = scratch(1)
        cround = scratch(1)
        wcomb = scratch(NT * NX3)
        aw = scratch(3 * 16)
        ax = scratch(16)
        mv3 = mv.rearrange("p (t k) -> p t k", k=2)

        ld = sems("ld", "zeroed x ctx small w0a w0f w1a w1f w2a w3a w3b w3g stored ctx3")
        cst = sems("const", "step ready")
        norm = sems("norm", "var rstd")
        xf = sems("features", "xn_ready xT_psum xT_act xT_dve")
        N_L01, N_D, N_E, N_F, N_CTX, N_G, N_H = 0, 12, 16, 20, 24, 25, 49
        J_D, J_E, J_F, J_G, J_H = 12, 16, 20, 24, 40

        class Chain:
            def __init__(self, eng, sem, base=0, it=None, per=0):
                self.eng, self.sem, self.base, self.it, self.per, self.n = eng, sem, base, it, per, 0

            def value(self, n):
                return self.base + (n if self.it is None else self.it * self.per + n)

            def mark(self, ins):
                ins.then_inc(self.sem, 1)
                self.n += 1
                return self.n

            def wait(self, n):
                self.eng.wait_ge(self.sem, self.value(n))

            def link(self, ins):
                self.wait(self.mark(ins))

            def close(self):
                assert self.it is None or self.n == self.per, f"{self.sem}: {self.n} steps, {self.per} said"

            def after(self, iterations=1):
                return self.base + self.n * iterations

        def dve_stats(src, tiles):
            nc.vector.memset(carrier, 0.0)
            for t in tiles:
                last = nc.vector.bn_stats(stats[:, 6 * t:6 * t + 6], src(t))
            return last

        def dve_norm(ch, it, src, dst, n=QT, first=0):
            v = nc.vector
            ch.link(dve_stats(src, range(first, n)))
            v.memset(carrier, 0.0)
            for t in range(n):
                last = v.bn_aggr(mv[:, 2 * t:2 * t + 2], stats[:, 6 * t:6 * t + 6])
            ch.link(last)
            v.tensor_scalar(varp[:, 0:n], mv3[:, 0:n, 1], EPS, None, ALU.add).then_inc(norm["var"], 1)
            v.wait_ge(norm["rstd"], it + 1)
            for t in range(n):
                last = v.tensor_scalar(dst(t), src(t), mv[:, 2 * t:2 * t + 1], rstd[:, t:t + 1],
                                       ALU.subtract, ALU.mult)
            return last

        def pool_norm(pool, it, n=QT):
            pool.wait_ge(norm["var"], it + 1)
            nc.gpsimd.tensor_tensor(rstd[:, 0:n], varp[:, 0:n], mhalf[:, 0:n], ALU.pow).then_inc(norm["rstd"], 1)

        def pe_to_features(src, nchunk, bank0):
            last = []
            for c in range(nchunk):
                for t in range(QT):
                    ins = nc.tensor.transpose(PS[:, bank0 + c, t * P:(t + 1) * P],
                                              src[:, t, c * P:(c + 1) * P], ident)
                last.append(ins)
            return last

        def pe_features(pe, j):
            pe.wait_ge(xf["xn_ready"], j + 1)
            for ins in pe_to_features(xn, KC, 6):
                ins.then_inc(xf["xT_psum"], 1)
            pe.wait_ge(xf["xT_act"], j + 1)
            pe.wait_ge(xf["xT_dve"], j + 1)

        def pe_context(pe, s, kv, wk, wv, kT_src, vdup, ready):
            ready()
            for c in range(kv["nch"]):
                nc.tensor.matmul(PS[:, c, 0:B * TC], wk[:, c * P:(c + 1) * P], kT_src,
                                 start=True, stop=True).then_inc(s["kv_psum"], 1)
            for b in range(B):
                nc.tensor.matmul(PS[:, 4 + b, 0:H * kv["d"]], vdup(b), wv, start=True, stop=True).then_inc(s["kv_psum"], 1)

        def dve_context(v, s, kv, inmask, bk, bv, tmp, ch):
            hc = P // kv["d"]
            for c in range(kv["nch"]):
                v.wait_ge(s["kv_psum"], c + 1)
                src = PS[:, c, 0:B * TC]
                if bk is not None:
                    t = tmp[:, c * B * TC:(c + 1) * B * TC]
                    ch.link(nc.vector.tensor_scalar(t, src, bk[:, c:c + 1], None, ALU.add))
                    src = t
                for b in range(B):
                    nc.vector.tensor_tensor(
                        kv["k"][:, c, b, :].rearrange("p (h n) -> p h n", h=hc),
                        src[:, b * TC:(b + 1) * TC].unsqueeze(1).to_broadcast([P, hc, TC]),
                        inmask.unsqueeze(2).to_broadcast([P, hc, TC]), ALU.mult).then_inc(s["kv_ready"], 1)
            for b in range(B):
                v.wait_ge(s["kv_psum"], kv["nch"] + b + 1)
                src = PS[:, 4 + b, 0:H * kv["d"]]
                if bv is not None:
                    at0 = kv["nch"] * B * TC + b * H * kv["d"]
                    t = tmp[:, at0:at0 + H * kv["d"]]
                    ch.link(nc.vector.tensor_tensor(t, src, bv, ALU.add))
                    src = t
                vb = kv["v"][:, b].rearrange("p r (j e) -> p r j e", j=2)
                for j in range(2):
                    nc.vector.tensor_scalar(
                        vb[:, :, j, 0:kv["d"]],
                        src.rearrange("p (r j e) -> p r j e", j=2, e=kv["d"])[:, :, j, :],
                        half[:, j:j + 1], None, ALU.mult).then_inc(s["kv_ready"], 1)
                    nc.vector.tensor_copy(vb[:, :, j, kv["d"]:kv["d"] + 1],
                                          half[:, j:j + 1].unsqueeze(1).to_broadcast([P, H // 2, 1])
                                          ).then_inc(s["kv_ready"], 1)

        half = region("in64")

        def kv_count(kv):
            return kv["nch"] * B + B * 4

        SELF = [(g, hh, qt) for g in range(G) for hh in range(4) for qt in range(QT)]
        NS = len(SELF)
        SELF_SEMS = ("q_head proj_psum proj_act proj_dve scores nmax probs pT_psum pT "
                     "heads y")

        def evac_engines(values_on):
            return "da" * G + values_on * QT

        def nth(e, engines, j):
            return engines[:j + 1].count(e)

        def keys_of(qt, causal):
            return (list(range(qt + 1)), (qt + 1) * P) if causal else (list(range(qt, QT)), T)

        def pe_self(pe, s, it, j, cfg):
            engines = cfg["engines"]
            n_a, n_d = engines.count("a"), engines.count("d")
            pe_features(pe, j)
            for i, e in enumerate(engines):
                if i >= 2:
                    before = engines[i - 2]
                    if before == "a":
                        pe.wait_ge(s["proj_act"], it * n_a + nth("a", engines, i - 2))
                    else:
                        pe.wait_ge(s["proj_dve"], it * n_d + nth("d", engines, i - 2))
                for k in range(KC):
                    if i < 2 * G:
                        w = (cfg["wq"], cfg["wk"])[i % 2][:, k * 512 + (i // 2) * P:k * 512 + (i // 2 + 1) * P]
                        src = (cfg["xq"], cfg["xkv"])[i % 2]
                        ins = nc.tensor.matmul(PS[:, 6 + i % 2, :], w, src[:, k, :], start=k == 0, stop=k == KC - 1)
                    else:
                        t = i - 2 * G
                        nv = H * cfg["d"]
                        ins = nc.tensor.matmul(PS[:, 6 + i % 2, 0:nv], cfg["xkv"][:, k, t * P:(t + 1) * P],
                                               cfg["wv"][:, k * nv:(k + 1) * nv], start=k == 0, stop=k == KC - 1)
                ins.then_inc(s["proj_psum"], 1)
            pe.wait_ge(s["proj_act"], it * n_a + n_a)
            pe.wait_ge(s["proj_dve"], it * n_d + n_d)

            for n in range(NS + 3):
                if n < NS:
                    g, hh, qt = SELF[n]
                    if qt == 0:
                        pe.wait_ge(s["q_head"], it * H + g * 4 + hh + 1)
                    if n >= 3:
                        pe.wait_ge(s["probs"], it * NS + n - 2)
                    kcs, w = keys_of(qt, cfg["causal"])
                    ins = nc.tensor.matmul(PS[:, n % 3, 0:w], cfg["qm"][(g + 1) % 2][hh][:, qt * P:(qt + 1) * P],
                                           kT[:, g, 0:w], start=True, stop=not cfg["causal"])
                    if cfg["causal"]:
                        ins = nc.tensor.matmul(PS[:, n % 3, qt * P:w], ident16[:, :], causal16[:, :], start=False, stop=True)
                    ins.then_inc(s["scores"], 1)
                m = n - 2
                if 0 <= m < NS:
                    g, hh, qt = SELF[m]
                    kcs, w = keys_of(qt, cfg["causal"])
                    pe.wait_ge(s["probs"], it * NS + m + 1)
                    if m >= 2:
                        pe.wait_ge(s["pT"], it * NS + m - 1)
                    for kc in kcs:
                        ins = nc.tensor.transpose(PS[:, (3, 6)[m % 2], kc * P:(kc + 1) * P],
                                                  PRB[m % 3][:, kc * P:(kc + 1) * P], ident)
                    ins.then_inc(s["pT_psum"], 1)
                m = n - 3
                if m >= 0:
                    g, hh, qt = SELF[m]
                    kcs, w = keys_of(qt, cfg["causal"])
                    pe.wait_ge(s["pT"], it * NS + m + 1)
                    if hh == 0 and qt == 0 and g >= 2:
                        pe.wait_ge(s["y"], it * G + g - 1)
                    col = (hh * QT + qt) * cfg["d"]
                    h = g * 4 + hh
                    for kc in kcs:
                        ins = nc.tensor.matmul(PS[:, 4 + g % 2, col:col + cfg["d"]],
                                               PTB[m % 2][:, kc * P:(kc + 1) * P],
                                               cfg["V"][:, kc, h * cfg["d"]:(h + 1) * cfg["d"]],
                                               start=kc == kcs[0], stop=kc == kcs[-1])
                    ins.then_inc(s["heads"], 1)

        def pool_self(pool, s, it, cfg, between={}):
            engines = cfg["engines"]
            n_a, n_d = engines.count("a"), engines.count("d")
            for g in range(G):
                pool.wait_ge(s["proj_dve"], it * n_d + g + 1)
                if g == 1:
                    pool.wait_ge(s["proj_dve"], it * n_d + n_d)
                    pool.wait_ge(s["proj_act"], it * n_a + n_a)
                if g >= 2:
                    pool.wait_ge(s["scores"], it * NS + (g - 1) * 16)
                for hh in range(4):
                    nc.gpsimd.tensor_tensor(cfg["qm"][(g + 1) % 2][hh], qT[:, g, :],
                                            region("in32")[:, hh:hh + 1].to_broadcast([P, T]), ALU.mult
                                            ).then_inc(s["q_head"], 1)
                if g in between:
                    between[g]()

        def act_self(act, s, it, j, cfg):
            engines = cfg["engines"]
            act.wait_ge(xf["xT_psum"], XT(j))
            cfg["copy_x_act"]()
            for i, e in enumerate(engines):
                if e == "a":
                    act.wait_ge(s["proj_psum"], it * len(engines) + i + 1)
                    if i < 2 * G:
                        bias = cfg["bk"][:, i // 2:i // 2 + 1] if cfg["bk"] is not None else 0.0
                        nc.scalar.activation(kT[:, i // 2, :], PS[:, 6 + i % 2, :], ACT.Identity, bias=bias
                                             ).then_inc(s["proj_act"], 1)
                    else:
                        nc.scalar.activation(cfg["V"][:, i - 2 * G, :], PS[:, 6 + i % 2, 0:H * cfg["d"]], ACT.Copy
                                             ).then_inc(s["proj_act"], 1)
            for n in range(NS):
                g, hh, qt = SELF[n]
                kcs, w = keys_of(qt, cfg["causal"])
                act.wait_ge(s["nmax"], it * NS + n + 1)
                if n >= 3:
                    act.wait_ge(s["pT_psum"], it * NS + n - 2)
                nc.scalar.activation(PRB[n % 3][:, 0:w], PS[:, n % 3, 0:w], ACT.Exp, bias=nmax[:, n:n + 1],
                                     accum_out=rsum[:, n:n + 1]).then_inc(s["probs"], 1)

        def dve_self(v, s, it, j, cfg, ch):
            engines = cfg["engines"]
            v.wait_ge(xf["xT_psum"], XT(j))
            cfg["copy_x_dve"]()
            for i, e in enumerate(engines):
                if e == "d":
                    v.wait_ge(s["proj_psum"], it * len(engines) + i + 1)
                    if i < 2 * G:
                        if cfg["bq"] is not None:
                            nc.vector.tensor_scalar(qT[:, i // 2, :], PS[:, 6 + i % 2, :], cfg["bq"][:, i // 2:i // 2 + 1],
                                                    cfg["scale"], ALU.add, ALU.mult).then_inc(s["proj_dve"], 1)
                        else:
                            nc.vector.tensor_scalar(qT[:, i // 2, :], PS[:, 6 + i % 2, :], cfg["scale"], None,
                                                    ALU.mult).then_inc(s["proj_dve"], 1)
                    else:
                        prod = PS[:, 6 + i % 2, 0:H * cfg["d"]]
                        if cfg["bv"] is not None:
                            ins = nc.vector.tensor_tensor(cfg["V"][:, i - 2 * G, :], prod, cfg["bv"], ALU.add)
                        else:
                            ins = nc.vector.tensor_copy(cfg["V"][:, i - 2 * G, :], prod)
                        ins.then_inc(s["proj_dve"], 1)

            def group_out(g):
                v.wait_ge(s["heads"], it * NS + (g + 1) * 16)
                ch.link(nc.vector.reciprocal(rrec[:, g * 16:(g + 1) * 16], rsum[:, g * 16:(g + 1) * 16]))
                for hh in range(4):
                    h = g * 4 + hh
                    ins = nc.vector.tensor_tensor(
                        cfg["y"][:, :, h * cfg["d"]:(h + 1) * cfg["d"]],
                        PS[:, 4 + g % 2, hh * QT * cfg["d"]:(hh + 1) * QT * cfg["d"]].rearrange("p (t d) -> p t d", t=QT),
                        rrec[:, g * 16 + hh * 4:g * 16 + hh * 4 + 4].unsqueeze(2).to_broadcast([P, QT, cfg["d"]]),
                        ALU.mult)
                ins.then_inc(s["y"], 1)

            for n in range(NS + 2):
                if n < NS:
                    g, hh, qt = SELF[n]
                    kcs, w = keys_of(qt, cfg["causal"])
                    v.wait_ge(s["scores"], it * NS + n + 1)
                    nc.vector.tensor_reduce(nmax[:, n:n + 1], PS[:, n % 3, 0:w], AX, ALU.max, negate=True
                                            ).then_inc(s["nmax"], 1)
                m = n - 2
                if m >= 0:
                    g, hh, qt = SELF[m]
                    kcs, w = keys_of(qt, cfg["causal"])
                    v.wait_ge(s["pT_psum"], it * NS + m + 1)
                    if m >= 2:
                        v.wait_ge(s["heads"], it * NS + m - 1)
                    lo, hi = kcs[0] * P, (kcs[-1] + 1) * P
                    if cfg["causal"]:
                        ins = nc.vector.tensor_copy(PTB[m % 2][:, lo:hi], PS[:, (3, 6)[m % 2], lo:hi])
                    else:
                        ins = nc.vector.tensor_tensor(PTB[m % 2][:, lo:lo + P], PS[:, (3, 6)[m % 2], lo:lo + P],
                                                      region("later"), ALU.mult)
                        if hi > lo + P:
                            ins = nc.vector.tensor_copy(PTB[m % 2][:, lo + P:hi], PS[:, (3, 6)[m % 2], lo + P:hi])
                    ins.then_inc(s["pT"], 1)
                if n % 16 == 4 and n > 16:
                    group_out(n // 16 - 1)
            group_out(G - 1)

        CROSS_SEMS = "q_psum q scores shifted probs pT_psum pT heads y"

        def pe_cross(pe, s, it, j, b, cfg):
            kv = cfg["kv"]
            if cfg["norm"]:
                pe_features(pe, j)
            for c in range(kv["nch"]):
                if c >= 2:
                    pe.wait_ge(s["q"], it * 4 + (c - 1) * (4 // kv["nch"]))
                for k in range(KC):
                    ins = nc.tensor.matmul(PS[:, 6 + c % 2, :], cfg["wq"][:, k * H * kv["d"] + c * P:k * H * kv["d"] + (c + 1) * P],
                                           xT[:, k, :], start=k == 0, stop=k == KC - 1)
                ins.then_inc(s["q_psum"], 4 // kv["nch"])
            pe.wait_ge(s["q"], it * 4 + 4)

            def scores(t):
                if t >= 2:
                    pe.wait_ge(s["shifted"], it * QT + t - 1)
                per = (P // kv["d"]) * TC
                for c in range(kv["nch"]):
                    bank, col = divmod(c * per, 512)
                    ins = nc.tensor.matmul(PS[:, 2 * (t % 2) + bank, col:col + per],
                                           qT[:, c, t * P:(t + 1) * P],
                                           kv["k"][:, c, bass.ds(b, 1), :].rearrange("p b n -> p (b n)"),
                                           start=True, stop=True)
                ins.then_inc(s["scores"], 1)
            scores(0)
            scores(1)
            for t in range(QT):
                pe.wait_ge(s["probs"], it * QT + t + 1)
                if t >= 1:
                    pe.wait_ge(s["pT"], (it * QT + t) * 2)
                for r in range(H // 2):
                    ins = nc.tensor.transpose(PS[:, 4 + r // 4, (r % 4) * P:(r % 4 + 1) * P],
                                              region("Pr", (t % 2) * 1024 + r * P, P), ident)
                    if r % 4 == 3:
                        ins.then_inc(s["pT_psum"], 1)
                if t + 2 < QT:
                    scores(t + 2)
                pe.wait_ge(s["pT"], (it * QT + t) * 2 + 2)
                if t >= 1:
                    pe.wait_ge(s["y"], it * QT + t)
                for r in range(H // 2):
                    col = (r % 4) * 2 * (kv["d"] + 1)
                    ins = nc.tensor.matmul(PS[:, 6 + r // 4, col:col + 2 * (kv["d"] + 1)],
                                           region("PT", (t % 2) * 1024 + r * P, P),
                                           kv["v"][:, bass.ds(b, 1), r, :].rearrange("p b e -> p (b e)"),
                                           start=True, stop=True)
                ins.then_inc(s["heads"], 1)

        def act_cross(act, s, it, j, b, cfg):
            if cfg["norm"]:
                act.wait_ge(xf["xT_psum"], XT(j))
                cfg["copy_x_act"]()

            def exp(t):
                act.wait_ge(s["shifted"], it * QT + t + 1)
                pr = region("Pr", (t % 2) * 1024, 1024)
                nc.scalar.activation(pr, pr, ACT.Exp).then_inc(s["probs"], 1)
            exp(0)
            for t in range(QT):
                if t + 1 < QT:
                    exp(t + 1)
                for i in range(2):
                    act.wait_ge(s["pT_psum"], (it * QT + t) * 2 + i + 1)
                    nc.scalar.activation(region("PT", (t % 2) * 1024 + i * 512, 512), PS[:, 4 + i, :], ACT.Copy
                                         ).then_inc(s["pT"], 1)

        def dve_cross(v, s, it, j, b, cfg, ch):
            kv = cfg["kv"]
            if cfg["norm"]:
                v.wait_ge(xf["xT_psum"], XT(j))
                cfg["copy_x_dve"]()
            for c in range(kv["nch"]):
                v.wait_ge(s["q_psum"], it * 4 + (c + 1) * (4 // kv["nch"]))
                if cfg["bq"] is not None:
                    nc.vector.tensor_scalar(qT[:, c, :], PS[:, 6 + c % 2, :], cfg["bq"][:, c:c + 1], cfg["scale"],
                                            ALU.add, ALU.mult).then_inc(s["q"], 4 // kv["nch"])
                else:
                    nc.vector.tensor_scalar(qT[:, c, :], PS[:, 6 + c % 2, :], cfg["scale"], None, ALU.mult
                                            ).then_inc(s["q"], 4 // kv["nch"])

            def shift(t):
                v.wait_ge(s["scores"], it * QT + t + 1)
                if t >= 2:
                    v.wait_ge(s["pT_psum"], (it * QT + t - 1) * 2)
                sc = PS[:, 2 * (t % 2):2 * (t % 2) + 2, :].rearrange("p a (h n) -> p a h n", n=TC)
                mx = nmax[:, t * H:(t + 1) * H]
                ch.link(nc.vector.tensor_reduce(mx, sc, AX, ALU.max))
                nc.vector.tensor_tensor(
                    region("Pr", (t % 2) * 1024, 1024).rearrange("p (a h n) -> p a h n", a=2, n=TC), sc,
                    mx.rearrange("p (a h) -> p a h", a=2).unsqueeze(3).to_broadcast([P, 2, H // 2, TC]), ALU.subtract
                    ).then_inc(s["shifted"], 1)
            shift(0)
            shift(1)
            for t in range(QT):
                if t + 2 < QT:
                    shift(t + 2)
                v.wait_ge(s["heads"], it * QT + t + 1)
                o = PS[:, 6:8, 0:H // 2 * (kv["d"] + 1)].rearrange("p a (h e) -> p a h e", e=kv["d"] + 1)
                rr = rrec[:, t * H:(t + 1) * H].rearrange("p (a h) -> p a h", a=2).unsqueeze(3)
                ch.link(nc.vector.reciprocal(rr, o[:, :, :, kv["d"]:kv["d"] + 1]))
                yt = cfg["y"][:, t, :].rearrange("p (a h e) -> p a h e", a=2, e=kv["d"])
                if cfg["add"]:
                    tmp = xn[:, t, :].rearrange("p (a h e) -> p a h e", a=2, e=kv["d"])
                    ch.link(nc.vector.tensor_tensor(tmp, o[:, :, :, 0:kv["d"]],
                                                    rr.to_broadcast([P, 2, H // 2, kv["d"]]), ALU.mult))
                    nc.vector.tensor_tensor(yt, yt, tmp, ALU.add).then_inc(s["y"], 1)
                else:
                    nc.vector.tensor_tensor(yt, o[:, :, :, 0:kv["d"]], rr.to_broadcast([P, 2, H // 2, kv["d"]]),
                                            ALU.mult).then_inc(s["y"], 1)

        OUT_SEMS = "yT_psum yT_act yT_dve out_psum"

        def pe_out(pe, s, it, cfg, y_wait):
            nch = cfg["nch"]
            y_wait()
            for c in range(nch):
                if c >= 2:
                    if c % 2 == 0:
                        pe.wait_ge(s["yT_act"], it * 2 + (c // 2) * (4 // nch))
                    else:
                        pe.wait_ge(s["yT_dve"], it * 2 + (c // 2) * (4 // nch))
                for t in range(QT):
                    ins = nc.tensor.transpose(PS[:, 6 + c % 2, t * P:(t + 1) * P],
                                              cfg["y"][:, t, c * P:(c + 1) * P], ident)
                ins.then_inc(s["yT_psum"], 4 // nch)
            pe.wait_ge(s["yT_act"], it * 2 + 2)
            pe.wait_ge(s["yT_dve"], it * 2 + 2)
            for t in range(QT):
                for c in range(nch):
                    ins = nc.tensor.matmul(PS[:, t // 2, (t % 2) * C:(t % 2 + 1) * C], qT[:, c, t * P:(t + 1) * P],
                                           cfg["wo"][:, c * C:(c + 1) * C], start=c == 0, stop=c == nch - 1)
                if t % 2:
                    ins.then_inc(s["out_psum"], 1)

        def act_out(act, s, it, cfg):
            for c in range(0, cfg["nch"], 2):
                act.wait_ge(s["yT_psum"], it * 4 + (c + 1) * (4 // cfg["nch"]))
                nc.scalar.activation(qT[:, c, :], PS[:, 6, :], ACT.Copy).then_inc(s["yT_act"], 4 // cfg["nch"])

        def dve_yT(v, s, it, cfg):
            for c in range(1, cfg["nch"], 2):
                v.wait_ge(s["yT_psum"], it * 4 + (c + 1) * (4 // cfg["nch"]))
                nc.vector.tensor_copy(qT[:, c, :], PS[:, 7, :]).then_inc(s["yT_dve"], 4 // cfg["nch"])

        def dve_residual(v, s, it, b, bank0, gate, bias, ch, src=None):
            if bias is not None:
                xr = X[:, bass.ds(b * QT, QT), :]
                ch.link(nc.vector.scalar_tensor_tensor(out=xr, in0=bias.unsqueeze(1).to_broadcast([P, QT, C]), scalar=gate,
                                                       in1=xr, op0=ALU.mult, op1=ALU.add))
            for i in range(2):
                v.wait_ge(s["out_psum"], it * 2 + i + 1)
                prod = PS[:, bank0 + i, :].rearrange("p (t c) -> p t c", t=2)
                xt = X[:, bass.ds(b * QT + 2 * i, 2), :]
                ch.link(nc.vector.scalar_tensor_tensor(out=xt, in0=prod, scalar=gate, in1=xt,
                                                       op0=ALU.mult, op1=ALU.add))
                if src is not None and i == 0:
                    dve_stats(src, range(2))

        FFN_SEMS = "h_psum h out_psum"

        def pe_ffn(pe, s, it, j, cfg):
            pe_features(pe, j)
            for f in range(FC):
                if f >= 4:
                    pe.wait_ge(s["h"], it * FC + f - 3)
                for k in range(KC):
                    ins = nc.tensor.matmul(PS[:, f % 4, :], cfg["w1"][:, k * FF + f * P:k * FF + (f + 1) * P], xT[:, k, :],
                                           start=k == 0, stop=k == KC - 1)
                ins.then_inc(s["h_psum"], 1)
            for t in range(QT):
                for f in range(FC):
                    if t == 0:
                        pe.wait_ge(s["h"], it * FC + f + 1)
                    ins = nc.tensor.matmul(PS[:, 4 + t // 2, (t % 2) * C:(t % 2 + 1) * C], hT[:, f, t * P:(t + 1) * P],
                                           cfg["w2"][:, f * C:(f + 1) * C], start=f == 0, stop=f == FC - 1)
                if t % 2:
                    ins.then_inc(s["out_psum"], 1)

        def act_ffn(act, s, it, j, cfg):
            act.wait_ge(xf["xT_psum"], XT(j))
            cfg["copy_x_act"]()
            for f in range(FC):
                act.wait_ge(s["h_psum"], it * FC + f + 1)
                nc.scalar.activation(hT[:, f, :], PS[:, f % 4, :], ACT.Gelu, bias=cfg["b1"][:, f:f + 1]).then_inc(s["h"], 1)

        def dve_ffn(v, s, it, j, cfg):
            v.wait_ge(xf["xT_psum"], XT(j))
            cfg["copy_x_dve"]()

        lora = arena[0:RANK, LAY["Pr"][0]:LAY["Pr"][0] + 2 * (FF + C)]
        B_fc, B_proj, A_fc, A_proj = (lora[:, i:i + n] for i, n in ((0, FF), (FF, C), (FF + C, C), (FF + 2 * C, FF)))

        def pe_lora():
            for i in range(4):
                nc.tensor.matmul(PS[:, i, :], A_fc[:, i // 2 * P:(i // 2 + 1) * P], B_fc[:, i % 2 * 512:(i % 2 + 1) * 512],
                                 start=True, stop=True)
            for f in range(FC):
                ins = nc.tensor.matmul(PS[:, 4 + f // 2, f % 2 * C:(f % 2 + 1) * C], A_proj[:, f * P:(f + 1) * P], B_proj,
                                       start=True, stop=True)
            ins.then_inc(sq["lora_psum"], 1)

        def dve_lora(v):
            v.wait_ge(sq["lora_psum"], 1)
            for j, w in enumerate((w0f["wfc"], w0f["wproj"])):
                for i in range(4):
                    wi = w[:, i * 512:(i + 1) * 512]
                    ins = nc.vector.scalar_tensor_tensor(out=wi, in0=PS[:, 4 * j + i, :], scalar=LORA_SCALE, in1=wi,
                                                         op0=ALU.mult, op1=ALU.add)
            ins.then_inc(sq["folded"], 1)

        def plain_copy_act():
            nc.scalar.activation(xT[:, 0, :], PS[:, 6, :], ACT.Copy).then_inc(xf["xT_act"], 1)

        def plain_copy_dve():
            nc.vector.tensor_copy(xT[:, 1, :], PS[:, 7, :]).then_inc(xf["xT_dve"], 1)

        def XT(j):
            return j * KC + KC

        def scaled_copies(g, bb, g2=None, b2=None):
            def a():
                ins = nc.scalar.activation(xT[:, 0, :], PS[:, 6, :], ACT.Identity, bias=bb[:, 0:1], scale=g[:, 0:1])
                if g2 is not None:
                    ins = nc.scalar.activation(xT2[:, 0, :], PS[:, 6, :], ACT.Identity, bias=b2[:, 0:1],
                                               scale=g2[:, 0:1])
                ins.then_inc(xf["xT_act"], 1)

            def d():
                ins = nc.vector.tensor_scalar(xT[:, 1, :], PS[:, 7, :], g[:, 1:2], bb[:, 1:2], ALU.mult, ALU.add)
                if g2 is not None:
                    ins = nc.vector.tensor_scalar(xT2[:, 1, :], PS[:, 7, :], g2[:, 1:2], b2[:, 1:2],
                                                  ALU.mult, ALU.add)
                ins.then_inc(xf["xT_dve"], 1)
            return a, d

        w0, w0f, w1, w3, w3b = W["w0a"], W["w0f"], W["w1a"], W["w3a"], W["w3b"]
        V0 = region("V", 0, QT * H * D0).rearrange("p (t c) -> p t c", t=QT)
        y0 = region("y", 0, QT * H * D0).rearrange("p (t c) -> p t c", t=QT)
        V3 = region("V", 0, QT * H * D3).rearrange("p (t c) -> p t c", t=QT)
        y3 = region("y", 0, QT * H * D3).rearrange("p (t c) -> p t c", t=QT)
        c0s = dict(qm=QM0, engines=evac_engines("d"), wq=w0["wq"], wk=w0["wk"], wv=w0["wv"], xq=xT, xkv=xT, d=D0, causal=True,
                  V=V0, y=y0, bq=w0["bq"], bk=w0["bk"], bv=row["b0v"], scale=D0 ** -0.5,
                  copy_x_act=plain_copy_act, copy_x_dve=plain_copy_dve)
        c0c = dict(kv=kv0, norm=False, wq=w0["wcq"], bq=w0["bcq"], scale=D0 ** -0.5, y=y0, add=True)
        c0o = dict(nch=2, y=y0, wo=w0["wp"])
        c0f = dict(w1=w0f["wfc"], w2=w0f["wproj"], b1=w0f["bfc"],
                  copy_x_act=plain_copy_act, copy_x_dve=plain_copy_dve)
        c1c = dict(kv=kv1, norm=True, wq=w1["wq"], bq=None, scale=D0 ** -0.5, y=y0, add=False,
                  copy_x_act=plain_copy_act, copy_x_dve=plain_copy_dve)
        c1o = dict(nch=2, y=y0, wo=w1["wo"])
        s0k, s1k = sems("kv0", "kv_psum kv_ready"), sems("kv1", "kv_psum kv_ready")
        ss, sc_, so_, sf = (sems("self", SELF_SEMS), sems("cross", CROSS_SEMS), sems("outproj", OUT_SEMS),
                            sems("ffn", FFN_SEMS))
        sq = sems("quant", "lora_psum folded amax all w1scale w1")
        gate_ready = sems("gate", "ready")["ready"]
        dve_step = sems("dve", "step")["step"]
        done = sems("done", "stages")["stages"]
        STAGE = {n: i + 1 for i, n in enumerate("l01 l1ffn l2a route2 l2moe l3a route3".split())}

        sd = sems("l1ffn", "win_psum win_act win_dve amax amax_all scale xq_act xq h_psum h hq_act hq out_psum "
                           "used")
        w1f = W["w1f"]
        Hall = arena[:, LAY["kv"][0]:LAY["kv"][0] + FC * B * T].rearrange("p (f n) -> p f n", f=FC)
        assert FC * B * T <= LAY["kv"][1] + LAY["wa"][1]

        def rows_of(b):
            return bass.ds(b * T, T)

        OUT1 = (4, 0)

        def pe_l1ffn(pe):
            s = sd
            pe.wait_ge(sq["w1"], 2)
            pe.wait_ge(done, STAGE["l01"])
            for k in range(KC):
                for f in range(FC):
                    ins = nc.tensor.transpose(PS[:, 2 * k + f // 4, (f % 4) * P:(f % 4 + 1) * P],
                                              w1f["winT"][:, f * C + k * P:f * C + (k + 1) * P], ident)
                ins.then_inc(s["win_psum"], 1)
            with pe.Fori(0, B) as b:
                pe_features(pe, b + J_D)
            pe.wait_ge(s["win_act"], 1)
            pe.wait_ge(s["win_dve"], 1)
            with pe.Fori(0, B) as b:
                pe.wait_ge(s["xq"], b + 1)
                for f in range(FC):
                    pe.wait_ge(s["h"], b * FC + f + 1)
                    for k in range(KC):
                        ins = nc.tensor.matmul(PS[:, f % 4, :], win[:, k * FF + f * P:k * FF + (f + 1) * P],
                                               XNT[:, k, rows_of(b)], start=k == 0, stop=k == KC - 1)
                    ins.then_inc(s["h_psum"], 1)
            for b in range(B):
                for f in range(FC):
                    pe.wait_ge(s["hq"], b * FC + f + 1)
                    for t in range(QT):
                        ins = nc.tensor.matmul(PS[:, OUT1[b % 2] + t, 0:C], hT[:, f, t * P:(t + 1) * P],
                                               w1f["wout"][:, f * C:(f + 1) * C], start=f == 0, stop=f == FC - 1)
                        if f == FC - 1 and t % 2:
                            ins.then_inc(s["out_psum"], 1)
                        elif t == QT - 1:
                            ins.then_inc(s["used"], 1)

        def act_l1ffn(act):
            s = sd
            act.wait_ge(s["win_psum"], 1)
            nc.scalar.activation(win[:, 0:FF], PS[:, 0:2, :].rearrange("p a n -> p (a n)"), ACT.Copy
                                 ).then_inc(s["win_act"], 1)
            with act.Fori(0, B) as b:
                act.wait_ge(xf["xT_psum"], XT(b + J_D))
                nc.scalar.activation(XNT[:, 0, rows_of(b)], PS[:, 6, :], ACT.Copy).then_inc(xf["xT_act"], 1)
            act.wait_ge(s["scale"], 1)
            act.wait_ge(xf["xT_act"], J_D + B)
            act.wait_ge(xf["xT_dve"], J_D + B)
            with act.Fori(0, B) as b:
                for k in range(KC):
                    ins = nc.scalar.activation(XNT[:, k, rows_of(b)], XNT[:, k, rows_of(b)], ACT.Identity, bias=cround,
                                               scale=ax[:, 11:12])
                ins.then_inc(s["xq_act"], 1)
            with act.Fori(0, B) as b:
                for f in range(FC):
                    act.wait_ge(s["h_psum"], b * FC + f + 1)
                    nc.scalar.activation(Hall[:, f, rows_of(b)], PS[:, f % 4, :], ACT.Gelu, bias=w1f["bin"][:, f:f + 1]
                                         ).then_inc(s["h"], 1)
            act.wait_ge(s["scale"], 2)
            for b in range(B):
                for f in range(FC):
                    if b > 0:
                        if f < FC - 1:
                            act.wait_ge(s["used"], (b - 1) * (FC - 1) + f + 1)
                        else:
                            act.wait_ge(s["out_psum"], b * 2)
                    nc.scalar.activation(hT[:, f, :], Hall[:, f, b * T:(b + 1) * T], ACT.Identity, bias=cround,
                                         scale=ax[:, 15:16]).then_inc(s["hq_act"], 1)

        def pool_l1ffn(pool):
            for b in range(B):
                pool_norm(pool, N_D + b)
            for i in range(2):
                pool.wait_ge(sd["amax"], i + 1)
                nc.gpsimd.partition_all_reduce(ax[:, 9 + 4 * i:10 + 4 * i], ax[:, 8 + 4 * i:9 + 4 * i], P, RMAX
                                               ).then_inc(sd["amax_all"], 1)

        def dve_scale(v, i, ch):
            c = 8 + 4 * i
            nc.vector.tensor_reduce(ax[:, c:c + 1], ax[:, 4 * i:4 * i + 4], AX, ALU.max).then_inc(sd["amax"], 1)
            v.wait_ge(sd["amax_all"], i + 1)
            ch.link(nc.vector.tensor_scalar(ax[:, c + 2:c + 3], ax[:, c + 1:c + 2], 1e-8, 1.0 / 32767.0,
                                            ALU.max, ALU.mult))
            nc.vector.reciprocal(ax[:, c + 3:c + 4], ax[:, c + 2:c + 3]).then_inc(sd["scale"], 1)

        def dve_l1ffn(v, base):
            s = sd
            v.memset(scratch(1), 0.0).then_inc(s["h"], 4)
            v.wait_ge(s["win_psum"], 2)
            nc.vector.tensor_copy(win[:, FF:2 * FF], PS[:, 2:4, :].rearrange("p a n -> p (a n)")).then_inc(s["win_dve"], 1)
            ch = Chain(v, dve_step, base, 0, 3)
            with v.Fori(0, B) as b:
                ch = Chain(v, dve_step, base, b, 3)
                dve_norm(ch, N_D + b, lambda t: X[:, bass.ds(b * QT + t, 1), :].rearrange("p a c -> p (a c)"),
                         lambda t: xn[:, t, :]).then_inc(xf["xn_ready"], 1)
                v.wait_ge(xf["xn_ready"], b + (J_D + 1))
                ch.link(nc.vector.tensor_reduce(ax[:, bass.ds(b, 1)], xn, AXY, ALU.max, apply_absolute_value=True))
                v.wait_ge(xf["xT_psum"], XT(b + J_D))
                nc.vector.tensor_copy(XNT[:, 1, rows_of(b)], PS[:, 7, :]).then_inc(xf["xT_dve"], 1)
                ch.close()
            ch = Chain(v, dve_step, ch.after(B))
            dve_scale(v, 0, ch)
            base = ch.after()
            with v.Fori(0, B) as b:
                ch = Chain(v, dve_step, base, b, 1)
                v.wait_ge(s["xq_act"], b + 1)
                x = XNT[:, :, rows_of(b)]
                ch.link(nc.vector.tensor_scalar(x, x, ROUND, 32767.0, ALU.subtract, ALU.min))
                nc.vector.tensor_scalar(x, x, -32768.0, ax[:, 10:11], ALU.max, ALU.mult).then_inc(s["xq"], 1)
                ch.close()
            ch = Chain(v, dve_step, ch.after(B))
            ch.link(nc.vector.scalar_tensor_tensor(out=X, in0=row["b1out"].unsqueeze(1).to_broadcast([P, NT, C]),
                                                   scalar=tg[:, 5:6], in1=X, op0=ALU.mult, op1=ALU.add))
            base = ch.after()
            with v.Fori(0, B) as b:
                ch = Chain(v, dve_step, base, b, 1)
                v.wait_ge(s["h"], b * FC + (FC + 4))
                ch.link(nc.vector.tensor_reduce(ax[:, bass.ds(b + 4, 1)], Hall[:, :, rows_of(b)], AXY, ALU.max,
                                                apply_absolute_value=True))
                ch.close()
            ch = Chain(v, dve_step, ch.after(B))
            dve_scale(v, 1, ch)
            for b in range(B + 1):
                for f in range(FC + 1) if b < B else ():
                    if f < FC:
                        v.wait_ge(s["hq_act"], b * FC + f + 1)
                        mark = ch.mark(nc.vector.tensor_scalar(hT[:, f, :], hT[:, f, :], ROUND, 32767.0,
                                                               ALU.subtract, ALU.min))
                    if f > 0:
                        ch.wait(mark if f == FC else mark - 1)
                        nc.vector.tensor_scalar(hT[:, f - 1, :], hT[:, f - 1, :], -32768.0, ax[:, 14:15],
                                                ALU.max, ALU.mult).then_inc(s["hq"], 1)
                if b > 0:
                    m = b - 1
                    for i in range(2):
                        v.wait_ge(s["out_psum"], m * 2 + i + 1)
                        prod = PS[:, OUT1[m % 2] + 2 * i:OUT1[m % 2] + 2 * i + 2, 0:C]
                        xt = X[:, m * QT + 2 * i:m * QT + 2 * i + 2, :]
                        ch.link(nc.vector.scalar_tensor_tensor(out=xt, in0=prod, scalar=tg[:, 5:6], in1=xt,
                                                               op0=ALU.mult, op1=ALU.add))
            v.memset(scratch(1), 0.0).then_inc(done, 1)
            return ch.after()

        s2 = sems("l2a", "kv_psum kv q_psum q vb scores shifted probs pT_psum pT heads")
        w2 = W["w2a"]
        k2T = region("spare", 0, KC * B * TC).rearrange("p (c n) -> p c n", c=KC)
        v2b = region("spare", KC * B * TC, C + 1)
        v2 = region("Pr", 512, B * (C + 1)).rearrange("p (b e) -> p b e", b=B)
        p2, pT2 = region("Pr", 0, QT * TC), region("PT", 0, QT * TC)

        def pe_l2a(pe):
            s = s2
            pe.wait_ge(ld["w2a"], 16)
            pe.wait_ge(done, STAGE["l1ffn"])
            for c in range(KC):
                nc.tensor.matmul(PS[:, c, 0:B * TC], w2["wk"][:, c * P:(c + 1) * P], ctxT, start=True, stop=True
                                 ).then_inc(s["kv_psum"], 1)
            for b in range(B):
                nc.tensor.matmul(PS[:, 4 + b, 0:C], ctxdup[:, b].rearrange("p j n -> p (j n)"), w2["wv"],
                                 start=True, stop=True).then_inc(s["kv_psum"], 1)
            pe.wait_ge(s["kv"], KC + B)
            with pe.Fori(0, B) as b:
                pe_features(pe, b + J_E)
                for c in range(KC):
                    for k in range(KC):
                        ins = nc.tensor.matmul(PS[:, 6 + c, :], w2["wq"][:, k * C + c * P:k * C + (c + 1) * P],
                                               xT[:, k, :], start=k == 0, stop=k == KC - 1)
                    ins.then_inc(s["q_psum"], 1)
                pe.wait_ge(s["q"], b * KC + KC)
                for t in range(QT):
                    for c in range(KC):
                        ins = nc.tensor.matmul(PS[:, 0, t * TC:(t + 1) * TC], qT[:, c, t * P:(t + 1) * P],
                                               k2T[:, c, bass.ds(b * TC, TC)], start=c == 0, stop=c == KC - 1)
                ins.then_inc(s["scores"], 1)
                pe.wait_ge(s["probs"], b + 1)
                for i in range(2):
                    ins = nc.tensor.transpose(PS[:, 1, i * P:(i + 1) * P], p2[:, i * P:(i + 1) * P], ident)
                ins.then_inc(s["pT_psum"], 1)
                pe.wait_ge(s["pT"], b + 1)
                pe.wait_ge(s["vb"], b + 1)
                for t in range(QT):
                    half_rows = slice(TC * (t % 2), TC * (t % 2) + TC)
                    ins = nc.tensor.matmul(PS[:, 2 + t, 0:C + 1], pT2[half_rows, (t // 2) * P:(t // 2 + 1) * P],
                                           v2b[half_rows, :], start=True, stop=True)
                ins.then_inc(s["heads"], 1)

        def act_l2a(act):
            s = s2
            with act.Fori(0, B) as b:
                act.wait_ge(xf["xT_psum"], XT(b + J_E))
                plain_copy_act()
                act.wait_ge(s["shifted"], b + 1)
                nc.scalar.activation(p2, p2, ACT.Exp).then_inc(s["probs"], 1)
                act.wait_ge(s["pT_psum"], b + 1)
                nc.scalar.activation(pT2, PS[:, 1, 0:2 * P], ACT.Copy).then_inc(s["pT"], 1)

        def dve_l2a(v, base):
            s = s2
            for c in range(KC):
                v.wait_ge(s["kv_psum"], c + 1)
                nc.vector.tensor_scalar(k2T[:, c, :], PS[:, c, 0:B * TC], w2["bk"][:, c:c + 1], None, ALU.add
                                        ).then_inc(s["kv"], 1)
            for b in range(B):
                v.wait_ge(s["kv_psum"], KC + b + 1)
                nc.vector.tensor_tensor(v2[:, b, 0:C], PS[:, 4 + b, 0:C], row["b2v"], ALU.add)
                v.memset(v2[:, b, C:C + 1], 1.0).then_inc(s["kv"], 1)
            v.wait_ge(s["kv"], KC + B)

            def first_norm(b, ch):
                dve_norm(ch, N_E + b, lambda t: X[:, bass.ds(b * QT + t, 1), :].rearrange("p a c -> p (a c)"),
                         lambda t: xn[:, t, :]).then_inc(xf["xn_ready"], 1)

            def batch_row(b, ch, last=False):
                nc.vector.tensor_copy(v2b, v2[:, bass.ds(b, 1), :].rearrange("p b e -> p (b e)")).then_inc(s["vb"], 1)
                v.wait_ge(xf["xT_psum"], XT(b + J_E))
                plain_copy_dve()
                for c in range(KC):
                    v.wait_ge(s["q_psum"], b * KC + c + 1)
                    nc.vector.tensor_scalar(qT[:, c, :], PS[:, 6 + c, :], w2["bq"][:, c:c + 1], None, ALU.add
                                            ).then_inc(s["q"], 1)
                v.wait_ge(s["scores"], b + 1)
                sc = PS[:, 0, 0:QT * TC].rearrange("p (t n) -> p t n", t=QT)
                ch.link(nc.vector.tensor_reduce(nmax[:, 0:QT], sc, AX, ALU.max))
                nc.vector.tensor_tensor(p2.rearrange("p (t n) -> p t n", t=QT), sc,
                                        nmax[:, 0:QT].unsqueeze(2).to_broadcast([P, QT, TC]), ALU.subtract
                                        ).then_inc(s["shifted"], 1)
                if not last:
                    first_norm(b + 1, ch)
                v.wait_ge(s["heads"], b + 1)
                ch.link(nc.vector.reciprocal(rrec[:, 0:QT].unsqueeze(2), PS[:, 2:2 + QT, C:C + 1]))
                ch.link(nc.vector.tensor_scalar(rsum[:, 0:QT], rrec[:, 0:QT], tg[:, 2:3], None, ALU.mult))
                for t in range(QT):
                    xt = X[:, bass.ds(b * QT + t, 1), :].rearrange("p a c -> p (a c)")
                    ins = nc.vector.scalar_tensor_tensor(out=xt, in0=PS[:, 2 + t, 0:C], scalar=rsum[:, t:t + 1],
                                                         in1=xt, op0=ALU.mult, op1=ALU.add)
                ch.link(ins)
            ch = Chain(v, dve_step, base)
            first_norm(0, ch)
            base = ch.after()
            with v.Fori(0, B - 1) as b:
                ch = Chain(v, dve_step, base, b, 6)
                batch_row(b, ch)
                ch.close()
            ch = Chain(v, dve_step, ch.after(B - 1))
            batch_row(B - 1, ch, last=True)
            v.memset(scratch(1), 0.0).then_inc(done, 1)
            return ch.after()

        
        MOE_SEMS = " wa wb act_in dve_in hidden o_psum acc used extra"
        sr = sems("route", "lg lg_psum")
        s2m = sems("l2moe", "masks rank_psum diff ediff slots scattered x0 x1 xT_psum xT copied y0_stored y1_stored "
                   "gathered0 gathered1 first wa wb act_in hidden o_psum")
        s3m = sems("l3moe", "sig index chosen rank_psum slots scattered x0 x1 x2 w0 w1 w2 xT_psum xT copied "
                   "y0_stored y1_stored y2_stored gathered0 gathered1 gathered2 gathered3" + MOE_SEMS)
        gtile = hT.rearrange("p a n -> p (a n)")
        etile = region("Pr", 0, 4096)
        temps = region("spare", 0, 4096)

        xT_other = view("yT", "p (k n) -> p k n", k=KC)

        def logits2():
            return dict(keep=XN, xts=[(xT, xT_other)[b % 2] for b in range(B)], w=w2["wg"], e=E2, lg=lg2,
                        j0=J_F, n0=N_F, r0=0)

        def logits3():
            return dict(keep=XN3, xts=[XNT[:, :, b * T:(b + 1) * T] for b in range(B)], w=W["w3g"]["gw"], e=E3,
                        lg=lg3, j0=J_H, n0=N_H, r0=B)

        def pe_logits(pe, cfg):
            e = cfg["e"]

            def product(b):
                pe.wait_ge(xf["xT_act"], cfg["j0"] + b + 1)
                pe.wait_ge(xf["xT_dve"], cfg["j0"] + b + 1)
                if b >= 2:
                    pe.wait_ge(sr["lg"], cfg["r0"] + b - 1)
                for t in range(QT):
                    for k in range(KC):
                        ins = nc.tensor.matmul(PS[:, 4 + b % 2, t * e:(t + 1) * e], cfg["xts"][b][:, k, t * P:(t + 1) * P],
                                               cfg["w"][:, k * e:(k + 1) * e], start=k == 0, stop=k == KC - 1)
                ins.then_inc(sr["lg_psum"], 1)
            for b in range(B):
                pe.wait_ge(xf["xn_ready"], cfg["j0"] + b + 1)
                for ins in pe_to_features(cfg["keep"][:, b * QT:(b + 1) * QT, :], KC, (6, 2)[b % 2]):
                    ins.then_inc(xf["xT_psum"], 1)
                if b > 0:
                    product(b - 1)
            product(B - 1)

        def act_logits(act, cfg):
            for b in range(B):
                act.wait_ge(xf["xT_psum"], XT(cfg["j0"] + b))
                if b >= 2:
                    act.wait_ge(sr["lg_psum"], cfg["r0"] + b - 1)
                nc.scalar.activation(cfg["xts"][b][:, 0, :], PS[:, (6, 2)[b % 2], :], ACT.Copy).then_inc(xf["xT_act"], 1)

        def dve_logits(v, base, cfg):
            ch = Chain(v, dve_step, base)
            e = cfg["e"]
            for b in range(B + 1):
                if b < B:
                    dve_norm(ch, cfg["n0"] + b, lambda t: X[:, b * QT + t, :], lambda t: cfg["keep"][:, b * QT + t, :]
                             ).then_inc(xf["xn_ready"], 1)
                if b > 0:
                    m = b - 1
                    v.wait_ge(xf["xT_psum"], XT(cfg["j0"] + m))
                    if m >= 2:
                        v.wait_ge(sr["lg_psum"], cfg["r0"] + m - 1)
                    nc.vector.tensor_copy(cfg["xts"][m][:, 1, :], PS[:, (7, 3)[m % 2], :]).then_inc(xf["xT_dve"], 1)
                    if m >= 1:
                        copy_logits(v, cfg, m - 1)
            copy_logits(v, cfg, B - 1)
            v.wait_ge(sr["lg"], cfg["r0"] + B)
            return ch.after()

        def copy_logits(v, cfg, b):
            n = QT * cfg["e"]
            v.wait_ge(sr["lg_psum"], cfg["r0"] + b + 1)
            nc.vector.tensor_copy(cfg["lg"][:, b * n:(b + 1) * n], PS[:, 4 + b % 2, 0:n]).then_inc(sr["lg"], 1)

        def pool_logits(pool, cfg):
            for b in range(B):
                pool_norm(pool, cfg["n0"] + b)

        def dve_rank(ch, val, rank, e, n=NT):
            v = nc.vector
            m = val.shape[1]
            g4 = gtile[:, 0:m * e * e].rearrange("p (t i j) -> p t i j", i=e, j=e)
            e4 = etile[:, 0:m * e * e].rearrange("p (t i j) -> p t i j", i=e, j=e)
            own = val.unsqueeze(3).to_broadcast([P, m, e, e])
            other = val.unsqueeze(2).to_broadcast([P, m, e, e])
            low = view("lower", "p (i j) -> p i j", i=E3)[:, 0:e, 0:e].unsqueeze(1).to_broadcast([P, m, e, e])
            v.tensor_tensor(g4, other, own, ALU.is_gt)
            ch.link(v.tensor_tensor(e4, other, own, ALU.is_equal))
            ch.link(v.tensor_tensor(e4, e4, low, ALU.mult))
            ch.link(v.tensor_tensor(g4, g4, e4, ALU.add))
            ch.link(v.tensor_reduce(rank, g4, AX, ALU.add))

        tcut = [0]

        def temp(n):
            tcut[0] += n
            assert tcut[0] <= 4096 - NT * E3
            return temps[:, tcut[0] - n:tcut[0]]

        lg2 = region("PT", 0, NT * E2)
        lg3 = region("PT", 0, NT * E3)
        chosen3 = temps[:, 4096 - NT * E3:]

        def dve_route2(v, base):
            s, ch = s2m, Chain(v, dve_step, base)
            V = nc.vector
            tcut[0] = 0
            val = temp(NT * E2).rearrange("p (t e) -> p t e", e=E2)
            ch.link(V.tensor_copy(val, lg2.rearrange("p (t e) -> p t e", e=E2)))
            rank = temp(NT * E2).rearrange("p (t e) -> p t e", e=E2)
            dve_rank(ch, val, rank, E2)
            masks = temp(2 * NT * E2)
            mk = masks.rearrange("p (k t e) -> p k t e", k=2, e=E2)
            for k in range(2):
                ins = V.tensor_scalar(mk[:, k], rank, float(k), None, ALU.is_equal)
            ins.then_inc(s["masks"], 1)
            v.wait_ge(s["masks"], 1)
            tmp = temp(2 * NT * E2)
            t4 = tmp.rearrange("p (k t e) -> p k t e", k=2, e=E2)
            top2 = temp(2 * NT).rearrange("p (k t) -> p k t", k=2)
            ch.link(V.tensor_tensor(t4, mk, val.unsqueeze(1).to_broadcast([P, 2, NT, E2]), ALU.mult))
            ch.link(V.tensor_reduce(top2, t4, AX, ALU.add))
            diff, ed, pk = temp(NT), temp(NT), temp(2 * NT).rearrange("p (k t) -> p k t", k=2)
            V.tensor_tensor(diff, top2[:, 1], top2[:, 0], ALU.subtract).then_inc(s["diff"], 1)
            v.wait_ge(s["ediff"], 1)
            den = temp(NT)
            ch.link(V.tensor_scalar(den, diff, 1.0, None, ALU.add))
            ch.link(V.reciprocal(pk[:, 0], den))
            ch.link(V.tensor_tensor(pk[:, 1], pk[:, 0], diff, ALU.mult))
            v.wait_ge(s["rank_psum"], 1)
            nseg = 2 * NT
            buf = [temp(nseg * E2), temp(nseg * E2)]
            tot = PS[:, 1, 0:nseg * E2]
            ch.link(V.tensor_copy(buf[0], tot))
            step, cur = 1, 0
            while step < nseg:
                a, z = buf[cur], buf[1 - cur]
                V.tensor_copy(z[:, 0:step * E2], a[:, 0:step * E2])
                ch.link(V.tensor_tensor(z[:, step * E2:], a[:, step * E2:], a[:, 0:(nseg - step) * E2], ALU.add))
                step, cur = 2 * step, 1 - cur
            pos = buf[cur]
            ch.link(V.tensor_tensor(pos, pos, tot, ALU.subtract))
            ch.link(V.tensor_tensor(pos, pos, PS[:, 0, 0:nseg * E2], ALU.add))
            m4 = masks.rearrange("p (s e) -> p s e", e=E2)
            first = temp(E2)
            for e in range(E2):
                V.memset(first[:, e:e + 1], float(e * CAP - 1))
            spare = temp(nseg)
            ch.link(V.tensor_copy(spare, spare_u[:, :]))
            ch.link(V.tensor_tensor(pos, pos, masks, ALU.mult))
            place, slot, picked = temp(nseg), temp(nseg), temp(nseg * E2)
            ch.link(V.tensor_reduce(place, pos.rearrange("p (s e) -> p s e", e=E2), AX, ALU.add))
            picked3 = picked.rearrange("p (s e) -> p s e", e=E2)
            ch.link(V.tensor_tensor(picked3, m4, first.unsqueeze(1).to_broadcast([P, nseg, E2]), ALU.mult))
            ch.link(V.tensor_reduce(slot, picked3, AX, ALU.add))
            ch.link(V.tensor_tensor(slot, slot, place, ALU.add))
            ch.link(V.tensor_scalar(place, place, float(CAP), None, ALU.is_le))
            ch.link(V.tensor_tensor(slot, slot, spare, ALU.subtract))
            ch.link(V.tensor_tensor(slot, slot, place, ALU.mult))
            ch.link(V.tensor_tensor(slot, slot, spare, ALU.add))
            V.tensor_copy(slot_of2[:, :], slot).then_inc(s["slots"], 1)
            ch.link(V.tensor_scalar(spare, slot, float(S2), None, ALU.min))
            V.tensor_copy(row_of2[:, :], spare).then_inc(s["slots"], 1)
            w2c = wcomb[:, 0:nseg]
            ch.link(V.tensor_tensor(w2c, pk.rearrange("p k t -> p (k t)"), place, ALU.mult))
            ch.link(V.tensor_scalar(w2c, w2c, tg[:, 6:7], None, ALU.mult))
            for name, n in (("copied", 1), ("o_psum", 1)):
                V.memset(scratch(1), 0.0).then_inc(s[name], n)
            V.memset(scratch(1), 0.0).then_inc(done, 1)
            return ch.after()

        def dve_route3(v, base):
            s, ch = s3m, Chain(v, dve_step, base)
            V = nc.vector
            tcut[0] = 0
            ng, eg = 4, E3 // 4
            score = temp(NT * E3).rearrange("p (t e) -> p t e", e=E3)
            V.memset(scratch(1), 0.0).then_inc(s["extra"], 1)
            v.wait_ge(s["sig"], 1)
            ch.link(V.tensor_copy(score, lg3.rearrange("p (t e) -> p t e", e=E3)))
            sfc = temp(NT * E3).rearrange("p (t e) -> p t e", e=E3)
            ch.link(V.tensor_tensor(sfc, score, gbias.unsqueeze(1).to_broadcast([P, NT, E3]), ALU.add))
            grp = sfc.rearrange("p t (g e) -> p (t g) e", e=eg)
            pairs = [(i, j) for i in range(eg) for j in range(i + 1, eg)]
            sums = temp(NT * ng * len(pairs)).rearrange("p (n q) -> p n q", q=len(pairs))
            for q, (i, j) in enumerate(pairs):
                ins = V.tensor_tensor(sums[:, :, q], grp[:, :, i], grp[:, :, j], ALU.add)
            ch.link(ins)
            gsc = temp(NT * ng)
            ch.link(V.tensor_reduce(gsc, sums, AX, ALU.max))
            grank = temp(NT * ng)
            dve_rank(ch, gsc.rearrange("p (t g) -> p t g", g=ng), grank.rearrange("p (t g) -> p t g", g=ng), ng)
            ch.link(V.tensor_scalar(grank, grank, float(2), None, ALU.is_lt))
            ch.link(V.tensor_tensor(grp, grp, grank.unsqueeze(2).to_broadcast([P, NT * ng, eg]), ALU.mult))
            rank = temp(NT * E3).rearrange("p (t e) -> p t e", e=E3)
            dve_rank(ch, sfc, rank, E3)
            ch3 = chosen3.rearrange("p (t e) -> p t e", e=E3)
            V.tensor_scalar(ch3, rank, float(TOPK3), None, ALU.is_lt).then_inc(s["chosen"], 1)
            v.wait_ge(s["chosen"], 1)
            onehot, picked = (gtile[:, i * TOPK3 * NT * E3:(i + 1) * TOPK3 * NT * E3] for i in range(2))
            onehot, picked = (z.rearrange("p (k t e) -> p k t e", k=TOPK3, e=E3) for z in (onehot, picked))
            for k in range(TOPK3):
                ins = V.tensor_scalar(onehot[:, k], rank, float(k), None, ALU.is_equal)
            ch.link(ins)
            ch.link(V.tensor_tensor(picked, onehot, score.unsqueeze(1).to_broadcast([P, TOPK3, NT, E3]), ALU.mult))
            wk = wcomb[:, 0:TOPK3 * NT].rearrange("p (k t) -> p k t", k=TOPK3)
            ch.link(V.tensor_reduce(wk, picked, AX, ALU.add))
            tot = temp(NT)
            ch.link(V.tensor_reduce(tot, wk.rearrange("p k t -> p t k"), AX, ALU.add))
            ch.link(V.tensor_scalar(tot, tot, 1e-20, None, ALU.add))
            ch.link(V.reciprocal(tot, tot))
            ch.link(V.tensor_scalar(tot, tot, tg[:, 7:8], None, ALU.mult))
            ch.link(V.tensor_tensor(wk, wk, tot.unsqueeze(1).to_broadcast([P, TOPK3, NT]), ALU.mult))
            v.wait_ge(s["rank_psum"], 1)
            buf = [temp(NT * E3), temp(NT * E3)]
            whole = PS[:, 1, 0:NT * E3]
            ch.link(V.tensor_copy(buf[0], whole))
            step, cur = 1, 0
            while step < NT:
                a, z = buf[cur], buf[1 - cur]
                V.tensor_copy(z[:, 0:step * E3], a[:, 0:step * E3])
                ch.link(V.tensor_tensor(z[:, step * E3:], a[:, step * E3:], a[:, 0:(NT - step) * E3], ALU.add))
                step, cur = 2 * step, 1 - cur
            pos, count = buf[cur], temp(E3)
            ch.link(V.tensor_copy(count, pos[:, (NT - 1) * E3:]))
            ch.link(V.tensor_tensor(pos, pos, whole, ALU.subtract))
            ch.link(V.tensor_tensor(pos, pos, PS[:, 0, 0:NT * E3], ALU.add))
            slots = ST3 * P
            nb = temp(E3)
            ch.link(V.tensor_scalar(nb, count, 1.0 / slots, (slots - 1) / (2.0 * slots), ALU.mult, ALU.add))
            ch.link(V.tensor_scalar(nb, nb, ROUND, None, ALU.add))
            ch.link(V.tensor_scalar(nb, nb, ROUND, None, ALU.subtract))
            ends = [temp(E3), temp(E3)]
            ch.link(V.tensor_copy(ends[0], nb))
            step, cur = 1, 0
            while step < E3:
                a, z = ends[cur], ends[1 - cur]
                V.tensor_copy(z[:, 0:step], a[:, 0:step])
                ch.link(V.tensor_tensor(z[:, step:], a[:, step:], a[:, 0:E3 - step], ALU.add))
                step, cur = 2 * step, 1 - cur
            end = ends[cur]
            ch.link(V.tensor_tensor(nb, end, nb, ALU.subtract))
            ch.link(V.tensor_scalar(nb, nb, float(slots), -1.0, ALU.mult, ALU.add))
            pos3 = pos.rearrange("p (t e) -> p t e", e=E3)
            ch.link(V.tensor_tensor(pos3, pos3, nb.unsqueeze(1).to_broadcast([P, NT, E3]), ALU.add))
            ch.link(V.tensor_tensor(picked, onehot, pos3.unsqueeze(1).to_broadcast([P, TOPK3, NT, E3]), ALU.mult))
            slot = temp(TOPK3 * NT)
            ch.link(V.tensor_reduce(slot.rearrange("p (k t) -> p k t", k=TOPK3), picked, AX, ALU.add))
            V.tensor_copy(slot_of3[:, :], slot).then_inc(s["slots"], 1)
            batch, lane, row_ = temp(NB3), temp(1), temp(NB3)
            V.tensor_copy(lane, lane_u[:, :])
            ch.link(V.tensor_copy(batch, batch_u[:, :]))
            over = etile[:, 0:NB3 * E3].rearrange("p (j e) -> p j e", e=E3)
            ch.link(V.tensor_tensor(over, batch.unsqueeze(2).to_broadcast([P, NB3, E3]),
                                    end.unsqueeze(1).to_broadcast([P, NB3, E3]), ALU.is_ge))
            ch.link(V.tensor_reduce(row_, over, AX, ALU.add))
            ch.link(V.tensor_scalar(row_, row_, float(E3 - 1), float(P), ALU.min, ALU.mult))
            ch.link(V.tensor_scalar(row_, row_, lane[:, 0:1], None, ALU.add))
            V.tensor_copy(weight_row3[:, :], row_).then_inc(s["slots"], 1)
            V.memset(scratch(1), 0.0).then_inc(s["copied"], 3)
            V.memset(scratch(1), 0.0).then_inc(s["acc"], 4)
            V.memset(scratch(1), 0.0).then_inc(s["used"], 1)
            V.memset(scratch(1), 0.0).then_inc(done, 1)
            return ch.after()

        ebuf2 = [region("spare", 0, W2X), region("Pr", 0, W2X)]
        ebuf3 = [region("spare", 0, W3X), region("Pr", 0, W3X)]
        sgate = [region("Pr", W3X + c * T, T) for c in range(3)]
        ARRIVED = ("wa", "wb")

        def pe_down(pe, s, it, w2off, buf, chunks_of, h0):
            for t in range(QT):
                for c, n in enumerate(chunks_of):
                    if t == 0:
                        pe.wait_ge(s["hidden"], it * len(chunks_of) + (h0 + c + 1))
                    if c == 0:
                        pe.wait_ge(s["acc"], it * QT + t + 1)
                    ins = nc.tensor.matmul(PS[:, 4 + t, 0:C], hT[0:n, c, t * P:(t + 1) * P],
                                           buf[0:n, w2off + c * C:w2off + (c + 1) * C],
                                           start=c == 0, stop=c == len(chunks_of) - 1)
                ins.then_inc(s["o_psum"], 1)
            nc.tensor.matmul(PS[0:1, 3, 0:1], ident[:, 0:1], ident[:, 0:1], start=True, stop=True
                             ).then_inc(s["used"], 1)

        def dve_accumulate(v, s, it, b, o0):
            for t in range(QT):
                v.wait_ge(s["o_psum"], it * QT + (o0 + t + 1))
                v.wait_ge(s["acc"], it * QT + t + 1)
                xt = X[:, bass.ds(b * QT + t, 1), :].rearrange("p a c -> p (a c)")
                nc.vector.scalar_tensor_tensor(out=xt, in0=PS[:, 4 + t, 0:C],
                                               scalar=tg[:, 7:8],
                                               in1=xt, op0=ALU.mult, op1=ALU.add).then_inc(s["acc"], 1)

        GC = GT2[0] * C
        xs = [view("V", "p (t c) -> p t c", g * GC, GT2[g] * C, c=C) for g in range(2)]
        xsT = [view("V", "p (k n) -> p k n", 2 * GC + g * GC, KC * GT2[g] * P, k=KC) for g in range(2)]
        ys = [view("kv", "p (t c) -> p t c", KV3_OFF + g * GC, GT2[g] * C, c=C) for g in range(2)]
        yk = [view("V", "p (t c) -> p t c", 0, NT * C, c=C),
              view("qT", "p (t c) -> p t c", 0, NT * C, c=C)]

        def slot_rows(dram, e, g):
            first, n = e * CAP + g * GT2[0] * P, GT2[g] * P
            return dram[bass.ds(first, n), :].rearrange("(t p) c -> p t c", p=P)

        def sp_moe2(sp):
            s = s2m
            for i in range(2):
                sp.dma_start(ebuf2[i], e2_in[i, :, :]).then_inc((s["wa"], s["wb"])[i], 16)
            sp.wait_ge(s["scattered"], 2 * NT * 16)
            for g in range(2):
                sp.dma_start(xs[g], slot_rows(slots2, 0, g)).then_inc(s[f"x{g}"], 16)

            def rows(e):
                for g in range(2):
                    sp.wait_ge(s["xT_psum"], e * 2 + (g - 1))
                    sp.dma_start(xs[g], slot_rows(slots2, e, g)).then_inc(s[f"x{g}"], 16)
            with sp.Fori(0, E2 // 2 - 1) as ep:
                for i in range(2):
                    rows(ep * 2 + (i + 1))
                    sp.wait_ge(s["o_psum"], ep * 10 + (5 * i + 6))
                    sp.dma_start(ebuf2[i], e2_in[bass.ds(ep * 2 + (i + 2), 1), :, :].rearrange("e p n -> p (e n)")
                                 ).then_inc((s["wa"], s["wb"])[i], 16)
            rows(E2 - 1)

        def pe_moe2(pe):
            s = s2m

            def transposes(e, g, first=False):
                pe.wait_ge(s[f"x{g}"], e * 16 + 16)
                if not first:
                    pe.wait_ge(s["xT"], e * 2 + g)
                for k in range(KC):
                    for t in range(GT2[g]):
                        ins = nc.tensor.transpose(PS[:, (3, 7)[k], t * P:(t + 1) * P],
                                                  xs[g][:, t, k * P:(k + 1) * P], ident)
                ins.then_inc(s["xT_psum"], 1)

            def expert(e, i, last=False):
                for g in range(2):
                    n, N = e * 2 + g, GT2[g] * P
                    if g == 0:
                        pe.wait_ge((s["wa"], s["wb"])[i], (e - i) * 8 + 16)
                    pe.wait_ge(s["xT"], n + 1)
                    for f in range(FC):
                        if f >= 3:
                            pe.wait_ge(s["hidden"], n * FC + f - 2)
                        for k in range(KC):
                            ins = nc.tensor.matmul(PS[:, f % 3, 0:N], ebuf2[i][:, k * FF + f * P:k * FF + (f + 1) * P],
                                                   xsT[g][:, k, :], start=k == 0, stop=k == KC - 1)
                        ins.then_inc(s["act_in"], 1)
                    if g == 0:
                        transposes(e, 1)
                    elif not last:
                        transposes(e + 1, 0)
                    for t in range(GT2[g]):
                        for c in range(FC):
                            if t == 0:
                                pe.wait_ge(s["hidden"], n * FC + c + 1)
                            if t == 0 and c == 0:
                                pe.wait_ge(s["copied"], e * 5 + (g * 3 + 1))
                            ins = nc.tensor.matmul(PS[:, 4 + t, 0:C], hT[:, c, t * P:(t + 1) * P],
                                                   ebuf2[i][:, 2 * FF + c * C:2 * FF + (c + 1) * C],
                                                   start=c == 0, stop=c == FC - 1)
                        ins.then_inc(s["o_psum"], 1)
            transposes(0, 0, first=True)
            with pe.Fori(0, E2 // 2 - 1) as ep:
                for i in range(2):
                    expert(ep * 2 + i, i)
            expert(E2 - 2, 0)
            expert(E2 - 1, 1, last=True)

        def act_moe2(act):
            s = s2m
            act.wait_ge(done, STAGE["route2"])
            with act.Fori(0, E2) as e:
                for g in range(2):
                    act.wait_ge(s["o_psum"], e * 5 + (3 * g + 1))
                    for f in range(FC):
                        act.wait_ge(s["act_in"], e * 2 * FC + (g * FC + f + 1))
                        nc.scalar.activation(hT[:, f, 0:GT2[g] * P], PS[:, f % 3, 0:GT2[g] * P], ACT.Gelu
                                             ).then_inc(s["hidden"], 1)

        def dve_moe2(v):
            s = s2m

            def rows_copy(e, g):
                v.wait_ge(s["xT_psum"], e * 2 + (g + 1))
                for k in range(KC):
                    ins = nc.vector.tensor_copy(xsT[g][:, k, :], PS[:, (3, 7)[k], 0:GT2[g] * P])
                ins.then_inc(s["xT"], 1)

            def outputs(e, g, first):
                if not first:
                    v.wait_ge(s[f"y{g}_stored"], e * 16)
                for t in range(GT2[g]):
                    v.wait_ge(s["o_psum"], e * 5 + (3 * g + t + 2))
                    nc.vector.tensor_copy(ys[g][:, t, :], PS[:, 4 + t, 0:C]).then_inc(s["copied"], 1)

            def expert(e, first=False, last=False):
                rows_copy(e, 1)
                outputs(e, 0, first)
                if not last:
                    rows_copy(e + 1, 0)
                outputs(e, 1, first)
            rows_copy(0, 0)
            expert(0, first=True)
            with v.Fori(1, E2 - 1) as e:
                expert(e)
            expert(E2 - 1, last=True)
            for g in range(2):
                v.wait_ge(s[f"y{g}_stored"], E2 * 16)

        def dve_combine2(v):
            s = s2m
            for q in range(2):
                v.wait_ge(s[f"gathered{q}"], NT * 16)
                for k in range(2):
                    for t in range(q * NT // 2, (q + 1) * NT // 2):
                        if k == 1 and t % (NT // 2) == 0:
                            v.wait_ge(s["first"], 2 * q + 1)
                        ins = nc.vector.scalar_tensor_tensor(out=X[:, t, :], in0=yk[k][:, t, :],
                                                             scalar=wcomb[:, k * NT + t:k * NT + t + 1],
                                                             in1=X[:, t, :], op0=ALU.mult, op1=ALU.add)
                    ins.then_inc(s["first"], 1)
            v.wait_ge(s["first"], 4)
            v.memset(scratch(1), 0.0).then_inc(done, 1)

        def pool_scatter2(pool):
            s = s2m
            pool.wait_ge(ld["zeroed"], 48)
            pool.wait_ge(xf["xn_ready"], J_F + B)
            pool.wait_ge(s["slots"], 1)
            for k in range(2):
                for t in range(NT):
                    at_ = bass.IndirectOffsetOnAxis(ap=slot_of2[:, k * NT + t:k * NT + t + 1], axis=0)
                    nc.gpsimd.indirect_dma_start(out=slots2, out_offset=at_, in_=XN[:, t, :], in_offset=None
                                                 ).then_inc(s["scattered"], 16)

        def pool_moe2(pool):
            s = s2m
            with pool.Fori(0, E2) as e:
                for g in range(2):
                    pool.wait_ge(s["copied"], e * 5 + (1 + (3, 5)[g]))
                    pool.dma_start(slot_rows(yslots2, e, g), ys[g]).then_inc(s[f"y{g}_stored"], 16)
            for g in range(2):
                pool.wait_ge(s[f"y{g}_stored"], E2 * 16)
            pool.wait_ge(s["slots"], 2)
            pool_norm(pool, N_CTX)
            for q in range(2):
                for k in range(2):
                    for t in range(q * NT // 2, (q + 1) * NT // 2):
                        at_ = bass.IndirectOffsetOnAxis(ap=row_of2[:, k * NT + t:k * NT + t + 1], axis=0)
                        nc.gpsimd.indirect_dma_start(out=yk[k][:, t, :], out_offset=None, in_=yslots2, in_offset=at_
                                                     ).then_inc(s[f"gathered{q}"], 16)

        def sp_shared3(sp):
            for i in range(2):
                sp.dma_start(ebuf3[i], e3_in[E3 + i, :, :]).then_inc((s3m["wa"], s3m["wb"])[i], 16)

        def pe_shared3(pe, i):
            s, h0 = s3m, i * NB3 * 3
            pe.wait_ge((s["wa"], s["wb"])[i], 16)
            if i:
                pe.wait_ge(s["copied"], NB3 + 3)
            with pe.Fori(0, B) as b:
                it = b + i * B
                for j in range(6):
                    c, up = j // 2, j % 2
                    n = IC3[c]
                    if j == 3:
                        pe.wait_ge(s["extra"], it * 3 + (h0 + 2))
                    if j >= 4:
                        pe.wait_ge(s["hidden"], it * 3 + (h0 + j - 3))
                    for k in range(KC):
                        off = up * 2 * I3 + k * I3 + c * P
                        ins = nc.tensor.matmul(PS[0:n, j % 3, :], ebuf3[i][:, off:off + n],
                                               XNT[:, k, rows_of(b)], start=k == 0, stop=k == KC - 1)
                    ins.then_inc((s["act_in"], s["dve_in"])[up], 1)
                pe_down(pe, s, it, 4 * I3, ebuf3[i], IC3, h0)

        def act_shared3(act, i):
            s, h0 = s3m, i * NB3 * 3
            act.wait_ge(done, STAGE["route3"])
            with act.Fori(i * B, (i + 1) * B) as it:
                for c, n in enumerate(IC3):
                    act.wait_ge(s["act_in"], it * 3 + (h0 + c + 1))
                    nc.scalar.activation(sgate[c][0:n, :], PS[0:n, (2 * c) % 3, :], ACT.Silu).then_inc(s["extra"], 1)

        def dve_shared3(v, i):
            s, h0 = s3m, i * NB3 * 3
            with v.Fori(0, B) as b:
                it = b + i * B
                v.wait_ge(s["used"], it + 1)
                for c, n in enumerate(IC3):
                    v.wait_ge(s["dve_in"], it * 3 + (h0 + c + 1))
                    v.wait_ge(s["extra"], it * 3 + (h0 + c + 2))
                    nc.vector.tensor_tensor(hT[0:n, c, :], sgate[c][0:n, :], PS[0:n, (2 * c + 1) % 3, :], ALU.mult
                                            ).then_inc(s["hidden"], 1)
                dve_accumulate(v, s, it, b, i * NB3)

        SH, SO = B * 3, B * QT
        BN = ST3 * P
        off3 = [0]

        def cut3(n):
            off3[0] += n
            return region("kv", off3[0] - n, n)
        XN3 = cut3(NT * C).rearrange("p (t c) -> p t c", c=C)
        wbuf3 = [cut3(W3X) for _ in range(3)]
        xs3 = [cut3(ST3 * C).rearrange("p (t c) -> p t c", c=C) for _ in range(3)]
        xsT3 = [cut3(KC * BN).rearrange("p (k n) -> p k n", k=KC) for _ in range(3)]
        ys3 = [cut3(ST3 * C) for _ in range(3)]
        hid3 = [cut3(BN) for _ in range(3)]
        assert off3[0] <= KV3_OFF - width("w3g")
        gate3 = [region("ctx", i * BN, BN) for i in range(3)]
        yk3 = region("kv", 0, TOPK3 * NT * C).rearrange("p (k t c) -> p k t c", k=TOPK3, c=C)

        def batch_rows(dram, j):
            return dram[bass.ds(j * BN, BN), :].rearrange("(t p) c -> p t c", p=P)

        def sp_moe3(sp):
            s = s3m

            def rows(j, i):
                sp.dma_start(xs3[i], batch_rows(slots3, j)).then_inc(s[f"x{i}"], 16)
            sp.wait_ge(s["scattered"], TOPK3 * NT * 16)
            for i in range(3):
                rows(i, i)
            with sp.Fori(1, NB3 // 3) as jj:
                for i in range(3):
                    sp.wait_ge(s["xT_psum"], jj * 3 + (i - 2))
                    rows(jj * 3 + i, i)

        def pe_moe3(pe):
            s = s3m
            pe.wait_ge(s["acc"], 4 + NT)

            def transposes(jj, i):
                pe.wait_ge(s[f"x{i}"], jj * 16 + 16)
                for k in range(KC):
                    for t in range(ST3):
                        ins = nc.tensor.transpose(PS[:, 6, (k * ST3 + t) * P:(k * ST3 + t + 1) * P],
                                                  xs3[i][:, t, k * P:(k + 1) * P], ident)
                ins.then_inc(s["xT_psum"], 1)

            def batch(jj, i, last=False):
                j = jj * 3 + i
                pe.wait_ge(s[f"w{i}"], jj * 16 + 16)
                pe.wait_ge(s["xT"], j + 1)
                for c, n in enumerate(IC3):
                    pe.wait_ge(s["hidden"], j * 3 + (SH + c - 2))
                    for up in range(2):
                        for k in range(KC):
                            off = up * 2 * I3 + k * I3 + c * P
                            ins = nc.tensor.matmul(PS[0:n, 2 * c + up, 0:BN], wbuf3[i][:, off:off + n],
                                                   xsT3[i][:, k, :], start=k == 0, stop=k == KC - 1)
                        ins.then_inc((s["act_in"], s["dve_in"])[up], 1)
                if i < 2:
                    transposes(jj, i + 1)
                elif not last:
                    transposes(jj + 1, 0)
                pe.wait_ge(s["copied"], j + 3)
                for t in range(ST3):
                    for c, n in enumerate(IC3):
                        if t == 0:
                            pe.wait_ge(s["hidden"], j * 3 + (SH + c + 1))
                        ins = nc.tensor.matmul(PS[:, 7, t * C:(t + 1) * C], hid3[c][0:n, t * P:(t + 1) * P],
                                               wbuf3[i][0:n, 4 * I3 + c * C:4 * I3 + (c + 1) * C],
                                               start=c == 0, stop=c == len(IC3) - 1)
                ins.then_inc(s["o_psum"], 1)
            transposes(0, 0)
            with pe.Fori(0, NB3 // 3 - 1) as jj:
                for i in range(3):
                    batch(jj, i)
            for i in range(3):
                batch(NB3 // 3 - 1, i, last=True)

        def act_moe3(act):
            s = s3m
            with act.Fori(0, NB3) as j:
                for c, n in enumerate(IC3):
                    act.wait_ge(s["hidden"], j * 3 + (SH + c - 2))
                    act.wait_ge(s["act_in"], j * 3 + (SH + c + 1))
                    nc.scalar.activation(gate3[c][0:n, :], PS[0:n, 2 * c, 0:BN], ACT.Silu).then_inc(s["extra"], 1)

        def dve_moe3(v):
            s = s3m

            def rows_copy(j, i):
                v.wait_ge(s["xT_psum"], j + 1)
                nc.vector.tensor_copy(xsT3[i].rearrange("p k n -> p (k n)"), PS[:, 6, :]).then_inc(s["xT"], 1)

            def batch(jj, i, first=False, last=False):
                j = jj * 3 + i
                for c, n in enumerate(IC3):
                    v.wait_ge(s["dve_in"], j * 3 + (SH + c + 1))
                    v.wait_ge(s["extra"], j * 3 + (SH + c + 2))
                    nc.vector.tensor_tensor(hid3[c][0:n, :], gate3[c][0:n, :], PS[0:n, 2 * c + 1, 0:BN], ALU.mult
                                            ).then_inc(s["hidden"], 1)
                if not (last and i == 2):
                    rows_copy(j + 1, (i + 1) % 3)
                if not first:
                    v.wait_ge(s[f"y{i}_stored"], jj * 16)
                v.wait_ge(s["o_psum"], j + (SO + 1))
                nc.vector.tensor_copy(ys3[i], PS[:, 7, :]).then_inc(s["copied"], 1)
            rows_copy(0, 0)
            for i in range(3):
                batch(0, i, first=True)
            with v.Fori(1, NB3 // 3 - 1) as jj:
                for i in range(3):
                    batch(jj, i)
            for i in range(3):
                batch(NB3 // 3 - 1, i, last=True)

        def dve_combine3(v):
            s = s3m
            base = 4 + 2 * NT
            for q in range(B):
                v.wait_ge(s[f"gathered{q}"], TOPK3 * QT * 16)
                for k in range(TOPK3):
                    for t in range(q * QT, (q + 1) * QT):
                        if k > 0 and t % QT == 0:
                            v.wait_ge(s["acc"], base + q * TOPK3 + k)
                        ins = nc.vector.scalar_tensor_tensor(out=X[:, t, :], in0=yk3[:, k, t, :],
                                                             scalar=wcomb[:, k * NT + t:k * NT + t + 1],
                                                             in1=X[:, t, :], op0=ALU.mult, op1=ALU.add)
                    ins.then_inc(s["acc"], 1)

        carrier3 = scratch(1)

        def pool_moe3(pool):
            s = s3m

            def weights(j, i):
                nc.gpsimd.tensor_copy(batch_row3[:, i:i + 1], weight_row3[:, bass.ds(j, 1)]).then_inc(s["index"], 1)
                pool.wait_ge(s["index"], j + 1)
                nc.gpsimd.tensor_tensor(carrier3, ones[:, 0:1], ones[:, 0:1], ALU.mult)
                at_ = bass.IndirectOffsetOnAxis(ap=batch_row3[:, i:i + 1], axis=0)
                nc.gpsimd.indirect_dma_start(out=wbuf3[i], out_offset=None, in_=e3_in.rearrange("e p n -> (e p) n"),
                                             in_offset=at_).then_inc(s[f"w{i}"], 16)

            def store(j, i):
                pool.wait_ge(s["copied"], j + 4)
                pool.dma_start(batch_rows(yslots3, j), ys3[i].rearrange("p (t c) -> p t c", c=C)
                               ).then_inc(s[f"y{i}_stored"], 16)
            pool.wait_ge(s["slots"], 2)
            for i in range(3):
                weights(i, i)
            pool.wait_ge(ld["zeroed"], 48)
            pool.wait_ge(xf["xn_ready"], J_H + B)
            for k in range(TOPK3):
                for t in range(NT):
                    at_ = bass.IndirectOffsetOnAxis(ap=slot_of3[:, k * NT + t:k * NT + t + 1], axis=0)
                    nc.gpsimd.indirect_dma_start(out=slots3, out_offset=at_, in_=XN3[:, t, :], in_offset=None
                                                 ).then_inc(s["scattered"], 16)
            with pool.Fori(1, NB3 // 3) as jj:
                for i in range(3):
                    store(jj * 3 + (i - 3), i)
                    weights(jj * 3 + i, i)
            for i in range(3):
                store(NB3 - 3 + i, i)
            for i in range(3):
                pool.wait_ge(s[f"y{i}_stored"], NB3 // 3 * 16)
            for q in range(B):
                for k in range(TOPK3):
                    for t in range(q * QT, (q + 1) * QT):
                        at_ = bass.IndirectOffsetOnAxis(ap=slot_of3[:, k * NT + t:k * NT + t + 1], axis=0)
                        nc.gpsimd.indirect_dma_start(out=yk3[:, k, t, :], out_offset=None, in_=yslots3, in_offset=at_
                                                     ).then_inc(s[f"gathered{q}"], 16)

        s3k = sems("kv3", "tok xT_psum xT kv_psum kv_ready")
        ca, cd = scaled_copies(w3["xg"], w3["xb"], w3["yg"], w3["yb"])
        c3s = dict(qm=QM3, engines=evac_engines("d"), wq=w3["wq"], wk=w3["wk"], wv=w3["wv"], xq=xT, xkv=xT2, d=D3, causal=False,
                  V=V3, y=y3, bq=None, bk=None, bv=None, scale=D3 ** -0.5, copy_x_act=ca, copy_x_dve=cd)
        c3o = dict(nch=4, y=y3, wo=w3["li1"])
        ca, cd = scaled_copies(w3["g3"], w3["b3"])
        c3f = dict(w1=w3["li2"], w2=w3["li3"], b1=w3["bh"], copy_x_act=ca, copy_x_dve=cd)
        ca, cd = scaled_copies(w3b["xg"], w3b["xb"])
        c3c = dict(kv=kv3, norm=True, wq=w3b["wq"], bq=None, scale=D3 ** -0.5, y=y3, add=False,
                  copy_x_act=ca, copy_x_dve=cd)
        c3p = dict(nch=4, y=y3, wo=w3b["li1"])
        ca, cd = scaled_copies(w3b["g3"], w3b["b3"])
        c3g = dict(w1=w3b["li2"], w2=w3b["li3"], b1=w3b["bh"], copy_x_act=ca, copy_x_dve=cd)
        ctok = region("ctx", 0, B * CC).rearrange("p (b c) -> p b c", b=B)
        ctx3 = xT.rearrange("p k n -> p (k n)")[:, 0:B * 2 * TC]

        def pe_context3(pe):
            pe.wait_ge(ld["w3b"], 16)
            pe.wait_ge(s3k["tok"], 1)
            for b in range(B):
                ins = nc.tensor.transpose(PS[:, 0, b * P:(b + 1) * P], xn[:, b, 0:CC], ident)
            ins.then_inc(s3k["xT_psum"], 1)
            pe_context(pe, s3k, kv3, w3b["wk"], w3b["wv"], ctx3.rearrange("p (b j n) -> p b j n", b=B, j=2)[:, :, 0, :],
                       lambda b: ctx3[:, b * P:(b + 1) * P], lambda: pe.wait_ge(s3k["xT"], 1))
            pe.wait_ge(s3k["kv_ready"], kv_count(kv3))

        def dve_context3(v, base):
            ch = Chain(v, dve_step, base)
            v.wait_ge(ld["ctx3"], 16)
            dve_norm(ch, N_CTX, lambda t: ctok[:, t, :], lambda t: xn[:, t, 0:CC]).then_inc(s3k["tok"], 1)
            v.wait_ge(s3k["xT_psum"], 1)
            v.wait_ge(ld["w3b"], 16)
            nc.vector.tensor_scalar(ctx3, PS[:, 0, :], w3b["yg"][:, 0:1], w3b["yb"][:, 0:1], ALU.mult, ALU.add
                                    ).then_inc(s3k["xT"], 1)
            dve_context(v, s3k, kv3, region("in32"), None, None, None, ch)
            return ch.after()

        def dve_affine(ch, g, bb):
            for x, r, op in ((xn, g, ALU.mult), (x1, bb, ALU.add)):
                ch.link(nc.vector.tensor_tensor(x1, x, r.unsqueeze(1).to_broadcast([P, QT, C]), op))

        def dve_add(v, s, it, bank0, terms, bias, ch):
            ch.link(nc.vector.tensor_tensor(xo, terms[0], bias.unsqueeze(1).to_broadcast([P, QT, C]), ALU.add))
            for x in terms[1:]:
                ch.link(nc.vector.tensor_tensor(xo, xo, x, ALU.add))
            for i in range(2):
                v.wait_ge(s["out_psum"], it * 2 + i + 1)
                prod = PS[:, bank0 + i, :].rearrange("p (t c) -> p t c", t=2)
                tiles = slice(2 * i, 2 * i + 2)
                ch.link(nc.vector.tensor_tensor(xo[:, tiles, :], prod, xo[:, tiles, :], ALU.add))
                if i == 0:
                    dve_stats(lambda t: xo[:, t, :], range(2))

        def dve_l3a(v, base):
            of = lambda z: (lambda t: z[:, t, :])

            def first_norms(b, ch):
                nb = b * 6 + N_G
                ch.link(dve_norm(ch, nb, lambda t: X[:, bass.ds(b * QT + t, 1), :].rearrange("p a c -> p (a c)"),
                                 of(xn)))
                dve_affine(ch, row["ln1g"], row["ln1b"])
                dve_norm(ch, nb + 1, of(x1), of(xn)).then_inc(xf["xn_ready"], 1)

            def batch_row(b, ch, last=False):
                nb, j = b * 6 + N_G, b * 4 + J_G
                dve_self(v, ss, b + B, j, c3s, ch)
                dve_yT(v, so_, b * 2 + 2 * B, c3o)
                dve_add(v, so_, b * 2 + 2 * B, 0, [x1], row["a1li1b"], ch)
                dve_norm(ch, nb + 2, of(xo), of(xn), first=2).then_inc(xf["xn_ready"], 1)
                dve_ffn(v, sf, b * 2 + B, j + 1, c3f)
                dve_add(v, sf, b * 2 + B, 4, [xo, x1], row["a1li3b"], ch)
                ch.link(dve_norm(ch, nb + 3, of(xo), of(xn), first=2))
                dve_affine(ch, row["ln2g"], row["ln2b"])
                dve_norm(ch, nb + 4, of(x1), of(xn)).then_inc(xf["xn_ready"], 1)
                dve_cross(v, sc_, b + 2 * B, j + 2, b, c3c, ch)
                dve_yT(v, so_, b * 2 + (2 * B + 1), c3p)
                dve_add(v, so_, b * 2 + (2 * B + 1), 0, [x1], row["a2li1b"], ch)
                dve_norm(ch, nb + 5, of(xo), of(xn), first=2).then_inc(xf["xn_ready"], 1)
                dve_ffn(v, sf, b * 2 + (B + 1), j + 3, c3g)
                for term in (row["a2li3b"].unsqueeze(1).to_broadcast([P, QT, C]), x1):
                    ch.link(nc.vector.tensor_tensor(xo, xo, term, ALU.add))
                xr = X[:, bass.ds(b * QT, QT), :]
                ch.link(nc.vector.scalar_tensor_tensor(out=xr, in0=xo, scalar=tg[:, 3:4], in1=xr,
                                                       op0=ALU.mult, op1=ALU.add))
                if not last:
                    first_norms(b + 1, ch)
                dve_residual(v, sf, b * 2 + (B + 1), b, 4, tg[:, 3:4], None, ch)
            ch = Chain(v, dve_step, base)
            first_norms(0, ch)
            base = ch.after()
            with v.Fori(0, B - 1) as b:
                ch = Chain(v, dve_step, base, b, DVE3_STEPS)
                batch_row(b, ch)
                ch.close()
            ch = Chain(v, dve_step, ch.after(B - 1))
            batch_row(B - 1, ch, last=True)
            v.memset(scratch(1), 0.0).then_inc(done, 1)
            return ch.after()

        DVE1_STEPS, DVE3_STEPS = 38, 45
        block = ctx.enter_context(nc.Block())

        @block.sync
        def _(sp):
            sp.dma_start(X, x_in.rearrange("(t p) c -> p t c", p=P)).then_inc(ld["x"], 16)
            sp.dma_start(region("ctx"), ctxT_in).then_inc(ld["ctx"], 16)
            sp.dma_start(region("rows"), rows_in.rearrange("a n -> (a n)").partition_broadcast(P)).then_inc(ld["small"], 16)
            sp.dma_start(region("gates"), gates_in.rearrange("a n -> (a n)").partition_broadcast(P)).then_inc(ld["small"], 16)
            sp.dma_start(lora, lora_in).then_inc(ld["small"], 16)
            n = width("w0a")
            sp.dma_start(region("wa", 0, n), packs_in["w0a"]).then_inc(ld["w0a"], 16)
            sp.dma_start(region("wa", n + width("w0f"), width("w1a")), packs_in["w1a"]).then_inc(ld["w1a"], 16)
            sp.dma_start(region("wa", n, width("w0f")), packs_in["w0f"]).then_inc(ld["w0f"], 16)
            sp.dma_start(region("wf", 0, width("w1f")), packs_in["w1f"]).then_inc(ld["w1f"], 16)
            sp.wait_ge(cst["ready"], 1)
            sp.dma_start(slots2[0:S2, :].rearrange("(t p) c -> p t c", p=P),
                         zeros[:, :].unsqueeze(1).to_broadcast([P, S2 // P, C])).then_inc(ld["zeroed"], 16)
            sp.dma_start(yslots2[S2:S2 + P, :], zeros[:, :]).then_inc(ld["zeroed"], 16)
            sp.dma_start(slots3.rearrange("(t p) c -> p t c", p=P),
                         zeros[:, :].unsqueeze(1).to_broadcast([P, NB3 * ST3, C])).then_inc(ld["zeroed"], 16)
            sp.wait_ge(done, STAGE["l1ffn"])
            sp.dma_start(region("kv", 0, width("w2a")), packs_in["w2a"]).then_inc(ld["w2a"], 16)
            off = W3_OFF
            for name in ("w3a", "w3b", "w3g"):
                sp.dma_start(region("kv", off, width(name)), packs_in[name]).then_inc(ld[name], 16)
                off += width(name)
            sp.wait_ge(done, STAGE["route2"])
            sp_moe2(sp)
            sp.dma_start(ctok, ctx_in.rearrange("p (b c) -> p b c", b=B)).then_inc(ld["ctx3"], 16)
            sp.wait_ge(done, STAGE["route3"])
            sp_shared3(sp)
            sp_moe3(sp)
            for q in range(B):
                sp.wait_ge(s3m["acc"], 4 + 2 * NT + (q + 1) * TOPK3)
                sp.dma_start(out[q * T:(q + 1) * T, :].rearrange("(t p) c -> p t c", p=P), X[:, q * QT:(q + 1) * QT, :]
                             ).then_inc(ld["stored"], 16)
            sp.wait_ge(ld["stored"], B * 16)

        @block.gpsimd
        def _(pool):
            g = nc.gpsimd
            n = [0]

            def link(ins):
                n[0] += 1
                ins.then_inc(cst["step"], 1)
                pool.wait_ge(cst["step"], n[0])

            def select(out, pattern, op, fill, base, mult):
                return g.affine_select(out=out, in_=out, compare_op=op, fill=fill, base=base, pattern=pattern,
                                       channel_multiplier=mult)
            g.memset(ident, 0.0)
            g.memset(region("causal"), 0.0)
            g.memset(mhalf, -0.5)
            g.memset(zeros[:, :], 0.0)
            g.memset(cround, ROUND)
            g.iota(batch_u[:, :], pattern=[[1, NB3]], base=0, channel_multiplier=0)
            g.iota(lane_u[:, :], pattern=[[0, 1]], base=0, channel_multiplier=1)
            g.iota(spare_u[:, :], pattern=[[P, 2 * NT]], base=S2, channel_multiplier=1)
            for name in ("ones", "later", "upto", "in16", "in32", "in64", "lower"):
                last = g.memset(region(name), 1.0)
            link(last)
            link(select(ident, [[-1, P]], ALU.not_equal, 1.0, 0, 1))
            link(select(region("causal"), [[-1, P]], ALU.is_ge, NEG, 0, 1))
            link(select(region("later"), [[-1, P]], ALU.is_gt, 0.0, 0, 1))
            link(select(region("upto"), [[1, P]], ALU.is_ge, 0.0, 0, -1))
            for name, w in (("in16", 16), ("in32", 32), ("in64", 64)):
                link(select(region(name), [[-w, P // w]], ALU.is_ge, 0.0, 0, 1))
                link(select(region(name), [[w, P // w]], ALU.is_ge, 0.0, w - 1, -1))
            g.tensor_copy(ident16[:, :], ident)
            g.tensor_copy(causal16[:, :], region("causal"))
            select(view("lower", "p (i j) -> p i j", i=E3), [[1, E3], [-1, E3]], ALU.is_gt, 0.0, 0, 0
                   ).then_inc(cst["ready"], 1)
            pool.wait_ge(sq["amax"], 1)
            link(g.partition_all_reduce(amax[:, 2:4], amax[:, 0:2], P, RMAX))
            g.tensor_copy(amax[:, 6:8], amax[:, 2:4]).then_inc(sq["all"], 1)

            def quantise_w1():
                pool.wait_ge(sq["w1scale"], 1)
                for i, w in enumerate((w1f["winT"], w1f["wout"])):
                    w = w.rearrange("p (f c) -> p f c", f=FC)
                    inv, sc = (aw[:, o + 8 * i:o + 8 * i + 8].unsqueeze(2).to_broadcast([P, FC, C]) for o in (16, 32))
                    link(g.tensor_tensor(w, w, sc, ALU.mult))
                    link(g.tensor_scalar(w, w, ROUND, ROUND, ALU.add, ALU.subtract))
                    link(g.tensor_scalar(w, w, 127.0, -128.0, ALU.min, ALU.max))
                    g.tensor_tensor(w, w, inv, ALU.mult).then_inc(sq["w1"], 1)
            pool_norm(pool, N_L01)
            pool_self(pool, ss, 0, c0s, between={2: quantise_w1})
            pool_norm(pool, 1)
            pool_norm(pool, 2)
            with pool.Fori(1, B) as b:
                pool_norm(pool, b * 3)
                pool_self(pool, ss, b, c0s)
                pool_norm(pool, b * 3 + 1)
                pool_norm(pool, b * 3 + 2)
            pool_l1ffn(pool)
            with pool.Fori(0, B) as b:
                pool_norm(pool, N_E + b)
            pool_logits(pool, logits2())
            pool_scatter2(pool)
            pool_moe2(pool)
            with pool.Fori(0, B) as b:
                for i in range(6):
                    pool_norm(pool, b * 6 + (N_G + i))
                    if i == 1:
                        pool_self(pool, ss, b + B, c3s)
            pool_logits(pool, logits3())
            pool_moe3(pool)

        @block.tensor
        def _(pe):
            pe.wait_ge(ld["ctx"], 16)
            pe.wait_ge(cst["ready"], 1)

            def w0_here():
                pe.wait_ge(ld["w0a"], 16)
            pe_context(pe, s0k, kv0, w0["wck"], w0["wcv"], ctxT, lambda b: ctxdup[:, b].rearrange("p j n -> p (j n)"), w0_here)

            def w1_here():
                pe.wait_ge(ld["w1a"], 16)
                pe.wait_ge(s0k["kv_ready"], kv_count(kv0))
            pe_context(pe, s1k, kv1, w1["wk"], w1["wv"], ctxT, lambda b: ctxdup[:, b].rearrange("p j n -> p (j n)"), w1_here)
            pe.wait_ge(s1k["kv_ready"], kv_count(kv1))
            pe.wait_ge(ld["small"], 48)
            pe_lora()
            with pe.Fori(0, B) as b:
                pe_self(pe, ss, b, b * 3, c0s)
                pe.wait_ge(ss["y"], b * G + G)
                pe_cross(pe, sc_, b * 2, None, b, c0c)
                pe_out(pe, so_, b * 2, c0o, lambda: pe.wait_ge(sc_["y"], b * 2 * QT + QT))
                pe.wait_ge(sq["folded"], 1)
                pe_ffn(pe, sf, b, b * 3 + 1, c0f)
                pe_cross(pe, sc_, b * 2 + 1, b * 3 + 2, b, c1c)
                pe_out(pe, so_, b * 2 + 1, c1o, lambda: pe.wait_ge(sc_["y"], b * 2 * QT + 2 * QT))
            pe_l1ffn(pe)
            pe_l2a(pe)
            pe_logits(pe, logits2())
            pe.wait_ge(s2m["masks"], 1)
            masks = temps[:, 2 * NT * E2:4 * NT * E2]
            nc.tensor.matmul(PS[:, 0, 0:2 * NT * E2], region("upto"), masks, start=True, stop=True)
            nc.tensor.matmul(PS[:, 1, 0:2 * NT * E2], ones, masks, start=True, stop=True
                             ).then_inc(s2m["rank_psum"], 1)
            pe.wait_ge(done, STAGE["route2"])
            pe_moe2(pe)
            pe_context3(pe)
            pe.wait_ge(ld["w3a"], 16)
            with pe.Fori(0, B) as b:
                j = b * 4 + J_G
                pe_self(pe, ss, b + B, j, c3s)
                pe_out(pe, so_, b * 2 + 2 * B, c3o, lambda: pe.wait_ge(ss["y"], b * G + (B * G + G)))
                pe_ffn(pe, sf, b * 2 + B, j + 1, c3f)
                pe_cross(pe, sc_, b + 2 * B, j + 2, b, c3c)
                pe_out(pe, so_, b * 2 + (2 * B + 1), c3p, lambda: pe.wait_ge(sc_["y"], b * QT + (2 * B * QT + QT)))
                pe_ffn(pe, sf, b * 2 + (B + 1), j + 3, c3g)
            pe.wait_ge(ld["w3g"], 16)
            pe_logits(pe, logits3())
            pe.wait_ge(s3m["chosen"], 1)
            nc.tensor.matmul(PS[:, 0, 0:NT * E3], region("upto"), chosen3, start=True, stop=True)
            nc.tensor.matmul(PS[:, 1, 0:NT * E3], ones, chosen3, start=True, stop=True
                             ).then_inc(s3m["rank_psum"], 1)
            pe.wait_ge(done, STAGE["route3"])
            pe_shared3(pe, 0)
            pe_moe3(pe)
            pe_shared3(pe, 1)

        @block.scalar
        def _(act):
            act.wait_ge(ld["small"], 48)
            nc.scalar.activation(tg, region("gates"), ACT.Tanh).then_inc(gate_ready, 1)
            act.wait_ge(ld["w0a"], 16)
            act.wait_ge(ld["w0f"], 16)
            with act.Fori(0, B) as b:
                act_self(act, ss, b, b * 3, c0s)
                act_cross(act, sc_, b * 2, None, b, c0c)
                act_out(act, so_, b * 2, c0o)
                act_ffn(act, sf, b, b * 3 + 1, c0f)
                act_cross(act, sc_, b * 2 + 1, b * 3 + 2, b, c1c)
                act_out(act, so_, b * 2 + 1, c1o)
            act_l1ffn(act)
            act_l2a(act)
            act_logits(act, logits2())
            act.wait_ge(s2m["diff"], 1)
            diff = temps[:, 6 * NT * E2 + 2 * NT:6 * NT * E2 + 3 * NT]
            nc.scalar.activation(diff, diff, ACT.Exp).then_inc(s2m["ediff"], 1)
            act_moe2(act)
            act.wait_ge(ld["w3a"], 16)
            act.wait_ge(ld["w3b"], 16)
            with act.Fori(0, B) as b:
                j = b * 4 + J_G
                act_self(act, ss, b + B, j, c3s)
                act_out(act, so_, b * 2 + 2 * B, c3o)
                act_ffn(act, sf, b * 2 + B, j + 1, c3f)
                act_cross(act, sc_, b + 2 * B, j + 2, b, c3c)
                act_out(act, so_, b * 2 + (2 * B + 1), c3p)
                act_ffn(act, sf, b * 2 + (B + 1), j + 3, c3g)
            act_logits(act, logits3())
            act.wait_ge(s3m["extra"], 1)
            nc.scalar.activation(lg3, lg3, ACT.Sigmoid).then_inc(s3m["sig"], 1)
            act_shared3(act, 0)
            act_moe3(act)
            act_shared3(act, 1)

        @block.vector
        def _(v):
            ch = Chain(v, dve_step)
            v.wait_ge(cst["ready"], 1)
            v.wait_ge(ld["small"], 48)
            v.wait_ge(ld["w0a"], 16)
            dve_context(v, s0k, kv0, region("in16"), w0["bck"], row["b0cv"], region("y"), ch)
            v.wait_ge(ld["w0f"], 16)
            nc.vector.tensor_reduce(amax[:, 0:1], w0f["wfc"], AX, ALU.max, apply_absolute_value=True)
            nc.vector.tensor_reduce(amax[:, 1:2], w0f["wproj"], AX, ALU.max, apply_absolute_value=True).then_inc(sq["amax"], 1)
            dve_context(v, s1k, kv1, region("in16"), None, None, region("y"), ch)
            v.wait_ge(sq["all"], 1)
            ch.link(nc.vector.tensor_scalar(amax[:, 4:6], amax[:, 6:8], 1.0 / 127.0, None, ALU.mult))
            ch.link(nc.vector.reciprocal(amax[:, 8:10], amax[:, 4:6]))
            for op, (first, second), (op0, op1) in (("scale", (None, ROUND), (ALU.mult, ALU.add)),
                                                    ("clip", (ROUND, 127.0), (ALU.subtract, ALU.min)),
                                                    ("back", (-128.0, None), (ALU.max, ALU.mult))):
                for i, w in enumerate((w0f["wfc"], w0f["wproj"])):
                    inv, sc = amax[:, 8 + i:9 + i], amax[:, 4 + i:5 + i]
                    ins = nc.vector.tensor_scalar(w, w, inv if op == "scale" else first, sc if op == "back" else second,
                                                  op0, op1)
                ch.link(ins)
            v.wait_ge(ld["w1f"], 16)
            for i, w in enumerate((w1f["winT"], w1f["wout"])):
                ins = nc.vector.tensor_reduce(aw[:, 8 * i:8 * i + 8], w.rearrange("p (f c) -> p f c", f=FC), AX,
                                              ALU.max, apply_absolute_value=True)
            ch.link(ins)
            ch.link(nc.vector.tensor_scalar(aw[:, 16:32], aw[:, 0:16], 1e-8, 1.0 / 127.0, ALU.max, ALU.mult))
            nc.vector.reciprocal(aw[:, 32:48], aw[:, 16:32]).then_inc(sq["w1scale"], 1)
            dve_lora(v)
            v.wait_ge(gate_ready, 1)
            v.wait_ge(ld["x"], 16)
            def x_tile(b):
                return lambda t: X[:, bass.ds(b * QT + t, 1), :].rearrange("p a c -> p (a c)")
            xnt = lambda t: xn[:, t, :]

            def first_norm(b, ch):
                dve_norm(ch, b * 3, x_tile(b), xnt).then_inc(xf["xn_ready"], 1)

            def batch_row(b, ch, last=False):
                dve_self(v, ss, b, b * 3, c0s, ch)
                dve_cross(v, sc_, b * 2, None, b, c0c, ch)
                dve_yT(v, so_, b * 2, c0o)
                dve_residual(v, so_, b * 2, b, 0, tg[:, 0:1], row["b0p"], ch, x_tile(b))
                dve_norm(ch, b * 3 + 1, x_tile(b), xnt, first=2).then_inc(xf["xn_ready"], 1)
                dve_ffn(v, sf, b, b * 3 + 1, c0f)
                dve_residual(v, sf, b, b, 4, tg[:, 4:5], row["b0proj"], ch, x_tile(b))
                dve_norm(ch, b * 3 + 2, x_tile(b), xnt, first=2).then_inc(xf["xn_ready"], 1)
                dve_cross(v, sc_, b * 2 + 1, b * 3 + 2, b, c1c, ch)
                dve_yT(v, so_, b * 2 + 1, c1o)
                if not last:
                    first_norm(b + 1, ch)
                dve_residual(v, so_, b * 2 + 1, b, 0, tg[:, 1:2], None, ch)
            first_norm(0, ch)
            base = ch.after()
            with v.Fori(0, B - 1) as b:
                ch = Chain(v, dve_step, base, b, DVE1_STEPS)
                batch_row(b, ch)
                ch.close()
            ch = Chain(v, dve_step, ch.after(B - 1))
            batch_row(B - 1, ch, last=True)
            v.memset(scratch(1), 0.0).then_inc(done, 1)
            base = ch.after()
            base = dve_l1ffn(v, base)
            base = dve_l2a(v, base)
            base = dve_logits(v, base, logits2())
            base = dve_route2(v, base)
            dve_moe2(v)
            base = dve_context3(v, base)
            dve_combine2(v)
            base = dve_l3a(v, base)
            base = dve_logits(v, base, logits3())
            base = dve_route3(v, base)
            dve_shared3(v, 0)
            dve_moe3(v)
            dve_shared3(v, 1)
            dve_combine3(v)


def kernel(**inputs):
    import numpy as np
    import concourse.bacc as bacc
    from concourse.bass_utils import run_bass_kernel_spmd

    a = {k: np.asarray(v) for k, v in inputs.items()}

    def chunks(w):
        k, m = w.shape
        return w.reshape(k // P, P, m).transpose(1, 0, 2).reshape(P, -1)

    def column(v):
        return v.reshape(-1, P).T

    def slots(w):
        z = np.zeros(w.shape[:-1] + (H, SLOT), w.dtype)
        z[..., :D0] = w.reshape(w.shape[:-1] + (H, D0))
        return z.reshape(w.shape[:-1] + (H * SLOT,))

    def heads(w):
        return w.transpose(1, 0, 2).reshape(w.shape[1], -1)

    x0 = {k[9:]: v for k, v in a.items() if k.startswith("L0_xattn_")}
    f0 = {k[7:]: v for k, v in a.items() if k.startswith("L0_ffn_")}
    x1 = {k[9:]: v for k, v in a.items() if k.startswith("L1_xattn_")}
    f1 = {k[7:]: v for k, v in a.items() if k.startswith("L1_ffn_")}
    x2 = {k[9:]: v for k, v in a.items() if k.startswith("L2_xattn_")}
    f2 = {k[7:]: v for k, v in a.items() if k.startswith("L2_ffn_")}
    x3 = {k[9:]: v for k, v in a.items() if k.startswith("L3_xattn_")}
    f3 = {k[7:]: v for k, v in a.items() if k.startswith("L3_ffn_")}
    packs = {
        "w0a": [chunks(slots(x0["Wq"])), chunks(slots(x0["Wk"])), chunks(x0["Wv"]), chunks(x0["Wcq"]), x0["Wck"],
                x0["Wcv"], chunks(x0["Wp"]), column(slots(x0["bq"])), column(slots(x0["bk"])), column(x0["bcq"]),
                column(x0["bck"])],
        "w0f": [chunks(f0["W_fc"].T), chunks(f0["W_proj"].T), column(f0["b_fc"])],
        "w1a": [chunks(x1["Wq"].T), x1["Wkv"].T[:, :C], x1["Wkv"].T[:, C:], chunks(x1["Wo"].T)],
        "w1f": [chunks(f1["W_in"].T), chunks(f1["W_out"]), column(f1["b_in"])],
        "w2a": [chunks(x2["Wq"]), x2["Wk"], x2["Wv"], column(x2["bq"]), column(x2["bk"]), chunks(f2["w_g"])],
        "w3g": [chunks(f3["gate_w"].T)],
    }
    for name, n in (("w3a", "a1_"), ("w3b", "a2_")):
        w = {k[3:]: v for k, v in x3.items() if k.startswith(n)}
        packs[name] = [chunks(heads(w["wq"])), chunks(heads(w["wk"])), chunks(heads(w["wv"])), chunks(w["li1_w"]),
                       chunks(w["li2_w"]), chunks(w["li3_w"]), column(w["lnx_g"]), column(w["lnx_b"]),
                       column(w["lny_g"]), column(w["lny_b"]), column(w["ln3_g"]), column(w["ln3_b"]),
                       column(w["li2_b"])]
    rows = [x0["bv"], x0["bcv"], x0["bp"], f0["b_proj"], f1["b_out"], x2["bv"], x3["ln1_g"], x3["ln1_b"],
            x3["ln2_g"], x3["ln2_b"], x3["a1_li1_b"], x3["a1_li3_b"], x3["a2_li1_b"], x3["a2_li3_b"], f3["gate_bias"]]
    ctx = a["ctx_512"]
    ctxT = ctx.transpose(2, 0, 1)
    e2 = np.concatenate([np.stack([chunks(w) for w in f2["c_fc"]]), np.stack([chunks(w) for w in f2["c_proj"]])], 2)

    def expert3(gate, up, down):
        d = np.zeros((3 * P, C), down.dtype)
        d[:I3] = down.T
        return np.concatenate([chunks(gate.T), chunks(up.T), chunks(d)], 1)
    e3 = [expert3(f3["gate_proj"][e], f3["up_proj"][e], f3["down_proj"][e]) for e in range(E3)]
    for i in range(2):
        part = slice(i * I3, (i + 1) * I3)
        e3.append(expert3(f3["shared_gate_w"][part], f3["shared_up_w"][part], f3["shared_down_w"][:, part]))

    arrays = {
        "x": a["x"].reshape(B * T, C),
        "ctxT": np.concatenate([np.stack([ctxT, ctxT], 2).reshape(P, -1), ctxT.reshape(P, -1)], 1),
        "ctx": np.concatenate([ctx, ctx], 1).transpose(1, 0, 2).reshape(P, -1),
        "gates": np.concatenate([a["g_xattn"], a["g_ffn"]])[None],
        "lora": np.concatenate([f0["B_fc"].T, f0["B_proj"].T, f0["A_fc"], f0["A_proj"]], 1),
        "rows": np.concatenate(rows)[None],
        "e2": e2, "e3": np.stack(e3),
    }
    arrays.update({k: np.concatenate(v, 1) for k, v in packs.items()})
    arrays = {k: np.ascontiguousarray(v) for k, v in arrays.items()}
    nc = bacc.Bacc("TRN2", target_bir_lowering=False, num_devices=1)
    ap = {k: nc.dram_tensor(k, v.shape, F32, kind="ExternalInput").ap() for k, v in arrays.items()}
    scratch = [nc.dram_tensor(name, (n, C), F32, kind="Internal").ap()
               for name, n in (("slots2", S2 + 2 * NT * P), ("yslots2", S2 + P), ("slots3", NB3 * ST3 * P),
                                ("yslots3", NB3 * ST3 * P))]
    out = nc.dram_tensor("out", (B * T, C), F32, kind="ExternalOutput").ap()
    program(nc, ap["x"], ap["ctxT"], ap["ctx"], ap["gates"], {k: ap[k] for k in packs}, ap["lora"], ap["rows"],
            ap["e2"], ap["e3"], *scratch, out)
    r = run_bass_kernel_spmd(nc, [arrays], core_ids=[0])
    return r.results[0]["out"].reshape(B, T, C)
```
